# Optimizing a Trainium2 kernel written in Bass

```python
import numpy as np
import jax
import jax.numpy as jnp

def _softmax(x, axis=-1):
    return jax.nn.softmax(x, axis=axis)

def _gelu(x):
    return jax.nn.gelu(x, approximate=True)

def _silu(x):
    return jax.nn.silu(x)

def _sigmoid(x):
    return jax.nn.sigmoid(x)

def _layernorm(x, axis=-1, eps=1e-05):
    m = jnp.mean(x, axis=axis, keepdims=True)
    v = jnp.var(x, axis=axis, keepdims=True)
    return (x - m) / jnp.sqrt(v + eps)

def _scatter_add(tgt, idx, src, axis=0):
    return tgt.at[idx].add(src)

def _segment_sum(src, seg, n):
    return jax.ops.segment_sum(src, seg, n)
kernel_name = 'mk_flamingo_gated_d4_seqx_r4_4b5ea9'

def setup_inputs(seed: int=0):
    np.random.seed(seed)
    _w = jnp.asarray

    def _rec_inputs():
        import jax
        import jax.numpy as jnp
        _rk = jax.random.key(seed)
        x = -1.394e-06 + 0.9999 * jax.random.normal(jax.random.fold_in(_rk, 1), (4, 512, 256), jnp.float32)
        _lenS = 512 - jax.random.randint(jax.random.fold_in(_rk, 7), (4,), 0, max(1, 512 // 4) + 1, jnp.int32)
        _lenS2 = 64 - jax.random.randint(jax.random.fold_in(_rk, 8), (4,), 0, max(1, 64 // 4) + 1, jnp.int32)
        _ctx_1024P = jax.random.normal(jax.random.fold_in(_rk, 11), (4, 16, 256), jnp.float32)
        _ctx_1024c = jax.random.dirichlet(jax.random.fold_in(_rk, 511), 0.3 * jnp.ones((16,), jnp.float32), (4, 64))
        _ctx_1024t = jnp.einsum('bsk,bkd->bsd', _ctx_1024c, _ctx_1024P)
        _ctx_1024t = _ctx_1024t * jax.lax.rsqrt(jnp.mean(jnp.square(_ctx_1024t)) + 1e-12) * 0.953939
        ctx_1024 = -0.000209053 + 0.999977 * (_ctx_1024t + 0.3 * jax.random.normal(jax.random.fold_in(_rk, 611), (4, 64, 256), jnp.float32))
        _validS = jnp.arange(512)[None, :] < _lenS[:, None]
        _validS2 = jnp.arange(64)[None, :] < _lenS2[:, None]
        _causal = jnp.tril(jnp.ones((512, 512), dtype=bool))
        mask_BxS_ff1 = jnp.where(jnp.ones((4, 512), dtype=bool), 1.0, 0.0).astype(jnp.float32)
        mask_BxS2_ik0 = jnp.where(jnp.broadcast_to(_validS2[:, :], (4, 64)), 0, 1).astype(jnp.int32)
        _g = jax.random.normal(jax.random.fold_in(_rk, 9001), (2, 4), jnp.float32)
        _g = jnp.sign(_g) * jnp.maximum(jnp.abs(_g), 1.0) + (_g == 0) * 1.0
        g_xattn = _g[0]
        g_ffn = _g[1]
        return (x, ctx_1024, mask_BxS_ff1, mask_BxS2_ik0, g_xattn, g_ffn)
    x, ctx_1024, mask_BxS_ff1, mask_BxS2_ik0, g_xattn, g_ffn = _rec_inputs()

    def _L0_xattn_setup():
        import jax, jax.numpy as jnp
        import numpy as np
        B, T, N = (128, 32, 196)
        E = 256
        FD = 256
        H = 256
        A = 256
        SCALE = 0.02

        def _lstm_cell(x, h, c, W_ih, W_hh, b_ih, b_hh):
            gates = x @ W_ih.T + h @ W_hh.T + (b_ih + b_hh)
            i, f, g, o = jnp.split(gates, 4, axis=-1)
            c_new = jax.nn.sigmoid(f) * c + jax.nn.sigmoid(i) * jnp.tanh(g)
            h_new = jax.nn.sigmoid(o) * jnp.tanh(c_new)
            return (h_new, c_new)
        key = jax.random.key(seed)
        ks = jax.random.split(key, 16)
        g = lambda k, shape: jax.random.normal(k, shape, dtype=jnp.float32) * SCALE
        return {'feats': jax.random.normal(ks[0], (B, N, FD), dtype=jnp.float32), 'embeddings': jax.random.normal(ks[1], (B, T, E), dtype=jnp.float32), 'Wf': g(ks[2], (FD, A)), 'Wh': g(ks[3], (H, A)), 'b_att': jnp.zeros((A,), dtype=jnp.float32), 'v': g(ks[4], (A,)), 'W_ih0': g(ks[5], (4 * H, E + FD)), 'W_hh0': g(ks[6], (4 * H, H)), 'b_ih0': jnp.zeros((4 * H,), dtype=jnp.float32), 'b_hh0': jnp.zeros((4 * H,), dtype=jnp.float32), 'W_ih1': g(ks[7], (4 * H, H)), 'W_hh1': g(ks[8], (4 * H, H)), 'b_ih1': jnp.zeros((4 * H,), dtype=jnp.float32), 'b_hh1': jnp.zeros((4 * H,), dtype=jnp.float32)}
    _L0_xattn_all = _L0_xattn_setup()
    _L0_xattn_in = {k: v for k, v in _L0_xattn_all.items() if k in ('Wf', 'Wh', 'b_att', 'v', 'W_ih0', 'W_hh0', 'b_ih0', 'b_hh0', 'W_ih1', 'W_hh1', 'b_ih1', 'b_hh1')}
    del _L0_xattn_all

    def _L0_ffn_setup():
        import jax, jax.numpy as jnp
        import numpy as np
        E, H, I = (8, 256, 1024)
        B, S = (4, 512)
        key = jax.random.key(seed)
        k0, k1, k2, k3 = jax.random.split(key, 4)
        s = 0.02
        return {'hidden_states': jax.random.normal(k0, (B, S, H), dtype=jnp.float32), 'w1': jax.random.normal(k1, (E, H, I), dtype=jnp.float32) * s, 'b1': jnp.zeros((E, I), dtype=jnp.float32), 'w2': jax.random.normal(k2, (E, I, H), dtype=jnp.float32) * s, 'b2': jnp.zeros((E, H), dtype=jnp.float32), 'wr': jax.random.normal(k3, (H, E), dtype=jnp.float32) * s, 'br': jnp.zeros((E,), dtype=jnp.float32)}
    _L0_ffn_all = _L0_ffn_setup()
    _L0_ffn_in = {k: v for k, v in _L0_ffn_all.items() if k in ('w1', 'b1', 'w2', 'b2', 'wr', 'br')}
    del _L0_ffn_all

    def _L1_xattn_setup():
        import jax, jax.numpy as jnp
        import numpy as np
        H = 256
        B = 8
        L_CHAR = 512
        L_SUB = 256

        def _linear(x, W, b):
            return jnp.einsum('blh,oh->blo', x, W) + b

        def _interp_linear(x, out_len):
            L_in = x.shape[1]
            pos = (jnp.arange(out_len, dtype=x.dtype) + 0.5) * (L_in / out_len) - 0.5
            pos = jnp.clip(pos, 0.0, L_in - 1)
            lo = jnp.floor(pos).astype(jnp.int32)
            hi = jnp.minimum(lo + 1, L_in - 1)
            w = (pos - lo.astype(x.dtype))[None, :, None]
            return x[:, lo] * (1 - w) + x[:, hi] * w
        key = jax.random.key(seed)
        ks = jax.random.split(key, 18)
        s = 0.02
        inp = {'char_emb': jax.random.normal(ks[0], (B, L_CHAR, H), jnp.float32), 'subword_emb': jax.random.normal(ks[1], (B, L_SUB, H), jnp.float32)}
        names = ['Wq_c', 'Wk_s', 'Wv_s', 'Wq_s', 'Wk_c', 'Wv_c']
        for i, n in enumerate(names):
            inp[n] = jax.random.normal(ks[2 + 2 * i], (H, H), jnp.float32) * s
            inp['b' + n[1:]] = jax.random.normal(ks[3 + 2 * i], (H,), jnp.float32) * s
        inp['Wg'] = jax.random.normal(ks[14], (H, 2 * H), jnp.float32) * s
        inp['bg'] = jax.random.normal(ks[15], (H,), jnp.float32) * s
        return inp
    _L1_xattn_all = _L1_xattn_setup()
    _L1_xattn_in = {k: v for k, v in _L1_xattn_all.items() if k in ('Wq_c', 'bq_c', 'Wk_s', 'bk_s', 'Wv_s', 'bv_s', 'Wq_s', 'bq_s', 'Wk_c', 'bk_c', 'Wv_c', 'bv_c', 'Wg', 'bg')}
    del _L1_xattn_all

    def _L1_ffn_setup():
        import jax, jax.numpy as jnp
        import numpy as np
        B, S, H, F, E, K = (2, 256, 256, 512, 8, 2)
        key = jax.random.key(seed)
        ks = jax.random.split(key, 5)
        scale_h = 1.0 / np.sqrt(H)
        scale_f = 1.0 / np.sqrt(F)
        return {'inputs': jax.random.normal(ks[0], (B, S, H), dtype=jnp.float32), 'router_w': jax.random.normal(ks[1], (H, E), dtype=jnp.float32) * scale_h, 'w1': jax.random.normal(ks[2], (E, H, F), dtype=jnp.float32) * scale_h, 'w3': jax.random.normal(ks[3], (E, H, F), dtype=jnp.float32) * scale_h, 'w2': jax.random.normal(ks[4], (E, F, H), dtype=jnp.float32) * scale_f}
    _L1_ffn_all = _L1_ffn_setup()
    _L1_ffn_in = {k: v for k, v in _L1_ffn_all.items() if k in ('router_w', 'w1', 'w3', 'w2')}
    del _L1_ffn_all

    def _L2_xattn_setup():
        import jax, jax.numpy as jnp
        import numpy as np
        B, F, T, D = (8, 64, 32, 256)
        NEG = -1e+30
        key = jax.random.key(seed)
        ks = jax.random.split(key, 10)
        s = 1.0 / np.sqrt(D)
        return {'features': jax.random.normal(ks[0], (B, F, D), jnp.float32), 'masks': jnp.ones((B, F), jnp.float32), 'textual_features': jax.random.normal(ks[1], (B, T, D), jnp.float32), 'q_masks': jax.random.randint(ks[2], (B, T), 0, 2, jnp.int32), 'Ws': jax.random.normal(ks[3], (D, D), jnp.float32) * s, 'W': jax.random.normal(ks[4], (D, D), jnp.float32) * s, 'w': jax.random.normal(ks[5], (D, 1), jnp.float32) * s, 'b': jax.random.normal(ks[6], (1, D), jnp.float32) * s, 'Wcw': jax.random.normal(ks[7], (1, D), jnp.float32) * s, 'bcw': jnp.zeros((1,), jnp.float32), 'Wcb': jax.random.normal(ks[8], (1, D), jnp.float32) * s, 'bcb': jnp.zeros((1,), jnp.float32)}
    _L2_xattn_all = _L2_xattn_setup()
    _L2_xattn_in = {k: v for k, v in _L2_xattn_all.items() if k in ('Ws', 'W', 'w', 'b', 'Wcw', 'bcw', 'Wcb', 'bcb')}
    del _L2_xattn_all

    def _L2_ffn_setup():
        import jax, jax.numpy as jnp
        import numpy as np
        TOP_P = 0.8
        B, T, H, F, E = (2, 512, 256, 1024, 8)
        key = jax.random.key(seed)
        k0, k1, k2, k3 = jax.random.split(key, 4)
        x = jax.random.normal(k0, (B, T, H), jnp.float32)
        Wr = jax.random.normal(k1, (H, E), jnp.float32) * 0.02
        br = jnp.zeros((E,), jnp.float32)
        W1 = jax.random.normal(k2, (E, H, F), jnp.float32) * 0.02
        b1 = jnp.zeros((E, F), jnp.float32)
        W2 = jax.random.normal(k3, (E, F, H), jnp.float32) * 0.02
        b2 = jnp.zeros((E, H), jnp.float32)
        return {'x': x, 'Wr': Wr, 'br': br, 'W1': W1, 'b1': b1, 'W2': W2, 'b2': b2}
    _L2_ffn_all = _L2_ffn_setup()
    _L2_ffn_in = {k: v for k, v in _L2_ffn_all.items() if k in ('Wr', 'br', 'W1', 'b1', 'W2', 'b2')}
    del _L2_ffn_all

    def _L3_xattn_setup():
        import jax, jax.numpy as jnp
        import numpy as np
        B, NQ, NK = (4, 512, 512)
        QDIM = CDIM = 256
        H, DH = (16, 64)
        SCALE = DH ** (-0.5)
        WSTD = 0.02
        key = jax.random.key(seed)
        ks = jax.random.split(key, 6)
        inner = H * DH
        return {'x': jax.random.normal(ks[0], (B, NQ, QDIM), dtype=jnp.float32), 'context': jax.random.normal(ks[1], (B, NK, CDIM), dtype=jnp.float32), 'Wq': jax.random.normal(ks[2], (inner, QDIM), dtype=jnp.float32) * WSTD, 'Wk': jax.random.normal(ks[3], (inner, CDIM), dtype=jnp.float32) * WSTD, 'Wv': jax.random.normal(ks[4], (inner, CDIM), dtype=jnp.float32) * WSTD, 'Wo': jax.random.normal(ks[5], (QDIM, inner), dtype=jnp.float32) * WSTD, 'bo': jnp.zeros((QDIM,), dtype=jnp.float32)}
    _L3_xattn_all = _L3_xattn_setup()
    _L3_xattn_in = {k: v for k, v in _L3_xattn_all.items() if k in ('Wq', 'Wk', 'Wv', 'Wo', 'bo')}
    del _L3_xattn_all

    def _L3_ffn_setup():
        import jax, jax.numpy as jnp
        import numpy as np
        INT8_MAX = 127.0

        def _absmax_scale(x, axes):
            amax = jnp.max(jnp.abs(x), axis=axes, keepdims=True)
            return jnp.maximum(amax, 1e-12) / INT8_MAX
        key = jax.random.key(seed)
        k1, k2 = jax.random.split(key)
        lhs = jax.random.normal(k1, (4, 2048, 256), dtype=jnp.float32)
        rhs = jax.random.normal(k2, (256, 256), dtype=jnp.float32)
        return {'lhs': lhs, 'rhs': rhs}
    _L3_ffn_all = _L3_ffn_setup()
    _L3_ffn_in = {k: v for k, v in _L3_ffn_all.items() if k in ('rhs',)}
    del _L3_ffn_all
    return {'x': x, 'ctx_1024': ctx_1024, 'mask_BxS_ff1': mask_BxS_ff1, 'mask_BxS2_ik0': mask_BxS2_ik0, 'g_xattn': g_xattn, 'g_ffn': g_ffn, 'L0_xattn_Wf': _L0_xattn_in['Wf'], 'L0_xattn_Wh': _L0_xattn_in['Wh'], 'L0_xattn_b_att': _L0_xattn_in['b_att'], 'L0_xattn_v': _L0_xattn_in['v'], 'L0_xattn_W_ih0': _L0_xattn_in['W_ih0'], 'L0_xattn_W_hh0': _L0_xattn_in['W_hh0'], 'L0_xattn_b_ih0': _L0_xattn_in['b_ih0'], 'L0_xattn_b_hh0': _L0_xattn_in['b_hh0'], 'L0_xattn_W_ih1': _L0_xattn_in['W_ih1'], 'L0_xattn_W_hh1': _L0_xattn_in['W_hh1'], 'L0_xattn_b_ih1': _L0_xattn_in['b_ih1'], 'L0_xattn_b_hh1': _L0_xattn_in['b_hh1'], 'L0_ffn_w1': _L0_ffn_in['w1'], 'L0_ffn_b1': _L0_ffn_in['b1'], 'L0_ffn_w2': _L0_ffn_in['w2'], 'L0_ffn_b2': _L0_ffn_in['b2'], 'L0_ffn_wr': _L0_ffn_in['wr'], 'L0_ffn_br': _L0_ffn_in['br'], 'L1_xattn_Wq_c': _L1_xattn_in['Wq_c'], 'L1_xattn_bq_c': _L1_xattn_in['bq_c'], 'L1_xattn_Wk_s': _L1_xattn_in['Wk_s'], 'L1_xattn_bk_s': _L1_xattn_in['bk_s'], 'L1_xattn_Wv_s': _L1_xattn_in['Wv_s'], 'L1_xattn_bv_s': _L1_xattn_in['bv_s'], 'L1_xattn_Wq_s': _L1_xattn_in['Wq_s'], 'L1_xattn_bq_s': _L1_xattn_in['bq_s'], 'L1_xattn_Wk_c': _L1_xattn_in['Wk_c'], 'L1_xattn_bk_c': _L1_xattn_in['bk_c'], 'L1_xattn_Wv_c': _L1_xattn_in['Wv_c'], 'L1_xattn_bv_c': _L1_xattn_in['bv_c'], 'L1_xattn_Wg': _L1_xattn_in['Wg'], 'L1_xattn_bg': _L1_xattn_in['bg'], 'L1_ffn_router_w': _L1_ffn_in['router_w'], 'L1_ffn_w1': _L1_ffn_in['w1'], 'L1_ffn_w3': _L1_ffn_in['w3'], 'L1_ffn_w2': _L1_ffn_in['w2'], 'L2_xattn_Ws': _L2_xattn_in['Ws'], 'L2_xattn_W': _L2_xattn_in['W'], 'L2_xattn_w': _L2_xattn_in['w'], 'L2_xattn_b': _L2_xattn_in['b'], 'L2_xattn_Wcw': _L2_xattn_in['Wcw'], 'L2_xattn_bcw': _L2_xattn_in['bcw'], 'L2_xattn_Wcb': _L2_xattn_in['Wcb'], 'L2_xattn_bcb': _L2_xattn_in['bcb'], 'L2_ffn_Wr': _L2_ffn_in['Wr'], 'L2_ffn_br': _L2_ffn_in['br'], 'L2_ffn_W1': _L2_ffn_in['W1'], 'L2_ffn_b1': _L2_ffn_in['b1'], 'L2_ffn_W2': _L2_ffn_in['W2'], 'L2_ffn_b2': _L2_ffn_in['b2'], 'L3_xattn_Wq': _L3_xattn_in['Wq'], 'L3_xattn_Wk': _L3_xattn_in['Wk'], 'L3_xattn_Wv': _L3_xattn_in['Wv'], 'L3_xattn_Wo': _L3_xattn_in['Wo'], 'L3_xattn_bo': _L3_xattn_in['bo'], 'L3_ffn_rhs': _L3_ffn_in['rhs']}

def reference(x, ctx_1024, mask_BxS_ff1, mask_BxS2_ik0, g_xattn, g_ffn, L0_xattn_Wf, L0_xattn_Wh, L0_xattn_b_att, L0_xattn_v, L0_xattn_W_ih0, L0_xattn_W_hh0, L0_xattn_b_ih0, L0_xattn_b_hh0, L0_xattn_W_ih1, L0_xattn_W_hh1, L0_xattn_b_ih1, L0_xattn_b_hh1, L0_ffn_w1, L0_ffn_b1, L0_ffn_w2, L0_ffn_b2, L0_ffn_wr, L0_ffn_br, L1_xattn_Wq_c, L1_xattn_bq_c, L1_xattn_Wk_s, L1_xattn_bk_s, L1_xattn_Wv_s, L1_xattn_bv_s, L1_xattn_Wq_s, L1_xattn_bq_s, L1_xattn_Wk_c, L1_xattn_bk_c, L1_xattn_Wv_c, L1_xattn_bv_c, L1_xattn_Wg, L1_xattn_bg, L1_ffn_router_w, L1_ffn_w1, L1_ffn_w3, L1_ffn_w2, L2_xattn_Ws, L2_xattn_W, L2_xattn_w, L2_xattn_b, L2_xattn_Wcw, L2_xattn_bcw, L2_xattn_Wcb, L2_xattn_bcb, L2_ffn_Wr, L2_ffn_br, L2_ffn_W1, L2_ffn_b1, L2_ffn_W2, L2_ffn_b2, L3_xattn_Wq, L3_xattn_Wk, L3_xattn_Wv, L3_xattn_Wo, L3_xattn_bo, L3_ffn_rhs):
    import jax
    import jax.numpy as jnp

    def _L0_xattn_ref(feats, embeddings, Wf, Wh, b_att, v, W_ih0, W_hh0, b_ih0, b_hh0, W_ih1, W_hh1, b_ih1, b_hh1):
        import jax, jax.numpy as jnp
        import numpy as np
        B, T, N = (128, 32, 196)
        E = 256
        FD = 256
        H = 256
        A = 256
        SCALE = 0.02

        def _lstm_cell(x, h, c, W_ih, W_hh, b_ih, b_hh):
            gates = x @ W_ih.T + h @ W_hh.T + (b_ih + b_hh)
            i, f, g, o = jnp.split(gates, 4, axis=-1)
            c_new = jax.nn.sigmoid(f) * c + jax.nn.sigmoid(i) * jnp.tanh(g)
            h_new = jax.nn.sigmoid(o) * jnp.tanh(c_new)
            return (h_new, c_new)
        Bb = embeddings.shape[0]
        f_proj = jnp.einsum('bnf,fa->bna', feats, Wf) + b_att
        h0 = jnp.zeros((Bb, H), dtype=feats.dtype)
        c0 = jnp.zeros((Bb, H), dtype=feats.dtype)

        def step(carry, embed_t):
            h0, c0 = carry
            e = jnp.tanh(f_proj + (h0 @ Wh)[:, None, :])
            scores = jnp.einsum('bna,a->bn', e, v)
            alpha = jax.nn.softmax(scores, axis=-1)
            attn = jnp.einsum('bn,bnf->bf', alpha, feats)
            x = jnp.concatenate([embed_t, attn], axis=1)
            h0n, c0n = _lstm_cell(x, h0, c0, W_ih0, W_hh0, b_ih0, b_hh0)
            h1, c1 = _lstm_cell(h0n, h0n, c0n, W_ih1, W_hh1, b_ih1, b_hh1)
            return ((h0n, c0n), h1)
        (_, _), outs = jax.lax.scan(step, (h0, c0), jnp.swapaxes(embeddings, 0, 1))
        return jnp.swapaxes(outs, 0, 1)

    def _L0_ffn_ref(hidden_states, w1, b1, w2, b2, wr, br):
        import jax, jax.numpy as jnp
        import numpy as np
        E, H, I = (8, 256, 1024)
        B, S = (4, 512)
        b, s, h = hidden_states.shape
        x = hidden_states.reshape(-1, h)
        logits = x @ wr + br
        probs = jax.nn.softmax(logits, axis=-1)
        top_p, top_i = jax.lax.top_k(probs, 2)
        gate = top_p[:, 0] / (top_p[:, 0] + top_p[:, 1])
        top1 = top_i[:, 0]
        out = jnp.zeros_like(x)
        n_experts = w1.shape[0]
        for e in range(n_experts):
            hmid = jax.nn.gelu(x @ w1[e] + b1[e], approximate=False)
            hout = hmid @ w2[e] + b2[e]
            mask = top1 == e
            out = out + jnp.where(mask[:, None], hout * gate[:, None], 0.0)
        return out.reshape(b, s, h)

    def _L1_xattn_ref(char_emb, subword_emb, Wq_c, bq_c, Wk_s, bk_s, Wv_s, bv_s, Wq_s, bq_s, Wk_c, bk_c, Wv_c, bv_c, Wg, bg):
        import jax, jax.numpy as jnp
        import numpy as np
        H = 256
        B = 8
        L_CHAR = 512
        L_SUB = 256

        def _linear(x, W, b):
            return jnp.einsum('blh,oh->blo', x, W) + b

        def _interp_linear(x, out_len):
            L_in = x.shape[1]
            pos = (jnp.arange(out_len, dtype=x.dtype) + 0.5) * (L_in / out_len) - 0.5
            pos = jnp.clip(pos, 0.0, L_in - 1)
            lo = jnp.floor(pos).astype(jnp.int32)
            hi = jnp.minimum(lo + 1, L_in - 1)
            w = (pos - lo.astype(x.dtype))[None, :, None]
            return x[:, lo] * (1 - w) + x[:, hi] * w
        h = char_emb.shape[-1]
        scale = 1.0 / jnp.sqrt(jnp.asarray(h, char_emb.dtype))
        Q_char = _linear(char_emb, Wq_c, bq_c)
        K_sub = _linear(subword_emb, Wk_s, bk_s)
        V_sub = _linear(subword_emb, Wv_s, bv_s)
        scores = jnp.einsum('bqh,bkh->bqk', Q_char, K_sub) * scale
        char2sub = jnp.einsum('bqk,bkh->bqh', jax.nn.softmax(scores, axis=-1), V_sub)
        Q_sub = _linear(subword_emb, Wq_s, bq_s)
        K_char = _linear(char_emb, Wk_c, bk_c)
        V_char = _linear(char_emb, Wv_c, bv_c)
        scores2 = jnp.einsum('bqh,bkh->bqk', Q_sub, K_char) * scale
        sub2char = jnp.einsum('bqk,bkh->bqh', jax.nn.softmax(scores2, axis=-1), V_char)
        L_char = char_emb.shape[1]
        if sub2char.shape[1] != L_char:
            sub2char = _interp_linear(sub2char, L_char)
        gate_in = jnp.concatenate([char2sub, sub2char], axis=-1)
        gate = jax.nn.sigmoid(jnp.einsum('blh,oh->blo', gate_in, Wg) + bg)
        return gate * char2sub + (1 - gate) * sub2char

    def _L1_ffn_ref(inputs, router_w, w1, w3, w2):
        import jax, jax.numpy as jnp
        import numpy as np
        B, S, H, F, E, K = (2, 256, 256, 512, 8, 2)
        b, s, h = inputs.shape
        x = inputs.reshape(-1, h)
        logits = x @ router_w
        top_vals, top_idx = jax.lax.top_k(logits, K)
        importance = jax.nn.softmax(top_vals.astype(jnp.float32), axis=-1).astype(x.dtype)
        one_hot = top_idx[..., None] == jnp.arange(E)[None, None, :]
        combine = jnp.sum(jnp.where(one_hot, importance[..., None], 0.0), axis=1)
        gate = jax.nn.silu(jnp.einsum('th,ehf->etf', x, w1))
        up = jnp.einsum('th,ehf->etf', x, w3)
        expert_out = jnp.einsum('etf,efh->eth', gate * up, w2)
        out = jnp.einsum('te,eth->th', combine, expert_out)
        return out.reshape(b, s, h)

    def _L2_xattn_ref(features, masks, textual_features, q_masks, Ws, W, w, b, Wcw, bcw, Wcb, bcb):
        import jax, jax.numpy as jnp
        import numpy as np
        B, F, T, D = (8, 64, 32, 256)
        NEG = -1e+30
        txt_proj = jnp.einsum('btd,de->bte', textual_features, Ws)
        feat_proj = jnp.einsum('bfd,de->bfe', features, W)
        h = jnp.tanh(txt_proj[:, None, :, :] + feat_proj[:, :, None, :] + b[None, None, :, :][..., 0, :])
        rho = jnp.einsum('bftd,d->bft', h, w[:, 0])
        qm = q_masks.astype(jnp.float32)
        rho = rho + (1.0 - qm)[:, None, :] * NEG
        att = jax.nn.softmax(rho, axis=-1)
        txt_h = jnp.einsum('bft,btd->bfd', att, textual_features)
        w_s = jnp.tanh(jnp.einsum('bfd,od->bfo', txt_h, Wcw) + bcw)
        b_s = jnp.tanh(jnp.einsum('bfd,od->bfo', txt_h, Wcb) + bcb)
        return w_s * features + b_s

    def _L2_ffn_ref(x, Wr, br, W1, b1, W2, b2):
        import jax, jax.numpy as jnp
        import numpy as np
        TOP_P = 0.8
        B, T, H, F, E = (2, 512, 256, 1024, 8)
        probs = jax.nn.softmax(x @ Wr + br, axis=-1)
        sorted_idx = jnp.argsort(-probs, axis=-1)
        sorted_probs = jnp.take_along_axis(probs, sorted_idx, axis=-1)
        cum = jnp.cumsum(sorted_probs, axis=-1)
        mask = cum < TOP_P
        mask = mask.at[..., 0].set(True)
        inv = jnp.argsort(sorted_idx, axis=-1)
        keep = jnp.take_along_axis(mask, inv, axis=-1)
        gate = probs * keep
        h = jax.nn.relu(jnp.einsum('bth,ehf->betf', x, W1) + b1[None, :, None, :])
        y = jnp.einsum('betf,efh->beth', h, W2) + b2[None, :, None, :]
        return jnp.einsum('bte,beth->bth', gate, y)

    def _L3_xattn_ref(x, context, Wq, Wk, Wv, Wo, bo):
        import jax, jax.numpy as jnp
        import numpy as np
        B, NQ, NK = (4, 512, 512)
        QDIM = CDIM = 256
        H, DH = (16, 64)
        SCALE = DH ** (-0.5)
        WSTD = 0.02
        b, nq, _ = x.shape
        nk = context.shape[1]
        q = (x @ Wq.T).reshape(b, nq, H, DH)
        k = (context @ Wk.T).reshape(b, nk, H, DH)
        v = (context @ Wv.T).reshape(b, nk, H, DH)
        sim = jnp.einsum('bihd,bjhd->bhij', q, k) * SCALE
        attn = jax.nn.softmax(sim, axis=-1)
        out = jnp.einsum('bhij,bjhd->bihd', attn, v).reshape(b, nq, H * DH)
        return out @ Wo.T + bo

    def _L3_ffn_ref(lhs, rhs):
        import jax, jax.numpy as jnp
        import numpy as np
        INT8_MAX = 127.0

        def _absmax_scale(x, axes):
            amax = jnp.max(jnp.abs(x), axis=axes, keepdims=True)
            return jnp.maximum(amax, 1e-12) / INT8_MAX
        lhs_scale = _absmax_scale(lhs, (2,))
        rhs_scale = _absmax_scale(rhs, (0,))
        q_lhs = jnp.clip(jnp.round(lhs / lhs_scale), -INT8_MAX, INT8_MAX).astype(jnp.int8)
        q_rhs = jnp.clip(jnp.round(rhs / rhs_scale), -INT8_MAX, INT8_MAX).astype(jnp.int8)
        acc = jax.lax.dot_general(q_lhs, q_rhs, (((2,), (0,)), ((), ())), preferred_element_type=jnp.int32)
        return acc.astype(jnp.float32) * lhs_scale * rhs_scale
    x = x + jnp.tanh(g_xattn[0]) * _L0_xattn_ref(ctx_1024, _layernorm(x, axis=-1), L0_xattn_Wf, L0_xattn_Wh, L0_xattn_b_att, L0_xattn_v, L0_xattn_W_ih0, L0_xattn_W_hh0, L0_xattn_b_ih0, L0_xattn_b_hh0, L0_xattn_W_ih1, L0_xattn_W_hh1, L0_xattn_b_ih1, L0_xattn_b_hh1)
    x = x + jnp.tanh(g_ffn[0]) * _L0_ffn_ref(_layernorm(x, axis=-1), L0_ffn_w1, L0_ffn_b1, L0_ffn_w2, L0_ffn_b2, L0_ffn_wr, L0_ffn_br)
    x = x + jnp.tanh(g_xattn[1]) * _L1_xattn_ref(_layernorm(x, axis=-1), ctx_1024, L1_xattn_Wq_c, L1_xattn_bq_c, L1_xattn_Wk_s, L1_xattn_bk_s, L1_xattn_Wv_s, L1_xattn_bv_s, L1_xattn_Wq_s, L1_xattn_bq_s, L1_xattn_Wk_c, L1_xattn_bk_c, L1_xattn_Wv_c, L1_xattn_bv_c, L1_xattn_Wg, L1_xattn_bg)
    x = x + jnp.tanh(g_ffn[1]) * _L1_ffn_ref(_layernorm(x, axis=-1), L1_ffn_router_w, L1_ffn_w1, L1_ffn_w3, L1_ffn_w2)
    x = x + jnp.tanh(g_xattn[2]) * _L2_xattn_ref(_layernorm(x, axis=-1), mask_BxS_ff1, ctx_1024, mask_BxS2_ik0, L2_xattn_Ws, L2_xattn_W, L2_xattn_w, L2_xattn_b, L2_xattn_Wcw, L2_xattn_bcw, L2_xattn_Wcb, L2_xattn_bcb)
    x = x + jnp.tanh(g_ffn[2]) * _L2_ffn_ref(_layernorm(x, axis=-1), L2_ffn_Wr, L2_ffn_br, L2_ffn_W1, L2_ffn_b1, L2_ffn_W2, L2_ffn_b2)
    x = x + jnp.tanh(g_xattn[3]) * _L3_xattn_ref(_layernorm(x, axis=-1), ctx_1024, L3_xattn_Wq, L3_xattn_Wk, L3_xattn_Wv, L3_xattn_Wo, L3_xattn_bo)
    x = x + jnp.tanh(g_ffn[3]) * _L3_ffn_ref(_layernorm(x, axis=-1), L3_ffn_rhs)
    return x

_drawn_inputs = setup_inputs


def setup_inputs(seed=0):
    import zlib

    import numpy as np

    out = dict(_drawn_inputs(seed))
    spreads = {'L0_xattn_b_att': (0.0, 2.0),
     'L0_xattn_b_ih0': (0.0, 0.1),
     'L0_xattn_b_hh0': (0.0, 0.1),
     'L0_xattn_b_ih1': (0.0, 0.1),
     'L0_xattn_b_hh1': (0.0, 0.1),
     'L0_ffn_b1': (0.0, 0.1),
     'L0_ffn_b2': (0.0, 0.1),
     'L0_ffn_br': (0.0, 0.1),
     'L2_ffn_br': (0.0, 0.62),
     'L2_ffn_b1': (0.0, 0.655),
     'L2_ffn_b2': (0.0, 0.378),
     'L3_xattn_bo': (0.0, 0.1)}
    factors = {'L0_xattn_Wf': 6.534,
     'L0_xattn_Wh': 149.933,
     'L0_xattn_v': 15.352,
     'L1_xattn_Wq_c': 3.908,
     'L1_xattn_bq_c': 8.0,
     'L1_xattn_Wk_s': 4.876,
     'L1_xattn_bk_s': 200.0,
     'L1_xattn_Wq_s': 5.287,
     'L1_xattn_bq_s': 8.0,
     'L1_xattn_Wk_c': 5.931,
     'L1_xattn_bk_c': 200.0,
     'L1_xattn_Wg': 4.301,
     'L1_xattn_bg': 18.348,
     'L2_xattn_Ws': 4.819,
     'L2_xattn_W': 8.0,
     'L2_xattn_w': 4.989,
     'L2_xattn_b': 25.517,
     'L2_xattn_Wcb': 3.236,
     'L3_xattn_Wq': 8.0,
     'L3_xattn_Wk': 8.0}
    for name, (base, spread) in spreads.items():
        noise = np.random.default_rng([zlib.crc32(name.encode()), seed]).standard_normal(out[name].shape)
        drawn = base * np.exp(spread * noise) if base else spread * noise
        out[name] = jnp.asarray(drawn.astype(out[name].dtype))
    for name, factor in factors.items():
        out[name] = (out[name] * factor).astype(out[name].dtype)
    return out
```

```python
from contextlib import ExitStack

import concourse.bass as bass
from concourse import mybir
from concourse.alu_op_type import AluOpType as ALU

F32, BF16, F16, I32 = mybir.dt.float32, mybir.dt.bfloat16, mybir.dt.float16, mybir.dt.int32
ACT = mybir.ActivationFunctionType
AX = mybir.AxisListType

P = 128
B, S, C, D = 4, 512, 64, 256
N = B * S
K = D // P
E = 8
FW = 1024
FW1 = 512
HEADS, DH = 16, 64
INNER = HEADS * DH
NG = 4 * D // P
QT = S // P
EPS = 1e-5
ROUND = 1.5 * 2.0 ** 23
NEG = 1e30
HS = 16.0
GS = 256.0

VECS = ["b_att", "v", "b_ih0", "b_hh0", "b_ih1", "b_hh1", "f0_b1", "f0_b2", "f0_br", "f2_b1", "f2_b2", "f2_br",
        "bq_c", "bk_s", "bv_s", "bq_s", "bk_c", "bv_c", "bg", "ab", "aw", "wcw", "wcb", "bcw", "bcb", "bo", "gx", "gf"]
WIDTH = dict(b_att=K, v=K, b_ih0=NG, b_hh0=NG, b_ih1=NG, b_hh1=NG, f0_b1=E * FW // P, f0_b2=E * K, f0_br=E,
             f2_b1=E * FW // P, f2_b2=E * K, f2_br=E, bq_c=K, bk_s=K, bv_s=K, bq_s=K, bk_c=K, bv_c=K, bg=K,
             ab=K, aw=K, wcw=K, wcb=K, bcw=1, bcb=1, bo=K, gx=4, gf=4)
VCOL, at = {}, 0
for name in VECS:
    VCOL[name] = at
    at += WIDTH[name]
NVEC = at
CONSTS = dict(ident=P, ones=P, mean=P, diag_b=B, before=E * E, upto=E * E, interp=S)
CCOL, at = {}, 0
for name in CONSTS:
    CCOL[name] = at
    at += CONSTS[name]
NCONST = at


class Line:

    def __init__(self, sem, steps):
        self.sem, self.n = sem, len(steps)
        self.pos = {s: i + 1 for i, s in enumerate(steps)}
        assert len(self.pos) == self.n

    def after(self, step, it=0):
        return self.sem, it * self.n + (self.pos[step] + 1)

    def before(self, it):
        return self.sem, it * self.n + 1


def build(nc, dram, out):
    ctx = ExitStack()
    with ctx:
        def sb(name, shape, dt=F32):
            return ctx.enter_context(nc.sbuf_tensor(name, shape, dt))

        def sem(name):
            return ctx.enter_context(nc.semaphore(name))

        def line(name, *steps):
            every_line[name.rsplit("_", 1)[1]].append(Line(sem(name), steps))
            return every_line[name.rsplit("_", 1)[1]][-1]

        every_line = dict(pe=[], act=[], dve=[], pool=[])

        def opened(eng, name):
            for one in every_line[name]:
                eng.sem_inc(one.sem, 1)

        xT = sb("xT", [P, K, N])
        nT = sb("nT", [P, K, N])
        big = sb("big", [P, 2, 8192])
        wbuf = sb("wbuf", [P, 2, 4096])
        hist_h = sb("hist_h", [P, K, B, S + 1])
        hist_s = sb("hist_s", [P, K, B, S + 1])
        nb = sb("nb", [P, K, S])
        sq = sb("sq", [P, K, S])
        rstd = sb("rstd", [P, S])
        cst = sb("cst", [P, NCONST])
        vec = sb("vec", [P, NVEC])
        ctxT = sb("ctxT", [P, K, B * C])
        tgx = sb("tgx", [P, 4])
        tgf = sb("tgf", [P, 4])
        bank = [ctx.enter_context(nc.psum_tensor(f"bank{i}", [P, 512], F32)) for i in range(8)]

        def const(name):
            return cst[:, CCOL[name]:CCOL[name] + CONSTS[name]]

        def v_(name, i=0, n=1):
            return vec[:, VCOL[name] + i:VCOL[name] + i + n]

        ident, ones, mean_w = const("ident"), const("ones"), const("mean")

        def cols(t, off, shape, dt=F32):
            n = 1
            for s in shape:
                n *= s
            words = n * (2 if dt in (BF16, F16) else 4) // 4
            a = t[:, off:off + words]
            if dt != F32:
                a = a.bitcast(dt)
            if len(shape) == 2:
                a = a.rearrange("p (a b) -> p a b", a=shape[0])
            elif len(shape) == 3:
                a = a.rearrange("p (a b c) -> p a b c", a=shape[0], b=shape[1])
            return a

        def flat(t):
            n = len(t.shape)
            return t[:, :, :].rearrange("p a b -> p (a b)") if n == 3 else \
                t[:, :, :, :].rearrange("p a b c -> p (a b c)")

        bigA, bigB, wflat = big[:, 0, :], big[:, 1, :], flat(wbuf)
        fh, fs, fn = flat(hist_h), flat(hist_s), flat(nT)

        def bcast(a, n):
            return a.unsqueeze(2).to_broadcast([a.shape[0], a.shape[1], n])

        def over(a, m):
            return a.unsqueeze(1).to_broadcast([a.shape[0], m, a.shape[1]])

        LN_PE, LN_ACT, LN_DVE = ("mean", "var"), ("squared", "std"), ("centered", "var_eps", "rstd", "normed")

        def ln_pe(pe, L, it, c):
            for k in range(K):
                i = nc.tensor.matmul(bank[0][:, :], mean_w, xT[:, k, bass.ds(c * S, S)], start=k == 0, stop=k == K - 1)
            i.then_inc(L["pe"].sem, 1)
            pe.wait_ge(*L["act"].after("squared", it))
            for k in range(K):
                i = nc.tensor.matmul(bank[1][:, :], mean_w, sq[:, k, :], start=k == 0, stop=k == K - 1)
            i.then_inc(L["pe"].sem, 1)

        def ln_act(act, L, it):
            act.wait_ge(*L["dve"].after("centered", it))
            nc.scalar.activation(sq[:, :, :], nb[:, :, :], ACT.Square).then_inc(L["act"].sem, 1)
            act.wait_ge(*L["dve"].after("var_eps", it))
            nc.scalar.activation(rstd[:, :], rstd[:, :], ACT.Sqrt).then_inc(L["act"].sem, 1)

        def ln_dve(dve, L, it, c):
            dve.wait_ge(*L["pe"].after("mean", it))
            nc.vector.tensor_tensor(nb[:, :, :], xT[:, :, bass.ds(c * S, S)], over(bank[0][:, :], K),
                                    ALU.subtract).then_inc(L["dve"].sem, 1)
            dve.wait_ge(*L["pe"].after("var", it))
            nc.vector.tensor_scalar(rstd[:, :], bank[1][:, :], EPS, None, ALU.add).then_inc(L["dve"].sem, 1)
            dve.wait_ge(*L["act"].after("std", it))
            nc.vector.reciprocal(rstd[:, :], rstd[:, :]).then_inc(L["dve"].sem, 1)
            dve.wait_ge(*L["dve"].after("rstd", it))
            nc.vector.tensor_tensor(nb[:, :, :], nb[:, :, :], over(rstd[:, :], K), ALU.mult).then_inc(L["dve"].sem, 1)

        def lines(name, **steps):
            return {e: line(f"{name}_{e}", *steps[e]) for e in steps}

        def finished(eng, L, iters=1):
            for e in L:
                eng.wait_ge(*L[e].before(iters))

        in_small, in_ctx, in_x, in_rec, in_l1 = (sem(n) for n in ("in_small", "in_ctx", "in_x", "in_rec", "in_l1"))
        xp = cols(flat(big), 0, (2 * NG * B, S), F16)
        xp_hi, xp_lo = (cols(big[:, u, :], 0, (NG, B, S), F16) for u in range(2))
        ctxTq = sb("ctxTq", [P, K, 2 * P])
        w_x = cols(fn, 0, (K, 4 * D))
        w_f, w_h32 = cols(fn, 2048, (K, D)), cols(fn, 2560, (K, D))
        w_hh32, w_at32 = cols(fh, 0, (K, 4 * D)), cols(fh, 2048, (K, 4 * D))
        g32 = cols(fs, 0, (2, 4 * D))
        whh = cols(wflat, 0, (2, K, 4 * D), F16)
        gat = cols(wflat, 2048, (2, 2, 4 * D), F16)
        wh = cols(wflat, 4096, (2, K, D), F16)
        h_t, s_t = sb("h_t", [P, K, B]), sb("s_t", [P, K, B])
        ident16 = sb("ident16", [P, P], F16)
        GROUPS = dict(f=(2, 3), ig=(0, 1, 4, 5), o=(6, 7))
        SLOT = {g: n for n, g in enumerate(sum(GROUPS.values(), ()))}
        fproj = sb("fproj", [P, K, B * C])
        vrep = sb("vrep", [P, K, 32])
        b0 = sb("b0", [P, NG])
        b1 = sb("b1", [P, NG])
        hp = sb("hp", [P, K, 2 * B], F16)

        def setup_sp(sp):
            sp.dma_start(vec[:, :], dram["vec"]).then_inc(in_small, 16)
            sp.dma_start(cst[:, :], dram["cst"]).then_inc(in_small, 16)
            sp.dma_start(ctxT[:, :, :], dram["ctxT"]).then_inc(in_ctx, 16)
            sp.dma_start(ctxTq[:, :, :], dram["ctxTq"]).then_inc(in_ctx, 16)
            sp.dma_start(xT[:, :, :], dram["xT"]).then_inc(in_x, 16)
            for dst, n in ((w_f, "w_f"), (w_at32, "w_at"), (w_x, "w_x"), (w_hh32, "w_hh"), (w_h32, "w_h")):
                sp.dma_start(dst, dram[n]).then_inc(in_rec, 16)

        SU = lines("setup", pe=("fproj0", "fproj1", "g0", "g1", "g2", "g3"),
                   act=("tgx", "tgf", "fproj0", "fproj1", "g0", "g1", "g2", "g3"),
                   dve=("b0", "b1", "vrep", "zero_h", "ident16", "b0_ifo", "b0_g", "b0_o", "b1_half", "b1_half2", "half_hh",
                        "half_h", *(f"{w}{i}" for w in ("whh", "wh", "gat") for i in range(3)), "zero_h_t", "done"))

        def setup_pe(pe):
            pe.wait_ge(in_ctx, 32)
            pe.wait_ge(in_rec, 80)
            for a in range(K):
                for k in range(K):
                    i = nc.tensor.matmul(bank[a][:, 0:B * C], w_f[:, k, a * P:(a + 1) * P], ctxT[:, k, :],
                                         start=k == 0, stop=k == K - 1)
                i.then_inc(SU["pe"].sem, 1)
            for j in range(2):
                for u in range(2):
                    for k in range(K):
                        i = nc.tensor.matmul(bank[2 + 2 * j + u][:, :], ctxTq[:, k, j * P:(j + 1) * P],
                                             w_at32[:, k, u * 512:(u + 1) * 512], start=k == 0, stop=k == K - 1)
                    i.then_inc(SU["pe"].sem, 1)

        def setup_act(act):
            act.wait_ge(in_small, 32)
            nc.scalar.activation(tgx[:, :], v_("gx", 0, 4), ACT.Tanh).then_inc(SU["act"].sem, 1)
            nc.scalar.activation(tgf[:, :], v_("gf", 0, 4), ACT.Tanh).then_inc(SU["act"].sem, 1)
            for a in range(K):
                act.wait_ge(*SU["pe"].after(f"fproj{a}"))
                nc.scalar.activation(fproj[:, a, :], bank[a][:, 0:B * C], ACT.Identity,
                                     bias=v_("b_att", a)).then_inc(SU["act"].sem, 1)
            for j in range(2):
                for u in range(2):
                    act.wait_ge(*SU["pe"].after(f"g{2 * j + u}"))
                    src, dst = bank[2 + 2 * j + u], g32[:, j, u * 512:(u + 1) * 512]
                    if u == 0:
                        i = nc.scalar.activation(dst, src[:, :], ACT.Copy, scale=GS / 2)
                    else:
                        nc.scalar.activation(dst[:, 0:256], src[:, 0:256], ACT.Copy, scale=GS)
                        i = nc.scalar.activation(dst[:, 256:512], src[:, 256:512], ACT.Copy, scale=GS / 2)
                    i.then_inc(SU["act"].sem, 1)

        def setup_dve(dve):
            L = SU["dve"]
            dve.wait_ge(in_small, 32)
            nc.vector.tensor_tensor(b0[:, :], v_("b_ih0", 0, NG), v_("b_hh0", 0, NG), ALU.add).then_inc(L.sem, 1)
            nc.vector.tensor_tensor(b1[:, :], v_("b_ih1", 0, NG), v_("b_hh1", 0, NG), ALU.add).then_inc(L.sem, 1)
            nc.vector.tensor_copy(vrep[:, :, :], bcast(v_("v", 0, K), 32)).then_inc(L.sem, 1)
            nc.vector.memset(hp[:, :, :], 0.0).then_inc(L.sem, 1)
            nc.vector.tensor_copy(ident16[:, :], ident).then_inc(L.sem, 1)
            dve.wait_ge(*L.after("b1"))
            for g0, g1, f in ((0, 4, GS / 2), (4, 6, GS), (6, 8, GS / 2)):
                nc.vector.tensor_scalar(b0[:, g0:g1], b0[:, g0:g1], f, None, ALU.mult).then_inc(L.sem, 1)
            nc.vector.tensor_scalar(b1[:, 0:4], b1[:, 0:4], 0.5, None, ALU.mult).then_inc(L.sem, 1)
            nc.vector.tensor_scalar(b1[:, 6:8], b1[:, 6:8], 0.5, None, ALU.mult).then_inc(L.sem, 1)
            dve.wait_ge(in_rec, 80)
            for g0, g1, f in ((0, 512, GS / HS / 2), (512, 768, GS / HS), (768, 1024, GS / HS / 2)):
                i = nc.vector.tensor_scalar(w_hh32[:, :, g0:g1], w_hh32[:, :, g0:g1], f, None, ALU.mult)
            i.then_inc(L.sem, 1)
            nc.vector.tensor_scalar(w_h32, w_h32, GS / HS, None, ALU.mult).then_inc(L.sem, 1)
            for n, src, dst in (("whh", w_hh32, whh), ("wh", w_h32, wh), ("gat", g32, gat)):
                if n == "gat":
                    dve.wait_ge(*SU["act"].after("g3"))
                else:
                    dve.wait_ge(*L.after("half_h"))
                nc.vector.tensor_copy(dst[:, 0], src).then_inc(L.sem, 1)
                dve.wait_ge(*L.after(f"{n}0"))
                nc.vector.tensor_tensor(src, src, dst[:, 0], ALU.subtract).then_inc(L.sem, 1)
                dve.wait_ge(*L.after(f"{n}1"))
                nc.vector.tensor_copy(dst[:, 1], src).then_inc(L.sem, 1)
            nc.vector.memset(h_t[:, :, :], 0.0).then_inc(L.sem, 1)
            nc.vector.memset(s_t[:, :, :], 0.0).then_inc(L.sem, 1)

        XP = lines("xproj", pe=(*LN_PE, *(f"g{g}" for g in range(NG))), act=(*LN_ACT, *(f"{u}{g}" for g in range(NG) for u in ("hi", "x"))), dve=(*LN_DVE, *(f"lo{g}" for g in range(NG))))

        def xproj_pe(pe):
            pe.wait_ge(in_x, 16)
            pe.wait_ge(in_small, 32)
            finished(pe, {"act": SU["act"]})
            with pe.Fori(0, B) as c:
                pe.wait_ge(*XP["act"].before(c))
                pe.wait_ge(*XP["dve"].before(c))
                ln_pe(pe, XP, c, c)
                pe.wait_ge(*XP["dve"].after("normed", c))
                for g in range(NG):
                    if g >= 4:
                        pe.wait_ge(*XP["act"].after(f"x{g - 4}", c))
                    for k in range(K):
                        i = nc.tensor.matmul(bank[2 + g % 4][:, :], w_x[:, k, g * P:(g + 1) * P], nb[:, k, :],
                                             start=k == 0, stop=k == K - 1)
                    i.then_inc(XP["pe"].sem, 1)

        def xproj_act(act):
            act.wait_ge(*SU["dve"].after("done"))
            with act.Fori(0, B) as c:
                ln_act(act, XP, c)
                for g in range(NG):
                    act.wait_ge(*XP["pe"].after(f"g{g}", c))
                    src, scale = bank[2 + g % 4][:, :], GS if g in (4, 5) else GS / 2
                    nc.scalar.activation(xp_hi[:, SLOT[g], bass.ds(c, 1), :].rearrange("p a s -> p (a s)"), src,
                                         ACT.Identity, bias=b0[:, g:g + 1], scale=scale).then_inc(XP["act"].sem, 1)
                    if g >= 2:
                        act.wait_ge(*XP["dve"].after(f"lo{g - 2}", c))
                    else:
                        act.wait_ge(*XP["pe"].after("var", c))
                    nc.scalar.activation(sq[:, g % 2, :], src, ACT.Identity, bias=b0[:, g:g + 1],
                                         scale=scale).then_inc(XP["act"].sem, 1)

        def xproj_dve(dve):
            dve.wait_ge(in_x, 16)
            with dve.Fori(0, B) as c:
                dve.wait_ge(*XP["pe"].before(c))
                ln_dve(dve, XP, c, c)
                for g in range(NG):
                    dve.wait_ge(*XP["act"].after(f"x{g}", c))
                    hi, lo = (t[:, SLOT[g], bass.ds(c, 1), :].rearrange("p a s -> p (a s)") for t in (xp_hi, xp_lo))
                    nc.vector.tensor_tensor(lo, sq[:, g % 2, :], hi, ALU.subtract).then_inc(XP["dve"].sem, 1)

        arg = sb("arg", [P, K, B * C])
        e = sb("e", [P, K, B * C])
        negmax = sb("negmax", [P, 1])
        ex = sb("ex", [P, C])
        den = sb("den", [P, 1])
        rden = sb("rden", [P, 1])
        exT = sb("exT", [P, 2, 32])
        al32 = sb("al32", [P, 2, B])
        al = sb("al", [P, 2, 2 * B], F16)
        t_f, t_o = sb("t_f", [P, K, B]), sb("t_o", [P, K, B])
        t_ig = sb("t_ig", [P, 2 * K, B])
        o1 = sb("o1", [P, K, B])
        fc = sb("fc", [P, K, B])
        ig = sb("ig", [P, K, B])
        tc = sb("tc", [P, K, B])
        query = [bank[0], bank[1]]
        score = bank[2]
        xp_t = sb("xp_t", [P, 2, NG, B], F16)
        GATE_OUT = {g: bank[3 + u][:, j * B:(j + 1) * B] for u, gs in enumerate(GROUPS.values()) for j, g in enumerate(gs)}

        R = lines("rec", pool=("xp", "hist_h", "hist_s"), pe=("query0", "query1", "scores", "gates_f", "gates_ig", "gates_o"),
                  act=("tanh0", "tanh1", "exp", "tanh_f", "tanh_ig", "tanh_o", "tanh_c"),
                  dve=("h_hi", "h", "h_lo", "arg0", "arg1", "negmax", "exT", "rden", "al_hi", "al32", "al_lo", "fc", "ig",
                       "s", "o1"))

        R_END = line("rec_end_pool", "hist_h", "hist_s")

        def rec_finished(eng):
            eng.wait_ge(*R["pe"].before(S))
            eng.wait_ge(*R["act"].before(S))
            eng.wait_ge(*R["dve"].after("h_lo", S))
            eng.wait_ge(*R_END.after("hist_s"))

        def gate_mm(g, w, moving, k, pairs):
            for part, lo in pairs:
                i = nc.tensor.matmul(GATE_OUT[g], w[:, part, k, g * P:(g + 1) * P], moving[:, k, lo * B:(lo + 1) * B],
                                     start=False, stop=False, skip_group_check=True)
            return i

        def rec_pe(pe):
            finished(pe, {"dve": SU["dve"]})
            pe.wait_ge(*XP["act"].before(B))
            pe.wait_ge(*XP["dve"].before(B))
            with pe.Fori(0, S) as t:
                for lo in range(2):
                    pe.wait_ge(*R["dve"].after("h_lo" if lo else "h_hi", t))
                    for a in range(K):
                        pairs = [(k, part) for k in range(K) for part in range(2 - lo)]
                        for n, (k, part) in enumerate(pairs):
                            i = nc.tensor.matmul(query[a][:, 0:B], wh[:, part, k, a * P:(a + 1) * P],
                                                 hp[:, k, lo * B:(lo + 1) * B], start=n + lo == 0,
                                                 stop=lo == 1 and n == len(pairs) - 1, skip_group_check=True)
                        if lo:
                            i.then_inc(R["pe"].sem, 1)
                pe.wait_ge(*R["pool"].after("xp", t))
                for u, gs in enumerate(GROUPS.values()):
                    for part in range(2):
                        nc.tensor.matmul(bank[3 + u][:, 0:len(gs) * B], ident16[:, :],
                                         xp_t[:, part, SLOT[gs[0]]:SLOT[gs[-1]] + 1, :].rearrange("p g b -> p (g b)"),
                                         start=part == 0, stop=False, skip_group_check=True)

                def state_part(gs):
                    for g in gs:
                        for k in range(K):
                            gate_mm(g, whh, hp, k, ((0, 0), (1, 0), (0, 1)))

                state_part(GROUPS["f"])
                for a in range(K):
                    pe.wait_ge(*R["act"].after(f"tanh{a}", t))
                    for b in range(B):
                        i = nc.tensor.matmul(score[32 * b:32 * b + 32, 0:C], vrep[:, a, :], e[:, a, b * C:(b + 1) * C],
                                             start=a == 0, stop=a == K - 1)
                i.then_inc(R["pe"].sem, 1)
                state_part(GROUPS["ig"])
                state_part(GROUPS["o"])
                fig = ("f", "ig")
                pe.wait_ge(*R["dve"].after("al_hi", t))
                for name in fig:
                    for g in GROUPS[name]:
                        for j in range(2):
                            gate_mm(g, gat, al, j, ((0, 0), (1, 0)))
                pe.wait_ge(*R["dve"].after("al_lo", t))
                for name in fig:
                    for g in GROUPS[name]:
                        for j in range(2):
                            i = gate_mm(g, gat, al, j, ((0, 1),))
                    i.then_inc(R["pe"].sem, 1)
                for g in GROUPS["o"]:
                    for j in range(2):
                        i = gate_mm(g, gat, al, j, ((0, 0), (1, 0), (0, 1)))
                i.then_inc(R["pe"].sem, 1)

        def remember(pool, L, t):
            pool.wait_ge(*R["dve"].after("h", t))
            for hist, src in ((hist_h, h_t), (hist_s, s_t)):
                nc.gpsimd.tensor_copy(hist[:, :, :, bass.ds(t, 1)].rearrange("p k b a -> p k (b a)"),
                                      src[:, :, :]).then_inc(L.sem, 1)

        def rec_pool(pool):
            pool.wait_ge(*XP["act"].before(B))
            pool.wait_ge(*XP["dve"].before(B))
            with pool.Fori(0, S) as t:
                pool.wait_ge(*R["dve"].after("h_hi", t))
                nc.gpsimd.tensor_copy(xp_t[:, :, :, :].rearrange("p u g b -> p (u g b)"),
                                      xp[:, :, bass.ds(t, 1)].rearrange("p c a -> p (c a)")).then_inc(R["pool"].sem, 1)
                remember(pool, R["pool"], t)
            remember(pool, R_END, S)

        def rec_act(act):
            nc.scalar.preload_act_table(ACT.Exp)
            with act.Fori(0, S) as t:
                for a in range(K):
                    act.wait_ge(*R["dve"].after(f"arg{a}", t))
                    nc.scalar.activation(e[:, a, :], arg[:, a, :], ACT.Tanh).then_inc(R["act"].sem, 1)
                act.wait_ge(*R["dve"].after("negmax", t))
                nc.scalar.activation(ex[:, :], score[:, 0:C], ACT.Exp, bias=negmax[:, :],
                                     accum_out=den[:, :]).then_inc(R["act"].sem, 1)
                for u, (name, dst) in enumerate((("f", t_f), ("ig", t_ig), ("o", t_o))):
                    act.wait_ge(*R["pe"].after(f"gates_{name}", t))
                    n = len(GROUPS[name])
                    nc.scalar.activation(dst[:, :, :].rearrange("p g b -> p (g b)"), bank[3 + u][:, 0:n * B], ACT.Tanh,
                                         scale=1 / GS).then_inc(R["act"].sem, 1)
                act.wait_ge(*R["dve"].after("s", t))
                nc.scalar.activation(tc[:, :, :], s_t[:, :, :], ACT.Tanh, scale=0.5).then_inc(R["act"].sem, 1)

        def rec_dve(dve):
            L = R["dve"]
            dve.wait_ge(*XP["act"].before(B))
            dve.sem_inc(L.sem, 3)
            with dve.Fori(0, S) as t:
                for a in range(K):
                    dve.wait_ge(*R["pe"].after(f"query{a}", t))
                    nc.vector.scalar_tensor_tensor(arg[:, a, :].rearrange("p (b n) -> p b n", b=B),
                                                   bcast(query[a][:, 0:B], C), 1 / GS,
                                                   fproj[:, a, :].rearrange("p (b n) -> p b n", b=B),
                                                   ALU.mult, ALU.add).then_inc(L.sem, 1)
                dve.wait_ge(*R["pe"].after("scores", t))
                nc.vector.tensor_reduce(negmax[:, :], score[:, 0:C], AX.X, ALU.max, negate=True).then_inc(L.sem, 1)
                dve.wait_ge(*R["act"].after("exp", t))
                nc.vector.transpose(exT[:, :, :].rearrange("p j c -> p (j c)"), ex[:, :]).then_inc(L.sem, 1)
                nc.vector.reciprocal(rden[:, :], den[:, :]).then_inc(L.sem, 1)
                dve.wait_ge(*L.after("rden", t))
                for dst in (al[:, :, 0:B], al32[:, :, :]):
                    nc.vector.scalar_tensor_tensor(dst, exT[:, :, 0:B], rden[:, 0:1], over(const("diag_b"), 2),
                                                   ALU.mult, ALU.mult).then_inc(L.sem, 1)
                dve.wait_ge(*L.after("al32", t))
                nc.vector.tensor_tensor(al[:, :, B:2 * B], al32[:, :, :], al[:, :, 0:B],
                                        ALU.subtract).then_inc(L.sem, 1)
                dve.wait_ge(*R["act"].after("tanh_f", t))
                nc.vector.scalar_tensor_tensor(fc[:, :, :], t_f[:, :, :], 1.0, s_t[:, :, :], ALU.add,
                                               ALU.mult).then_inc(L.sem, 1)
                dve.wait_ge(*R["act"].after("tanh_ig", t))
                nc.vector.scalar_tensor_tensor(ig[:, :, :], t_ig[:, 0:2, :], 1.0, t_ig[:, 2:4, :], ALU.add,
                                               ALU.mult).then_inc(L.sem, 1)
                dve.wait_ge(*R["pool"].after("hist_s", t))
                dve.wait_ge(*L.after("ig", t))
                nc.vector.scalar_tensor_tensor(s_t[:, :, :], fc[:, :, :], 0.5, ig[:, :, :], ALU.mult,
                                               ALU.add).then_inc(L.sem, 1)
                dve.wait_ge(*R["act"].after("tanh_o", t))
                nc.vector.tensor_scalar(o1[:, :, :], t_o[:, :, :], 1.0, HS / 2, ALU.add, ALU.mult).then_inc(L.sem, 1)
                dve.wait_ge(*L.after("o1", t))
                dve.wait_ge(*R["act"].after("tanh_c", t))
                for dst in (hp[:, :, 0:B], h_t[:, :, :]):
                    nc.vector.tensor_tensor(dst, o1[:, :, :], tc[:, :, :], ALU.mult).then_inc(L.sem, 1)
                dve.wait_ge(*L.after("h", t + 1))
                nc.vector.tensor_tensor(hp[:, :, B:2 * B], h_t[:, :, :], hp[:, :, 0:B],
                                        ALU.subtract).then_inc(L.sem, 1)

        w1s = cols(fn, 0, (K, 4 * D))
        w1b = cols(fn, 2048, (K, 4 * D))
        t2 = cols(bigA, 0, (NG, S))
        fc2, ig2 = cols(bigA, 4096, (K, S)), cols(bigA, 5120, (K, S))
        tc2 = cols(bigA, 6144, (K, S))
        tgh = sb("tgh", [P, 1])
        L2 = lines("lstm2", pe=tuple(f"g{g}" for g in range(NG)), act=(*(f"t{g}" for g in range(NG)), "tanh_c"),
                   dve=("fc", "ig", "c", "h", "x0", "x1"))
        L2W = line("lstm2_w_dve", "sum", "half", "tgh")

        def lstm2_sp(sp):
            finished(sp, XP, B)
            finished(sp, SU)
            sp.dma_start(w1s, dram["w_ih1"]).then_inc(in_l1, 16)
            sp.dma_start(w1b, dram["w_hh1"]).then_inc(in_l1, 16)

        def lstm2_pe(pe):
            pe.wait_ge(*L2W.after("half"))
            rec_finished(pe)
            with pe.Fori(0, B) as c:
                for g in range(NG):
                    if g >= 4:
                        pe.wait_ge(*L2["act"].after(f"t{g - 4}", c))
                    else:
                        pe.wait_ge(*L2["act"].before(c))
                    for k in range(K):
                        h = hist_h[:, k, bass.ds(c, 1), 1:S + 1].rearrange("p a s -> p (a s)")
                        i = nc.tensor.matmul(bank[g % 4][:, :], w1s[:, k, g * P:(g + 1) * P], h,
                                             start=k == 0, stop=k == K - 1)
                    i.then_inc(L2["pe"].sem, 1)

        def lstm2_act(act):
            rec_finished(act)
            with act.Fori(0, B) as c:
                act.wait_ge(*L2["dve"].before(c))
                for g in range(NG):
                    act.wait_ge(*L2["pe"].after(f"g{g}", c))
                    nc.scalar.activation(t2[:, g, :], bank[g % 4][:, :], ACT.Tanh, bias=b1[:, g:g + 1],
                                         scale=1.0 if g in (4, 5) else 0.5).then_inc(L2["act"].sem, 1)
                act.wait_ge(*L2["dve"].after("c", c))
                nc.scalar.activation(tc2, fc2, ACT.Tanh, scale=0.5).then_inc(L2["act"].sem, 1)

        def lstm2_dve(dve):
            dve.wait_ge(in_l1, 32)
            nc.vector.tensor_tensor(w1s, w1s, w1b, ALU.add).then_inc(L2W.sem, 1)
            dve.wait_ge(*L2W.after("sum"))
            nc.vector.tensor_scalar(w1s, w1s, 1 / HS, None, ALU.mult).then_inc(L2W.sem, 1)
            dve.wait_ge(*SU["act"].after("tgx"))
            nc.vector.tensor_scalar(tgh[:, :], tgx[:, 0:1], 0.5, None, ALU.mult).then_inc(L2W.sem, 1)
            rec_finished(dve)
            with dve.Fori(0, B) as c:
                s0 = hist_s[:, :, bass.ds(c, 1), 1:S + 1].rearrange("p k a s -> p k (a s)")
                dve.wait_ge(*L2["act"].after("t7", c))
                nc.vector.scalar_tensor_tensor(fc2, t2[:, 2:4, :], 1.0, s0, ALU.add, ALU.mult).then_inc(L2["dve"].sem, 1)
                nc.vector.scalar_tensor_tensor(ig2, t2[:, 0:2, :], 1.0, t2[:, 4:6, :], ALU.add,
                                               ALU.mult).then_inc(L2["dve"].sem, 1)
                dve.wait_ge(*L2["dve"].after("ig", c))
                nc.vector.scalar_tensor_tensor(fc2, fc2, 0.5, ig2, ALU.mult, ALU.add).then_inc(L2["dve"].sem, 1)
                dve.wait_ge(*L2["act"].after("tanh_c", c))
                nc.vector.scalar_tensor_tensor(ig2, t2[:, 6:8, :], 1.0, tc2, ALU.add, ALU.mult).then_inc(L2["dve"].sem, 1)
                dve.wait_ge(*L2["dve"].after("h", c))
                for k in range(K):
                    xs = xT[:, k, bass.ds(c * S, S)]
                    nc.vector.scalar_tensor_tensor(xs, ig2[:, k, :], tgh[:, 0:1], xs, ALU.mult,
                                                   ALU.add).then_inc(L2["dve"].sem, 1)

        wr = sb("wr", [P, K, E])
        T = N // P
        lg = sb("lg", [P, T, E])
        gates = sb("gates", [P, T, E])
        rank = sb("rank", [P, T, E])
        m0, m1 = sb("m0", [P, T, E]), sb("m1", [P, T, E])
        r0, r1 = sb("r0", [P, T]), sb("r1", [P, T])
        in_wr, in_w, in_gate, out_gate = sem("in_wr"), [sem("in_w0"), sem("in_w1")], [sem("in_gate0"), sem("in_gate1")], \
            sem("out_gate")
        gate_dram = [nc.dram_tensor(f"gates_of_layer{i}", (E, N), F32, kind="Internal").ap() for i in range(3)]
        hid = cols(bigA, 0, (FW // P, S))
        silu = cols(bigA, 2048, (FW1 // P, S))
        gate_bc = [bigA[:, 4096:6144], bigA[:, 6144:8192]]
        gT = bigA[0:E, 0:N]
        pair0, pair1 = cols(bigA, 2048, (T, E * E)), cols(bigA, 3072, (T, E * E))
        fo = sb("fo", [P, K, S])

        RANKED = ("gt", "equal", "tie", "pairs", "rank")
        SOFTMAX = ("max", "shift", "sum", "rsum", "probs")
        BEST2 = ("first", "second", "p1", "p2", "s1", "s2")
        ROUTE = [(*SOFTMAX, *RANKED, *BEST2, "s12", "rs12", "share", "gates"),
                 (*RANKED, *BEST2, "diff", "denom", "w1", "w2", "g1", "g2", "gates"),
                 (*SOFTMAX, *RANKED, "cum_in", "cum", "low", "first", "keep", "gates")]

        def expert_layer(n, prev, prev_iters):
            F = FW1 if n == 1 else FW
            FT = F // P
            LR = lines(f"ln{n}", pe=(*LN_PE, "logits"), act=LN_ACT, dve=(*LN_DVE, "logits", "stored"))
            RT = lines(f"route{n}", pe=("gT0", "gT1", "gT2", "gT3"), act=("exp", "gT0", "gT1", "gT2", "gT3"),
                       dve=ROUTE[n])
            XL = lines(f"experts{n}",
                       pe=(*(f"{u}{f}" for f in range(FT) for u in (("gate", "up") if n == 1 else ("up",))), "out0", "out1"),
                       act=tuple(f"act{f}" for f in range(FT)),
                       dve=(*((f"hid{f}" for f in range(FT)) if n == 1 else ()), "gated0", "gated1", "x0", "x1"))
            names = ("f1_w1", "f1_w3", "f1_w2") if n == 1 else (f"f{n}_w1", f"f{n}_w2")
            w_base = 16 * (E // 2) * sum(3 if i == 1 else 2 for i in range(n))
            g_base = 16 * (E // 2) * n

            def weights(half):
                o = wbuf[:, half, :]
                if n == 1:
                    return cols(o, 0, (K, F)), cols(o, K * F, (K, F)), cols(o, 2 * K * F, (FT, D))
                return cols(o, 0, (K, F)), cols(o, K * F, (FT, D))

            def load_weights(sp, e, half):
                for dst, nm in zip(weights(half), names):
                    sp.dma_start(dst, dram[nm][bass.ds(e, 1)].rearrange("a p k f -> p (a k) f")).then_inc(in_w[half], 16)

            def load_gates(sp, e, half):
                sp.dma_start(gate_bc[half], gate_dram[n][bass.ds(e, 1), :].to_broadcast([P, N])).then_inc(in_gate[half], 16)

            def route_sp(sp):
                finished(sp, prev, prev_iters)
                sp.dma_start(wr[:, :, :], dram[f"f{n}_wr"]).then_inc(in_wr, 16)
                for half in range(2):
                    load_weights(sp, half, half)
                sp.wait_ge(*RT["act"].after("gT3"))
                sp.dma_start(gate_dram[n], gT).then_inc(out_gate, 16)
                sp.wait_ge(out_gate, 16 * (n + 1))
                for half in range(2):
                    load_gates(sp, half, half)

            def experts_sp(sp):
                with sp.Fori(1, E // 2) as ep:
                    for half in range(2):
                        done = (ep * 2 + half - 1) * B
                        sp.wait_ge(*XL["pe"].before(done))
                        load_weights(sp, ep * 2 + half, half)
                        sp.wait_ge(*XL["dve"].before(done))
                        load_gates(sp, ep * 2 + half, half)

            def route_pe(pe):
                finished(pe, prev, prev_iters)
                pe.wait_ge(in_wr, 16 * (n + 1))
                with pe.Fori(0, B) as c:
                    pe.wait_ge(*LR["dve"].before(c))
                    ln_pe(pe, LR, c, c)
                    pe.wait_ge(*LR["dve"].after("normed", c))
                    for q in range(QT):
                        for k in range(K):
                            i = nc.tensor.matmul(bank[2][:, q * E:(q + 1) * E], nb[:, k, q * P:(q + 1) * P], wr[:, k, :],
                                                 start=k == 0, stop=k == K - 1)
                    i.then_inc(LR["pe"].sem, 1)
                pe.wait_ge(*RT["dve"].after("gates"))
                for b in range(B):
                    for q in range(QT):
                        i = nc.tensor.transpose(bank[3 + b][0:E, q * P:(q + 1) * P], gates[:, b * QT + q, :], ident)
                    i.then_inc(RT["pe"].sem, 1)

            def route_act(act):
                finished(act, prev, prev_iters)
                with act.Fori(0, B) as c:
                    ln_act(act, LR, c)
                if n == 1:
                    act.wait_ge(*RT["dve"].after("diff"))
                    i = nc.scalar.activation(r1[:, :], r1[:, :], ACT.Exp)
                else:
                    act.wait_ge(*RT["dve"].after("shift"))
                    i = nc.scalar.activation(gates[:, :, :], lg[:, :, :], ACT.Exp)
                i.then_inc(RT["act"].sem, 1)
                for b in range(B):
                    act.wait_ge(*RT["pe"].after(f"gT{b}"))
                    nc.scalar.activation(gT[:, b * S:(b + 1) * S], bank[3 + b][0:E, :], ACT.Copy).then_inc(RT["act"].sem, 1)

            def route_dve(dve):
                finished(dve, prev, prev_iters)
                with dve.Fori(0, B) as c:
                    ln_dve(dve, LR, c, c)
                    dve.wait_ge(*LR["dve"].after("normed", c))
                    nc.vector.tensor_copy(nT[:, :, bass.ds(c * S, S)], nb[:, :, :]).then_inc(LR["dve"].sem, 1)
                    dve.wait_ge(*LR["pe"].after("logits", c))
                    dst = lg[:, bass.ds(c * QT, QT), :]
                    src = bank[2][:, 0:QT * E].rearrange("p (q e) -> p q e", e=E)
                    if n == 1:
                        i = nc.vector.tensor_copy(dst, src)
                    else:
                        i = nc.vector.tensor_tensor(dst, src, over(v_(f"f{n}_br", 0, E), QT), ALU.add)
                    i.then_inc(LR["dve"].sem, 1)
                dve.wait_ge(*LR["dve"].before(B))
                L = RT["dve"]
                rank_by = lg
                if n != 1:
                    nc.vector.tensor_reduce(r0[:, :], lg[:, :, :], AX.X, ALU.max).then_inc(L.sem, 1)
                    dve.wait_ge(*L.after("max"))
                    nc.vector.tensor_tensor(lg[:, :, :], lg[:, :, :], bcast(r0[:, :], E), ALU.subtract).then_inc(L.sem, 1)
                    dve.wait_ge(*RT["act"].after("exp"))
                    nc.vector.tensor_reduce(r0[:, :], gates[:, :, :], AX.X, ALU.add).then_inc(L.sem, 1)
                    dve.wait_ge(*L.after("sum"))
                    nc.vector.reciprocal(r0[:, :], r0[:, :]).then_inc(L.sem, 1)
                    dve.wait_ge(*L.after("rsum"))
                    nc.vector.tensor_tensor(gates[:, :, :], gates[:, :, :], bcast(r0[:, :], E), ALU.mult).then_inc(L.sem, 1)
                    dve.wait_ge(*L.after("probs"))
                    rank_by = gates
                e_of = rank_by[:, :, :].unsqueeze(3).to_broadcast([P, T, E, E])
                j_of = rank_by[:, :, :].unsqueeze(2).to_broadcast([P, T, E, E])
                p0 = pair0.rearrange("p t (e j) -> p t e j", e=E)
                p1 = pair1.rearrange("p t (e j) -> p t e j", e=E)
                nc.vector.tensor_tensor(p0, j_of, e_of, ALU.is_gt).then_inc(L.sem, 1)
                nc.vector.tensor_tensor(p1, j_of, e_of, ALU.is_equal).then_inc(L.sem, 1)
                dve.wait_ge(*L.after("equal"))
                nc.vector.tensor_tensor(pair1, pair1, over(const("upto" if n == 2 else "before"), T),
                                        ALU.mult).then_inc(L.sem, 1)
                dve.wait_ge(*L.after("tie"))
                nc.vector.tensor_tensor(pair0, pair0, pair1, ALU.add).then_inc(L.sem, 1)
                dve.wait_ge(*L.after("pairs"))
                nc.vector.tensor_reduce(rank[:, :, :], p0, AX.X, ALU.add).then_inc(L.sem, 1)
                dve.wait_ge(*L.after("rank"))
                if n == 2:
                    nc.vector.tensor_tensor(p0, p0, j_of, ALU.mult).then_inc(L.sem, 1)
                    dve.wait_ge(*L.after("cum_in"))
                    nc.vector.tensor_reduce(m0[:, :, :], p0, AX.X, ALU.add).then_inc(L.sem, 1)
                    dve.wait_ge(*L.after("cum"))
                    nc.vector.tensor_scalar(m0[:, :, :], m0[:, :, :], 0.8, None, ALU.is_lt).then_inc(L.sem, 1)
                    nc.vector.tensor_scalar(m1[:, :, :], rank[:, :, :], 1.5, None, ALU.is_lt).then_inc(L.sem, 1)
                    dve.wait_ge(*L.after("first"))
                    nc.vector.tensor_tensor(m0[:, :, :], m0[:, :, :], m1[:, :, :], ALU.max).then_inc(L.sem, 1)
                    dve.wait_ge(*L.after("keep"))
                    nc.vector.tensor_tensor(gates[:, :, :], gates[:, :, :], m0[:, :, :], ALU.mult).then_inc(L.sem, 1)
                    return
                nc.vector.tensor_scalar(m0[:, :, :], rank[:, :, :], 0.0, None, ALU.is_equal).then_inc(L.sem, 1)
                nc.vector.tensor_scalar(m1[:, :, :], rank[:, :, :], 1.0, None, ALU.is_equal).then_inc(L.sem, 1)
                dve.wait_ge(*L.after("second"))
                nc.vector.tensor_tensor(pair0[:, :, 0:E], rank_by[:, :, :], m0[:, :, :], ALU.mult).then_inc(L.sem, 1)
                nc.vector.tensor_tensor(pair1[:, :, 0:E], rank_by[:, :, :], m1[:, :, :], ALU.mult).then_inc(L.sem, 1)
                dve.wait_ge(*L.after("p2"))
                nc.vector.tensor_reduce(r0[:, :], pair0[:, :, 0:E], AX.X, ALU.add).then_inc(L.sem, 1)
                nc.vector.tensor_reduce(r1[:, :], pair1[:, :, 0:E], AX.X, ALU.add).then_inc(L.sem, 1)
                dve.wait_ge(*L.after("s2"))
                if n == 0:
                    nc.vector.tensor_tensor(r1[:, :], r0[:, :], r1[:, :], ALU.add).then_inc(L.sem, 1)
                    dve.wait_ge(*L.after("s12"))
                    nc.vector.reciprocal(r1[:, :], r1[:, :]).then_inc(L.sem, 1)
                    dve.wait_ge(*L.after("rs12"))
                    nc.vector.tensor_tensor(r0[:, :], r0[:, :], r1[:, :], ALU.mult).then_inc(L.sem, 1)
                    dve.wait_ge(*L.after("share"))
                    nc.vector.tensor_tensor(gates[:, :, :], m0[:, :, :], bcast(r0[:, :], E), ALU.mult).then_inc(L.sem, 1)
                    return
                nc.vector.tensor_tensor(r1[:, :], r1[:, :], r0[:, :], ALU.subtract).then_inc(L.sem, 1)
                dve.wait_ge(*RT["act"].after("exp"))
                nc.vector.tensor_scalar(r0[:, :], r1[:, :], 1.0, None, ALU.add).then_inc(L.sem, 1)
                dve.wait_ge(*L.after("denom"))
                nc.vector.reciprocal(r0[:, :], r0[:, :]).then_inc(L.sem, 1)
                dve.wait_ge(*L.after("w1"))
                nc.vector.tensor_tensor(r1[:, :], r1[:, :], r0[:, :], ALU.mult).then_inc(L.sem, 1)
                dve.wait_ge(*L.after("w2"))
                nc.vector.tensor_tensor(m0[:, :, :], m0[:, :, :], bcast(r0[:, :], E), ALU.mult).then_inc(L.sem, 1)
                nc.vector.tensor_tensor(m1[:, :, :], m1[:, :, :], bcast(r1[:, :], E), ALU.mult).then_inc(L.sem, 1)
                dve.wait_ge(*L.after("g2"))
                nc.vector.tensor_tensor(gates[:, :, :], m0[:, :, :], m1[:, :, :], ALU.add).then_inc(L.sem, 1)

            def experts_pe(pe):
                pe.wait_ge(*RT["act"].after("gT3"))
                pe.wait_ge(*LR["dve"].before(B))
                outs = [bank[6], bank[7]]

                def up(f, half, c, it):
                    r = [nT[:, k, bass.ds(c * S, S)] for k in range(K)]
                    for m in range(2 if n == 1 else 1):
                        ps = bank[2 * m + f % 2] if n == 1 else bank[f % 3]
                        for k in range(K):
                            i = nc.tensor.matmul(ps[:, :], weights(half)[m][:, k, f * P:(f + 1) * P], r[k],
                                                 start=k == 0, stop=k == K - 1)
                        i.then_inc(XL["pe"].sem, 1)

                def down(f, half, it):
                    if f == 0:
                        pe.wait_ge(*XL["dve"].before(it))
                    pe.wait_ge(*(XL["dve"].after(f"hid{f}", it) if n == 1 else XL["act"].after(f"act{f}", it)))
                    for h in range(K):
                        i = nc.tensor.matmul(outs[h][:, :], weights(half)[-1][:, f, h * P:(h + 1) * P], hid[:, f, :],
                                             start=f == 0, stop=f == FT - 1)
                        if f == FT - 1:
                            i.then_inc(XL["pe"].sem, 1)

                with pe.Fori(0, E // 2) as ep:
                    for half in range(2):
                        with pe.Fori(0, B) as c:
                            pe.wait_ge(in_w[half], (ep + 1) * 16 * len(names) + w_base)
                            it = (ep * 2 + half) * B + c
                            up(0, half, c, it)
                            for f in range(1, FT):
                                up(f, half, c, it)
                                down(f - 1, half, it)
                            down(FT - 1, half, it)

            def experts_act(act):
                act.wait_ge(out_gate, 16 * (n + 1))
                act.wait_ge(*RT["dve"].before(1))
                with act.Fori(0, E) as ex_:
                    with act.Fori(0, B) as c:
                        it = ex_ * B + c
                        for f in range(FT):
                            if n == 1:
                                act.wait_ge(*XL["pe"].after(f"gate{f}", it))
                                i = nc.scalar.activation(silu[:, f, :], bank[f % 2][:, :], ACT.Silu)
                            else:
                                act.wait_ge(*XL["pe"].after(f"up{f}", it))
                                col = VCOL[f"f{n}_b1"] + f
                                i = nc.scalar.activation(hid[:, f, :], bank[f % 3][:, :], ACT.Gelu if n == 0 else ACT.Relu,
                                                         bias=vec[:, bass.ds(ex_ * FT + col, 1)])
                            i.then_inc(XL["act"].sem, 1)

            def experts_dve(dve):
                dve.wait_ge(out_gate, 16 * (n + 1))
                with dve.Fori(0, E // 2) as ep:
                    for half in range(2):
                        with dve.Fori(0, B) as c:
                            dve.wait_ge(in_gate[half], (ep + 1) * 16 + g_base)
                            ex_ = ep * 2 + half
                            it = ex_ * B + c
                            if n == 1:
                                for f in range(FT):
                                    dve.wait_ge(*XL["pe"].after(f"up{f}", it))
                                    dve.wait_ge(*XL["act"].after(f"act{f}", it))
                                    nc.vector.tensor_tensor(hid[:, f, :], silu[:, f, :], bank[2 + f % 2][:, :],
                                                            ALU.mult).then_inc(XL["dve"].sem, 1)
                            g = gate_bc[half][:, bass.ds(c * S, S)]
                            for h in range(K):
                                dve.wait_ge(*XL["pe"].after(f"out{h}", it))
                                if n == 1:
                                    i = nc.vector.tensor_tensor(fo[:, h, :], bank[6 + h][:, :], g, ALU.mult)
                                else:
                                    col = VCOL[f"f{n}_b2"] + h
                                    i = nc.vector.scalar_tensor_tensor(fo[:, h, :], bank[6 + h][:, :],
                                                                       vec[:, bass.ds(ex_ * K + col, 1)], g,
                                                                       ALU.add, ALU.mult)
                                i.then_inc(XL["dve"].sem, 1)
                            for h in range(K):
                                dve.wait_ge(*XL["dve"].after(f"gated{h}", it))
                                xs = xT[:, h, bass.ds(c * S, S)]
                                nc.vector.scalar_tensor_tensor(xs, fo[:, h, :], tgf[:, n:n + 1], xs, ALU.mult,
                                                               ALU.add).then_inc(XL["dve"].sem, 1)

            return XL, route_sp, experts_sp, route_pe, experts_pe, route_act, experts_act, route_dve, experts_dve

        F0, f0_route_sp, f0_sp, f0_route_pe, f0_pe, f0_route_act, f0_act, f0_route_dve, f0_dve = expert_layer(0, L2, B)

        in_x1 = sem("in_x1")
        w_x1 = cols(bigB, 0, (6, K, D))
        WQC, WKS, WVS, WQS, WKC, WVC = range(6)
        w_g = cols(bigB, 3072, (2 * K, D))
        ctxb = sb("ctxb", [P, K, 2 * C])
        qcT, kcT = cols(bigA, 0, (K, S)), cols(bigA, 1024, (K, S))
        c2s, s2c = cols(bigA, 2048, (K, S)), cols(bigA, 3072, (K, S))
        vc = cols(bigA, 4096, (QT, D))
        gate1, mix = cols(bigA, 5120, (K, S)), cols(bigA, 6144, (K, S))
        ksT, qsT = cols(fh, 0, (K, C)), cols(fh, 128, (K, C))
        vs = fh[0:C, 256:512]
        s1 = cols(fh, 512, (QT, C))
        s2 = fh[0:C, 1024:1536]
        s1T = fh[0:C, 1536:2048]
        s2T = cols(fh, 2048, (QT, C))
        s2o = fh[0:C, 2304:2560]
        mx1, sum1 = sb("mx1", [P, QT]), sb("sum1", [P, QT])
        mx2, sum2 = sb("mx2", [P, 1]), sb("sum2", [P, 1])
        bgh = sb("bgh", [P, K])
        tg1h = sb("tg1h", [P, 1])
        SC1 = 1.0 / 16.0
        X1 = lines("x1", pe=(*LN_PE, "ks", "qs", "vs", "qc0", "qc1", "kc0", "kc1", "vc", "s1", "s2", "s1T", "s2T",
                             "c2s0", "c2s1", "s2o", "s2c0", "s2c1", "gate0", "gate1"),
                   act=(*LN_ACT, "ks", "qs", "vs", "qc0", "qc1", "kc0", "kc1", "vc", "e1", "e2", "c2s0", "c2s1",
                        "s2c0", "s2c1", "gate0", "gate1"),
                   dve=("ctxb", *LN_DVE, "mx1", "mx2", "nmx2", "shift1", "sum1", "rsum1", "p1", "rsum2", "p2", "s1T", "s2T",
                        "s2o", "diff", "prod", "mix", "x0", "x1"))
        X1C = line("x1_consts_dve", "bgh", "tg1h")

        def x1_load(sp):
            sp.wait_ge(*R["dve"].after("h_lo", S))
            sp.dma_start(w_x1.rearrange("p w k d -> p (w k d)"), dram["x1_w"]).then_inc(in_x1, 16)
            sp.dma_start(w_g, dram["x1_wg"]).then_inc(in_x1, 16)

        def x1_pe(pe):
            finished(pe, F0, E * B)
            pe.wait_ge(in_x1, 32)
            L = X1["pe"]

            def proj(dst, w, o, rhs):
                for k in range(K):
                    i = nc.tensor.matmul(dst, w_x1[:, w, k, o * P:(o + 1) * P], rhs[k], start=k == 0, stop=k == K - 1)
                return i

            with pe.Fori(0, B) as c:
                pe.wait_ge(*X1["dve"].before(c))
                ln_pe(pe, X1, c, c)
                pe.wait_ge(*X1["dve"].after("ctxb", c))
                cx = [ctxb[:, k, 0:C] for k in range(K)]
                for o in range(K):
                    i = proj(bank[2][:, o * C:(o + 1) * C], WKS, o, cx)
                i.then_inc(L.sem, 1)
                for o in range(K):
                    i = proj(bank[3][:, o * C:(o + 1) * C], WQS, o, cx)
                i.then_inc(L.sem, 1)
                for k in range(K):
                    i = nc.tensor.matmul(bank[4][0:C, 0:D], cx[k], w_x1[:, WVS, k, :], start=k == 0, stop=k == K - 1)
                i.then_inc(L.sem, 1)
                pe.wait_ge(*X1["dve"].after("normed", c))
                nbk = [nb[:, k, :] for k in range(K)]
                proj(bank[5][:, :], WQC, 0, nbk).then_inc(L.sem, 1)
                proj(bank[6][:, :], WQC, 1, nbk).then_inc(L.sem, 1)
                proj(bank[7][:, :], WKC, 0, nbk).then_inc(L.sem, 1)
                proj(bank[0][:, :], WKC, 1, nbk).then_inc(L.sem, 1)
                pe.wait_ge(*X1["act"].after("qs", c))
                for q in range(QT):
                    for k in range(K):
                        i = nc.tensor.matmul(bank[2 + q // 2][:, q % 2 * D:q % 2 * D + D], nb[:, k, q * P:(q + 1) * P],
                                             w_x1[:, WVC, k, :], start=k == 0, stop=k == K - 1)
                i.then_inc(L.sem, 1)
                pe.wait_ge(*X1["act"].after("kc1", c))
                for q in range(QT):
                    for o in range(K):
                        i = nc.tensor.matmul(bank[1][:, q * C:(q + 1) * C], qcT[:, o, q * P:(q + 1) * P], ksT[:, o, :],
                                             start=o == 0, stop=o == K - 1)
                i.then_inc(L.sem, 1)
                for o in range(K):
                    i = nc.tensor.matmul(bank[4][0:C, :], qsT[:, o, :], kcT[:, o, :], start=o == 0, stop=o == K - 1)
                i.then_inc(L.sem, 1)
                pe.wait_ge(*X1["dve"].after("p1", c))
                for q in range(QT):
                    i = nc.tensor.matmul(bank[5][0:C, q * P:(q + 1) * P], s1[:, q, :], ident, start=True, stop=True)
                i.then_inc(L.sem, 1)
                pe.wait_ge(*X1["dve"].after("p2", c))
                for q in range(QT):
                    i = nc.tensor.matmul(bank[6][:, q * C:(q + 1) * C], s2[:, q * P:(q + 1) * P], ident[0:C, 0:C],
                                         start=True, stop=True)
                i.then_inc(L.sem, 1)
                pe.wait_ge(*X1["dve"].after("s1T", c))
                for o in range(K):
                    nc.tensor.matmul(bank[7 * (1 - o)][:, :], vs[:, o * P:(o + 1) * P], s1T, start=True,
                                     stop=True).then_inc(L.sem, 1)
                pe.wait_ge(*X1["dve"].after("s2T", c))
                pe.wait_ge(*X1["act"].after("vc", c))
                for q in range(QT):
                    i = nc.tensor.matmul(bank[2][0:C, 0:D], s2T[:, q, :], vc[:, q, :], start=q == 0, stop=q == QT - 1)
                i.then_inc(L.sem, 1)
                pe.wait_ge(*X1["dve"].after("s2o", c))
                for o in range(K):
                    nc.tensor.matmul(bank[3 + o][:, :], s2o[:, o * P:(o + 1) * P], const("interp")[0:C, :], start=True,
                                     stop=True).then_inc(L.sem, 1)
                pe.wait_ge(*X1["act"].after("s2c1", c))
                for o in range(K):
                    for m in range(2 * K):
                        r = c2s[:, m, :] if m < K else s2c[:, m - K, :]
                        i = nc.tensor.matmul(bank[5 + o][:, :], w_g[:, m, o * P:(o + 1) * P], r, start=m == 0,
                                             stop=m == 2 * K - 1)
                    i.then_inc(L.sem, 1)

        def x1_act(act):
            L = X1["act"]
            finished(act, F0, E * B)
            act.wait_ge(*X1C.before(1))
            with act.Fori(0, B) as c:
                ln_act(act, X1, c)

                def evac(dst, ps, step, bias, scale=1.0, func=ACT.Identity):
                    act.wait_ge(*X1["pe"].after(step, c))
                    nc.scalar.activation(dst, ps, func, bias=bias, scale=scale).then_inc(L.sem, 1)

                def evac2(dst, b, step, bias):
                    act.wait_ge(*X1["pe"].after(step, c))
                    for o in range(K):
                        i = nc.scalar.activation(dst[:, o, :], bank[b][:, o * C:(o + 1) * C], ACT.Identity, bias=v_(bias, o))
                    i.then_inc(L.sem, 1)

                evac2(ksT, 2, "ks", "bk_s")
                evac2(qsT, 3, "qs", "bq_s")
                act.wait_ge(*X1["pe"].after("vs", c))
                nc.scalar.activation(vs, bank[4][0:C, 0:D], ACT.Copy).then_inc(L.sem, 1)
                evac(qcT[:, 0, :], bank[5][:, :], "qc0", v_("bq_c", 0))
                evac(qcT[:, 1, :], bank[6][:, :], "qc1", v_("bq_c", 1))
                evac(kcT[:, 0, :], bank[7][:, :], "kc0", v_("bk_c", 0))
                evac(kcT[:, 1, :], bank[0][:, :], "kc1", v_("bk_c", 1))
                act.wait_ge(*X1["pe"].after("vc", c))
                for u in range(2):
                    i = nc.scalar.activation(vc[:, 2 * u:2 * u + 2, :].rearrange("p q d -> p (q d)"), bank[2 + u][:, :],
                                             ACT.Copy)
                i.then_inc(L.sem, 1)
                act.wait_ge(*X1["dve"].after("shift1", c))
                nc.scalar.activation(s1, s1, ACT.Exp, scale=SC1).then_inc(L.sem, 1)
                act.wait_ge(*X1["dve"].after("nmx2", c))
                nc.scalar.activation(s2, bank[4][0:C, :], ACT.Exp, scale=SC1, bias=mx2[0:C, :],
                                     accum_out=sum2[0:C, :]).then_inc(L.sem, 1)
                evac(c2s[:, 0, :], bank[7][:, :], "c2s0", v_("bv_s", 0))
                evac(c2s[:, 1, :], bank[0][:, :], "c2s1", v_("bv_s", 1))
                evac(s2c[:, 0, :], bank[3][:, :], "s2c0", v_("bv_c", 0))
                evac(s2c[:, 1, :], bank[4][:, :], "s2c1", v_("bv_c", 1))
                evac(gate1[:, 0, :], bank[5][:, :], "gate0", bgh[:, 0:1], 0.5, ACT.Tanh)
                evac(gate1[:, 1, :], bank[6][:, :], "gate1", bgh[:, 1:2], 0.5, ACT.Tanh)

        def x1_dve(dve):
            L = X1["dve"]
            finished(dve, F0, E * B)
            nc.vector.tensor_scalar(bgh[:, :], v_("bg", 0, K), 0.5, None, ALU.mult).then_inc(X1C.sem, 1)
            nc.vector.tensor_scalar(tg1h[:, :], tgx[:, 1:2], 0.5, None, ALU.mult).then_inc(X1C.sem, 1)
            with dve.Fori(0, B) as c:
                dve.wait_ge(*X1["pe"].before(c))
                nc.vector.tensor_copy(ctxb[:, :, 0:C], ctxT[:, :, bass.ds(c * C, C)]).then_inc(L.sem, 1)
                ln_dve(dve, X1, c, c)
                dve.wait_ge(*X1["pe"].after("s1", c))
                sc = bank[1][:, 0:QT * C].rearrange("p (q n) -> p q n", q=QT)
                nc.vector.tensor_reduce(mx1[:, :], sc, AX.X, ALU.max).then_inc(L.sem, 1)
                dve.wait_ge(*X1["pe"].after("s2", c))
                nc.vector.tensor_reduce(mx2[0:C, :], bank[4][0:C, :], AX.X, ALU.max).then_inc(L.sem, 1)
                dve.wait_ge(*L.after("mx2", c))
                nc.vector.tensor_scalar(mx2[0:C, :], mx2[0:C, :], -SC1, None, ALU.mult).then_inc(L.sem, 1)
                nc.vector.tensor_tensor(s1, sc, bcast(mx1[:, :], C), ALU.subtract).then_inc(L.sem, 1)
                dve.wait_ge(*X1["act"].after("e1", c))
                nc.vector.tensor_reduce(sum1[:, :], s1, AX.X, ALU.add).then_inc(L.sem, 1)
                dve.wait_ge(*L.after("sum1", c))
                nc.vector.reciprocal(sum1[:, :], sum1[:, :]).then_inc(L.sem, 1)
                dve.wait_ge(*L.after("rsum1", c))
                nc.vector.tensor_tensor(s1, s1, bcast(sum1[:, :], C), ALU.mult).then_inc(L.sem, 1)
                dve.wait_ge(*X1["act"].after("e2", c))
                nc.vector.reciprocal(sum2[0:C, :], sum2[0:C, :]).then_inc(L.sem, 1)
                dve.wait_ge(*L.after("rsum2", c))
                nc.vector.tensor_scalar(s2, s2, sum2[0:C, 0:1], None, ALU.mult).then_inc(L.sem, 1)
                dve.wait_ge(*X1["pe"].after("s1T", c))
                nc.vector.tensor_copy(s1T, bank[5][0:C, :]).then_inc(L.sem, 1)
                dve.wait_ge(*X1["pe"].after("s2T", c))
                nc.vector.tensor_copy(s2T, bank[6][:, 0:QT * C].rearrange("p (q n) -> p q n", q=QT)).then_inc(L.sem, 1)
                dve.wait_ge(*X1["pe"].after("s2o", c))
                nc.vector.tensor_copy(s2o, bank[2][0:C, 0:D]).then_inc(L.sem, 1)
                dve.wait_ge(*X1["act"].after("s2c1", c))
                nc.vector.tensor_tensor(mix, c2s, s2c, ALU.subtract).then_inc(L.sem, 1)
                dve.wait_ge(*X1["act"].after("gate1", c))
                dve.wait_ge(*L.after("diff", c))
                nc.vector.scalar_tensor_tensor(mix, gate1, 1.0, mix, ALU.add, ALU.mult).then_inc(L.sem, 1)
                dve.wait_ge(*L.after("prod", c))
                nc.vector.scalar_tensor_tensor(mix, s2c, 2.0, mix, ALU.mult, ALU.add).then_inc(L.sem, 1)
                dve.wait_ge(*L.after("mix", c))
                for k in range(K):
                    xs = xT[:, k, bass.ds(c * S, S)]
                    nc.vector.scalar_tensor_tensor(xs, mix[:, k, :], tg1h[:, 0:1], xs, ALU.mult, ALU.add).then_inc(L.sem, 1)

        F1, f1_route_sp, f1_sp, f1_route_pe, f1_pe, f1_route_act, f1_act, f1_route_dve, f1_dve = \
            expert_layer(1, X1, B)

        in_x2 = sem("in_x2")
        w_s, w_w = cols(bigB, 0, (K, D)), cols(bigB, 512, (K, D))
        mask_i = cols(bigB, 1024, (1, B * C))[:, 0, :].bitcast(I32)
        mask = bigB[:, 1280:1536]
        wcr = cols(bigB, 1536, (2, K * P))
        u2 = cols(bigB, 2048, (2, B * C))
        txtT = cols(bigB, 2560, (K, B * C))
        ones_at = bigB[:, 3072:3072 + 2 * C]
        NH2, NR2 = 4, 3
        h2 = [cols(bigA, i * 1024, (K, S)) for i in range(NH2)]
        r2 = cols(bigA, 4096, (NR2, S))
        rhoT = bigA[0:C, 5632:6144]
        rho = cols(bigA, 6144, (QT, C))
        eu = cols(bigA, 6400, (QT, C))
        diag = cols(bigA, 6656, (2, S))
        y2 = cols(bigA, 0, (K, S))
        WEIGHED = ["m0"] + [w for t in range(C) for w in ([f"m{t + 1}"] if t + 1 < C else []) + [f"r{t}"]]
        ws = sb("ws", [P, 2, QT])
        X2S = lines("x2_setup", pe=("txt0", "txt1", "u0", "u1"), act=("txt0", "txt1", "u0", "u1"),
                    dve=("mask_f", "mask", "wcr0", "wcr1", "zeros", "one"))
        X2 = lines("x2", pe=(*LN_PE, "feat0", "feat1", *(f"rho{t}" for t in range(C)), "rhoT", "bc0", "bc1"),
                   act=(*LN_ACT, *(f"h{t}" for t in range(C)), "rhoT", "exp", "ws", "bs"),
                   dve=(*LN_DVE, *WEIGHED, "masked", "mx", "shift", "sum", "rsum",
                        "ew", "sw", "eb", "sb", "nw", "nb_", "diag", "scaled", "moved", "x0", "x1"))

        def x2_load(sp):
            finished(sp, X1, B)
            sp.dma_start(w_s, dram["x2_ws"]).then_inc(in_x2, 16)
            sp.dma_start(w_w, dram["x2_w"]).then_inc(in_x2, 16)
            sp.dma_start(mask_i, dram["mask"]).then_inc(in_x2, 16)

        def x2_pe(pe):
            finished(pe, F1, E * B)
            pe.wait_ge(in_x2, 48)
            pe.wait_ge(*X2S["dve"].before(1))
            for a in range(K):
                for k in range(K):
                    i = nc.tensor.matmul(bank[a][:, 0:B * C], w_s[:, k, a * P:(a + 1) * P], ctxT[:, k, :],
                                         start=k == 0, stop=k == K - 1)
                i.then_inc(X2S["pe"].sem, 1)
            for m in range(2):
                for k in range(K):
                    i = nc.tensor.matmul(bank[2 + m][:, 0:B * C], wcr[:, m, k * P:(k + 1) * P], ctxT[:, k, :],
                                         start=k == 0, stop=k == K - 1)
                i.then_inc(X2S["pe"].sem, 1)
            pe.wait_ge(*X2S["act"].before(1))
            L = X2["pe"]
            with pe.Fori(0, B) as c:
                pe.wait_ge(*X2["dve"].before(c))
                ln_pe(pe, X2, c, c)
                pe.wait_ge(*X2["dve"].after("normed", c))
                for a in range(K):
                    for k in range(K):
                        i = nc.tensor.matmul(bank[2 + a][:, :], w_w[:, k, a * P:(a + 1) * P], nb[:, k, :],
                                             start=k == 0, stop=k == K - 1)
                    i.then_inc(L.sem, 1)
                for t in range(C):
                    pe.wait_ge(*X2["dve"].after(f"r{t}", c))
                    i = nc.tensor.matmul(bank[4][0:C, :], ones_at[:, C - 1 - t:2 * C - 1 - t], r2[:, t % NR2, :],
                                         start=t == 0, stop=t == C - 1)
                    i.then_inc(L.sem, 1)
                pe.wait_ge(*X2["act"].after("rhoT", c))
                for q in range(QT):
                    i = nc.tensor.matmul(bank[5][:, q * C:(q + 1) * C], rhoT[:, q * P:(q + 1) * P], ident[0:C, 0:C],
                                         start=True, stop=True)
                i.then_inc(L.sem, 1)
                pe.wait_ge(*X2["dve"].after("diag", c))
                for m in range(2):
                    i = nc.tensor.matmul(bank[6 + m][:, :], ones, diag[:, m, :], start=True, stop=True)
                    i.then_inc(L.sem, 1)

        def x2_act(act):
            finished(act, F1, E * B)
            L = X2S["act"]
            for a in range(K):
                act.wait_ge(*X2S["pe"].after(f"txt{a}"))
                nc.scalar.activation(txtT[:, a, :], bank[a][:, 0:B * C], ACT.Identity, bias=v_("ab", a)).then_inc(L.sem, 1)
            for m in range(2):
                act.wait_ge(*X2S["pe"].after(f"u{m}"))
                nc.scalar.activation(u2[:, m, :], bank[2 + m][:, 0:B * C], ACT.Copy).then_inc(L.sem, 1)
            act.wait_ge(*L.before(1))
            L = X2["act"]
            with act.Fori(0, B) as c:
                ln_act(act, X2, c)
                act.wait_ge(*X2["pe"].after("feat1", c))
                for t in range(C):
                    if t >= NH2:
                        act.wait_ge(*X2["dve"].after(f"r{t - NH2}", c))
                    for a in range(K):
                        i = nc.scalar.activation(h2[t % NH2][:, a, :], bank[2 + a][:, :], ACT.Tanh,
                                                 bias=txtT[:, a, bass.ds(c * C + t, 1)])
                    i.then_inc(L.sem, 1)
                act.wait_ge(*X2["pe"].after(f"rho{C - 1}", c))
                nc.scalar.activation(rhoT, bank[4][0:C, :], ACT.Copy).then_inc(L.sem, 1)
                act.wait_ge(*X2["dve"].after("shift", c))
                nc.scalar.activation(rho, rho, ACT.Exp).then_inc(L.sem, 1)
                act.wait_ge(*X2["dve"].after("nb_", c))
                nc.scalar.activation(ws[:, 0, :], ws[:, 0, :], ACT.Tanh, bias=v_("bcw")).then_inc(L.sem, 1)
                nc.scalar.activation(ws[:, 1, :], ws[:, 1, :], ACT.Tanh, bias=v_("bcb")).then_inc(L.sem, 1)

        def x2_dve(dve):
            finished(dve, F1, E * B)
            dve.wait_ge(in_x2, 48)
            L = X2S["dve"]
            nc.vector.tensor_copy(mask, mask_i).then_inc(L.sem, 1)
            dve.wait_ge(*L.after("mask_f"))
            nc.vector.tensor_scalar(mask, mask, NEG, NEG, ALU.mult, ALU.subtract).then_inc(L.sem, 1)
            for m, n in enumerate(("wcw", "wcb")):
                nc.vector.tensor_copy(wcr[:, m, :].rearrange("p (k a) -> p k a", k=K), bcast(v_(n, 0, K), P)).then_inc(L.sem, 1)
            nc.vector.memset(ones_at, 0.0).then_inc(L.sem, 1)
            dve.wait_ge(*L.after("zeros"))
            nc.vector.memset(ones_at[:, C - 1:C], 1.0).then_inc(L.sem, 1)
            dve.wait_ge(*X2S["act"].before(1))
            dve.wait_ge(*L.before(1))
            L = X2["dve"]
            with dve.Fori(0, B) as c:
                ln_dve(dve, X2, c, c)

                def weigh(t):
                    dve.wait_ge(*X2["act"].after(f"h{t}", c))
                    if t >= NR2:
                        dve.wait_ge(*X2["pe"].after(f"rho{t - NR2}", c))
                    nc.vector.tensor_scalar(r2[:, t % NR2, :], h2[t % NH2][:, 0, :], v_("aw", 0), None,
                                            ALU.mult).then_inc(L.sem, 1)

                weigh(0)
                for t in range(C):
                    if t + 1 < C:
                        weigh(t + 1)
                    dve.wait_ge(*L.after(f"m{t}", c))
                    nc.vector.scalar_tensor_tensor(r2[:, t % NR2, :], h2[t % NH2][:, 1, :], v_("aw", 1), r2[:, t % NR2, :],
                                                   ALU.mult, ALU.add).then_inc(L.sem, 1)
                dve.wait_ge(*X2["pe"].after("rhoT", c))
                nc.vector.tensor_tensor(rho, bank[5][:, 0:QT * C].rearrange("p (q n) -> p q n", q=QT),
                                        over(mask[:, bass.ds(c * C, C)], QT), ALU.add).then_inc(L.sem, 1)
                dve.wait_ge(*L.after("masked", c))
                nc.vector.tensor_reduce(mx1[:, :], rho, AX.X, ALU.max).then_inc(L.sem, 1)
                dve.wait_ge(*L.after("mx", c))
                nc.vector.tensor_tensor(rho, rho, bcast(mx1[:, :], C), ALU.subtract).then_inc(L.sem, 1)
                dve.wait_ge(*X2["act"].after("exp", c))
                nc.vector.tensor_reduce(sum1[:, :], rho, AX.X, ALU.add).then_inc(L.sem, 1)
                dve.wait_ge(*L.after("sum", c))
                nc.vector.reciprocal(sum1[:, :], sum1[:, :]).then_inc(L.sem, 1)
                for m, (w, s_) in enumerate((("ew", "sw"), ("eb", "sb"))):
                    if m:
                        dve.wait_ge(*L.after("sw", c))
                    nc.vector.tensor_tensor(eu, rho, over(u2[:, m, bass.ds(c * C, C)], QT), ALU.mult).then_inc(L.sem, 1)
                    dve.wait_ge(*L.after(w, c))
                    nc.vector.tensor_reduce(ws[:, m, :], eu, AX.X, ALU.add).then_inc(L.sem, 1)
                dve.wait_ge(*L.after("sb", c))
                nc.vector.tensor_tensor(ws[:, 0, :], ws[:, 0, :], sum1[:, :], ALU.mult).then_inc(L.sem, 1)
                nc.vector.tensor_tensor(ws[:, 1, :], ws[:, 1, :], sum1[:, :], ALU.mult).then_inc(L.sem, 1)
                dve.wait_ge(*X2["act"].after("bs", c))
                for m in range(2):
                    for q in range(QT):
                        i = nc.vector.tensor_scalar(diag[:, m, q * P:(q + 1) * P], ident, ws[:, m, q:q + 1], None, ALU.mult)
                i.then_inc(L.sem, 1)
                dve.wait_ge(*X2["pe"].after("bc0", c))
                nc.vector.tensor_tensor(y2, nb[:, :, :], over(bank[6][:, :], K), ALU.mult).then_inc(L.sem, 1)
                dve.wait_ge(*X2["pe"].after("bc1", c))
                dve.wait_ge(*L.after("scaled", c))
                nc.vector.tensor_tensor(y2, y2, over(bank[7][:, :], K), ALU.add).then_inc(L.sem, 1)
                dve.wait_ge(*L.after("moved", c))
                for k in range(K):
                    xs = xT[:, k, bass.ds(c * S, S)]
                    nc.vector.scalar_tensor_tensor(xs, y2[:, k, :], tgx[:, 2:3], xs, ALU.mult, ALU.add).then_inc(L.sem, 1)

        F2, f2_route_sp, f2_sp, f2_route_pe, f2_pe, f2_route_act, f2_act, f2_route_dve, f2_dve = \
            expert_layer(2, X2, B)

        in_x3 = sem("in_x3")
        HP = HEADS // 2
        w_q3, w_k3, w_v3 = (cols(bigB, 2048 * i, (K, INNER)) for i in range(3))
        w_o3 = cols(bigB, 6144, (HP, D))
        q3, p3T = cols(bigA, 0, (HP, S)), cols(bigA, 4096, (HP, S))
        o3 = cols(fh, 0, (HP, S))
        kbd = cols(fs, 0, (HP, 2 * C))
        vbd = cols(fs, 1024, (HP, 2 * DH))
        p3 = cols(fs, 2048, (HEADS, C))
        mx3, sum3 = sb("mx3", [P, HEADS]), sb("sum3", [P, HEADS])
        SC3 = DH ** -0.5
        TQ = range(QT)
        X3 = lines("x3", pe=(*LN_PE, "k", "v", *(f"q{i}" for i in range(HP)),
                             *(f"{w}{q}" for q in TQ for w in ("s", "pT")), *(f"o{i}" for i in range(HP)), "y0", "y1"),
                   act=(*LN_ACT, "k", "v", *(f"q{i}" for i in range(HP)), *(f"{w}{q}" for q in TQ for w in ("exp", "pT")),
                        *(f"o{i}" for i in range(HP)), "y0", "y1"),
                   dve=("ctx0", "ctx1", *LN_DVE, *(f"{w}{q}" for q in TQ for w in ("mx", "shift", "sum", "rsum", "p")),
                        "x0", "x1"))
        X3Z = line("x3_zero_dve", "k", "v")

        def x3_load(sp):
            finished(sp, X2, B)
            for dst, n in ((w_q3, "x3_wq"), (w_k3, "x3_wk"), (w_v3, "x3_wv"), (w_o3, "x3_wo")):
                sp.dma_start(dst, dram[n]).then_inc(in_x3, 16)

        def x3_pe(pe):
            finished(pe, F2, E * B)
            pe.wait_ge(in_x3, 64)
            L = X3["pe"]
            with pe.Fori(0, B) as c:
                pe.wait_ge(*X3["dve"].before(c))
                ln_pe(pe, X3, c, c)
                pe.wait_ge(*X3["dve"].after("ctx1", c))
                for h in range(HP):
                    for k in range(K):
                        i = nc.tensor.matmul(bank[2][:, h * C:(h + 1) * C], w_k3[:, k, h * P:(h + 1) * P], ctxb[:, k, 0:C],
                                             start=k == 0, stop=k == K - 1)
                i.then_inc(L.sem, 1)
                for u in range(2):
                    for k in range(K):
                        i = nc.tensor.matmul(bank[3 + u][:, :], ctxb[:, k, :], w_v3[:, k, u * 512:(u + 1) * 512],
                                             start=k == 0, stop=k == K - 1)
                i.then_inc(L.sem, 1)
                pe.wait_ge(*X3["dve"].after("normed", c))
                for h in range(HP):
                    if h >= 3:
                        pe.wait_ge(*X3["act"].after(f"q{h - 3}", c))
                    for k in range(K):
                        i = nc.tensor.matmul(bank[5 + h % 3][:, :], w_q3[:, k, h * P:(h + 1) * P], nb[:, k, :],
                                             start=k == 0, stop=k == K - 1)
                    i.then_inc(L.sem, 1)
                pe.wait_ge(*X3["act"].after(f"q{HP - 1}", c))

                def scores(q):
                    for h in range(HP):
                        i = nc.tensor.matmul(bank[q % 2 * 2 + h // 4][:, h % 4 * P:(h % 4 + 1) * P],
                                             q3[:, h, q * P:(q + 1) * P], kbd[:, h, :], start=True, stop=True)
                    i.then_inc(L.sem, 1)

                def turned(q):
                    pe.wait_ge(*X3["dve"].after(f"p{q}", c))
                    if q:
                        pe.wait_ge(*X3["act"].after(f"pT{q - 1}", c))
                    for h in range(HP):
                        i = nc.tensor.transpose(bank[4 + h // 4][:, h % 4 * P:(h % 4 + 1) * P],
                                                p3[:, 2 * h:2 * h + 2, :].rearrange("p h n -> p (h n)"), ident)
                    i.then_inc(L.sem, 1)

                for q in TQ:
                    scores(q)
                    turned(q)
                pe.wait_ge(*X3["act"].after(f"pT{QT - 1}", c))
                for h in range(HP):
                    if h >= 2:
                        pe.wait_ge(*X3["act"].after(f"o{h - 2}", c))
                    nc.tensor.matmul(bank[6 + h % 2][:, :], vbd[:, h, :], p3T[:, h, :], start=True, stop=True).then_inc(L.sem, 1)
                pe.wait_ge(*X3["act"].after(f"o{HP - 1}", c))
                for k in range(K):
                    for h in range(HP):
                        i = nc.tensor.matmul(bank[k][:, :], w_o3[:, h, k * P:(k + 1) * P], o3[:, h, :], start=h == 0,
                                             stop=h == HP - 1)
                    i.then_inc(L.sem, 1)

        def x3_act(act):
            finished(act, F2, E * B)
            act.wait_ge(*X3Z.before(1))
            L = X3["act"]
            with act.Fori(0, B) as c:
                ln_act(act, X3, c)
                act.wait_ge(*X3["pe"].after("k", c))
                for u in range(2):
                    i = nc.scalar.activation(kbd[u * 64:(u + 1) * 64, :, u * C:(u + 1) * C],
                                             bank[2][u * 64:(u + 1) * 64, :].rearrange("p (h n) -> p h n", h=HP), ACT.Copy)
                i.then_inc(L.sem, 1)
                act.wait_ge(*X3["pe"].after("v", c))
                for u in range(2):
                    for g in range(2):
                        src = bank[3 + g][u * 64:(u + 1) * 64, :].rearrange("p (h d) -> p h d", d=2 * DH)
                        i = nc.scalar.activation(vbd[u * 64:(u + 1) * 64, 4 * g:4 * g + 4, u * DH:(u + 1) * DH],
                                                 src[:, :, u * DH:(u + 1) * DH], ACT.Copy)
                i.then_inc(L.sem, 1)
                for h in range(HP):
                    act.wait_ge(*X3["pe"].after(f"q{h}", c))
                    nc.scalar.activation(q3[:, h, :], bank[5 + h % 3][:, :], ACT.Copy).then_inc(L.sem, 1)
                for q in TQ:
                    act.wait_ge(*X3["dve"].after(f"shift{q}", c))
                    nc.scalar.activation(p3, p3, ACT.Exp, scale=SC3).then_inc(L.sem, 1)
                    act.wait_ge(*X3["pe"].after(f"pT{q}", c))
                    for u in range(2):
                        i = nc.scalar.activation(p3T[:, 4 * u:4 * u + 4, q * P:(q + 1) * P],
                                                 bank[4 + u][:, :].rearrange("p (h q) -> p h q", h=4), ACT.Copy)
                    i.then_inc(L.sem, 1)
                for h in range(HP):
                    act.wait_ge(*X3["pe"].after(f"o{h}", c))
                    nc.scalar.activation(o3[:, h, :], bank[6 + h % 2][:, :], ACT.Copy).then_inc(L.sem, 1)
                for k in range(K):
                    act.wait_ge(*X3["pe"].after(f"y{k}", c))
                    nc.scalar.activation(sq[:, k, :], bank[k][:, :], ACT.Identity, bias=v_("bo", k)).then_inc(L.sem, 1)

        def x3_dve(dve):
            finished(dve, F2, E * B)
            nc.vector.memset(kbd, 0.0).then_inc(X3Z.sem, 1)
            nc.vector.memset(vbd, 0.0).then_inc(X3Z.sem, 1)
            L = X3["dve"]
            with dve.Fori(0, B) as c:
                dve.wait_ge(*X3["pe"].before(c))
                for u in range(2):
                    nc.vector.tensor_copy(ctxb[:, :, u * C:(u + 1) * C], ctxT[:, :, bass.ds(c * C, C)]).then_inc(L.sem, 1)
                ln_dve(dve, X3, c, c)
                for q in TQ:
                    dve.wait_ge(*X3["pe"].after(f"s{q}", c))
                    if q:
                        dve.wait_ge(*X3["pe"].after(f"pT{q - 1}", c))
                    for u in range(2):
                        i = nc.vector.tensor_reduce(mx3[:, 8 * u:8 * u + 8],
                                                    bank[q % 2 * 2 + u][:, :].rearrange("p (h n) -> p h n", n=C),
                                                    AX.X, ALU.max)
                    i.then_inc(L.sem, 1)
                    dve.wait_ge(*L.after(f"mx{q}", c))
                    for u in range(2):
                        i = nc.vector.tensor_tensor(p3[:, 8 * u:8 * u + 8, :],
                                                    bank[q % 2 * 2 + u][:, :].rearrange("p (h n) -> p h n", n=C),
                                                    bcast(mx3[:, 8 * u:8 * u + 8], C), ALU.subtract)
                    i.then_inc(L.sem, 1)
                    dve.wait_ge(*X3["act"].after(f"exp{q}", c))
                    nc.vector.tensor_reduce(sum3[:, :], p3, AX.X, ALU.add).then_inc(L.sem, 1)
                    dve.wait_ge(*L.after(f"sum{q}", c))
                    nc.vector.reciprocal(sum3[:, :], sum3[:, :]).then_inc(L.sem, 1)
                    dve.wait_ge(*L.after(f"rsum{q}", c))
                    nc.vector.tensor_tensor(p3, p3, bcast(sum3[:, :], C), ALU.mult).then_inc(L.sem, 1)
                for k in range(K):
                    dve.wait_ge(*X3["act"].after(f"y{k}", c))
                    xs = xT[:, k, bass.ds(c * S, S)]
                    nc.vector.scalar_tensor_tensor(xs, sq[:, k, :], tgx[:, 3:4], xs, ALU.mult, ALU.add).then_inc(L.sem, 1)

        in_f3, sent = sem("in_f3"), sem("sent")
        rhsT = cols(wflat, 0, (K, D))
        rq32 = cols(wflat, 512, (K, D))
        rqT = cols(wflat, 1024, (K, D), BF16)
        rq = cols(wflat, 1280, (K, D), BF16)
        identb = cols(wflat, 1536, (1, P), BF16)[:, 0, :]
        rdiag = cols(wflat, 1600, (1, D))[:, 0, :]
        rsb = cols(wflat, 1856, (1, D))[:, 0, :]
        rs, rinv = sb("rs", [P, K]), sb("rinv", [P, K])
        xt = cols(bigA, 0, (T, D))
        xn = cols(bigA, 4096, (T, D))
        q_tok = cols(fn, 0, (T, D), BF16)
        q_f = cols(fh, 0, (K, N), BF16)
        yo = cols(bigB, 0, (T, D))
        stats, mv = sb("stats", [P, T, 6]), sb("mv", [P, T, 2])
        std = sb("std", [P, T])
        ls, linv = sb("ls", [P, T]), sb("linv", [P, T])
        F3 = lines("f3", pe=(*(f"x{i}" for i in range(T)), "rq", "rsb", *(f"q{i}" for i in range(T)), *(f"y{i}" for i in range(T))),
                   act=(*(f"x{i}" for i in range(T)), "std", *(f"q{i}" for i in range(T))),
                   dve=("identb", "rmax", "rs", "rinv", "rmul", "rround", "rclip", "rq", "rdiag0", "rdiag1", "rsb",
                        *(f"stats{i}" for i in range(T)), *(f"mv{i}" for i in range(T)),
                        "eps", "rstd", *(f"n{i}" for i in range(T)), "amax", "ls", "linv", *(f"mul{i}" for i in range(T)), "round", "clip",
                        *(f"{w}{i}" for i in range(T) for w in ("y", "x"))))

        def f3_sp(sp):
            finished(sp, F2, E * B)
            sp.dma_start(rhsT, dram["f3_rhsT"]).then_inc(in_f3, 16)
            for i in range(T):
                sp.wait_ge(*F3["dve"].after(f"x{i}"))
                sp.dma_start(out[i * P:(i + 1) * P, :], yo[:, i, :]).then_inc(sent, 16)
            sp.wait_ge(sent, 16 * T)

        def f3_pe(pe):
            finished(pe, X3, B)
            L = F3["pe"]
            for i in range(T):
                if i >= 4:
                    pe.wait_ge(*F3["act"].after(f"x{i - 4}"))
                for k in range(K):
                    m = nc.tensor.transpose(bank[i % 4][:, k * P:(k + 1) * P], xT[:, k, i * P:(i + 1) * P], ident)
                m.then_inc(L.sem, 1)
            pe.wait_ge(*F3["dve"].after("rclip"))
            b16 = bank[4][:, 0:2 * P].bitcast(BF16)
            for k in range(K):
                for o in range(K):
                    m = nc.tensor.transpose(b16[:, (k * K + o) * P:(k * K + o + 1) * P], rqT[:, o, k * P:(k + 1) * P], identb)
            m.then_inc(L.sem, 1)
            pe.wait_ge(*F3["dve"].after("rdiag1"))
            nc.tensor.matmul(bank[5][:, 0:D], ones, rdiag, start=True, stop=True).then_inc(L.sem, 1)
            pe.wait_ge(*F3["dve"].after("clip"))
            for i in range(T):
                if i >= 2:
                    pe.wait_ge(*F3["act"].after(f"q{i - 2}"))
                bq = bank[6 + i % 2][:, 0:P].bitcast(BF16)
                for k in range(K):
                    m = nc.tensor.transpose(bq[:, k * P:(k + 1) * P], q_tok[:, i, k * P:(k + 1) * P], identb)
                m.then_inc(L.sem, 1)
            for i in range(T):
                pe.wait_ge(*F3["act"].after(f"q{i}"))
                if i >= 4:
                    pe.wait_ge(*F3["dve"].after(f"y{i - 4}"))
                for k in range(K):
                    m = nc.tensor.matmul(bank[i % 4][:, 0:D], q_f[:, k, i * P:(i + 1) * P], rq[:, k, :], start=k == 0,
                                         stop=k == K - 1)
                m.then_inc(L.sem, 1)

        def f3_act(act):
            finished(act, X3, B)
            L = F3["act"]
            for i in range(T):
                act.wait_ge(*F3["pe"].after(f"x{i}"))
                nc.scalar.activation(xt[:, i, :], bank[i % 4][:, 0:D], ACT.Copy).then_inc(L.sem, 1)
            act.wait_ge(*F3["dve"].after("eps"))
            nc.scalar.activation(std[:, :], std[:, :], ACT.Sqrt).then_inc(L.sem, 1)
            for i in range(T):
                act.wait_ge(*F3["pe"].after(f"q{i}"))
                bq = bank[6 + i % 2][:, 0:P].bitcast(BF16)
                nc.scalar.activation(q_f[:, :, i * P:(i + 1) * P], bq.rearrange("p (k q) -> p k q", k=K),
                                     ACT.Copy).then_inc(L.sem, 1)

        def f3_dve(dve):
            finished(dve, X3, B)
            dve.wait_ge(in_f3, 16)
            L = F3["dve"]
            nc.vector.tensor_copy(identb, ident).then_inc(L.sem, 1)
            nc.vector.tensor_reduce(rs[:, :], rhsT, AX.X, ALU.max, apply_absolute_value=True).then_inc(L.sem, 1)
            dve.wait_ge(*L.after("rmax"))
            nc.vector.tensor_scalar(rs[:, :], rs[:, :], 1e-12, 1.0 / 127.0, ALU.max, ALU.mult).then_inc(L.sem, 1)
            dve.wait_ge(*L.after("rs"))
            nc.vector.reciprocal(rinv[:, :], rs[:, :]).then_inc(L.sem, 1)
            dve.wait_ge(*L.after("rinv"))
            for k in range(K):
                i = nc.vector.tensor_scalar(rq32[:, k, :], rhsT[:, k, :], rinv[:, k:k + 1], ROUND, ALU.mult, ALU.add)
            i.then_inc(L.sem, 1)
            dve.wait_ge(*L.after("rmul"))
            nc.vector.tensor_scalar(rq32, rq32, ROUND, 127.0, ALU.subtract, ALU.min).then_inc(L.sem, 1)
            dve.wait_ge(*L.after("rround"))
            nc.vector.tensor_scalar(rqT, rq32, -127.0, None, ALU.max).then_inc(L.sem, 1)
            dve.wait_ge(*F3["pe"].after("rq"))
            nc.vector.tensor_copy(rq.rearrange("p k d -> p (k d)"), bank[4][:, 0:2 * P].bitcast(BF16)).then_inc(L.sem, 1)
            for k in range(K):
                nc.vector.tensor_scalar(rdiag[:, k * P:(k + 1) * P], ident, rs[:, k:k + 1], None, ALU.mult).then_inc(L.sem, 1)
            dve.wait_ge(*F3["pe"].after("rsb"))
            nc.vector.tensor_copy(rsb, bank[5][:, 0:D]).then_inc(L.sem, 1)
            for i in range(T):
                dve.wait_ge(*F3["act"].after(f"x{i}"))
                nc.vector.bn_stats(stats[:, i, :], xt[:, i, :]).then_inc(L.sem, 1)
            for i in range(T):
                dve.wait_ge(*L.after(f"stats{i}"))
                nc.vector.bn_aggr(mv[:, i, :], stats[:, i, :]).then_inc(L.sem, 1)
            dve.wait_ge(*L.after(f"mv{T - 1}"))
            nc.vector.tensor_scalar(std[:, :], mv[:, :, 1], EPS, None, ALU.add).then_inc(L.sem, 1)
            dve.wait_ge(*F3["act"].after("std"))
            nc.vector.reciprocal(std[:, :], std[:, :]).then_inc(L.sem, 1)
            dve.wait_ge(*L.after("rstd"))
            for i in range(T):
                nc.vector.tensor_scalar(xn[:, i, :], xt[:, i, :], mv[:, i, 0:1], std[:, i:i + 1], ALU.subtract,
                                        ALU.mult).then_inc(L.sem, 1)
            dve.wait_ge(*L.after(f"n{T - 1}"))
            nc.vector.tensor_reduce(ls[:, :], xn, AX.X, ALU.max, apply_absolute_value=True).then_inc(L.sem, 1)
            dve.wait_ge(*L.after("amax"))
            nc.vector.tensor_scalar(ls[:, :], ls[:, :], 1e-12, 1.0 / 127.0, ALU.max, ALU.mult).then_inc(L.sem, 1)
            dve.wait_ge(*L.after("ls"))
            nc.vector.reciprocal(linv[:, :], ls[:, :]).then_inc(L.sem, 1)
            dve.wait_ge(*L.after("linv"))
            for i in range(T):
                nc.vector.tensor_scalar(xn[:, i, :], xn[:, i, :], linv[:, i:i + 1], ROUND, ALU.mult, ALU.add).then_inc(L.sem, 1)
            dve.wait_ge(*L.after(f"mul{T - 1}"))
            nc.vector.tensor_scalar(xn, xn, ROUND, 127.0, ALU.subtract, ALU.min).then_inc(L.sem, 1)
            dve.wait_ge(*L.after("round"))
            nc.vector.tensor_scalar(q_tok, xn, -127.0, None, ALU.max).then_inc(L.sem, 1)
            for i in range(T):
                dve.wait_ge(*F3["pe"].after(f"y{i}"))
                nc.vector.scalar_tensor_tensor(yo[:, i, :], bank[i % 4][:, 0:D], ls[:, i:i + 1], rsb, ALU.mult,
                                               ALU.mult).then_inc(L.sem, 1)
                dve.wait_ge(*L.after(f"y{i}"))
                nc.vector.scalar_tensor_tensor(yo[:, i, :], yo[:, i, :], tgf[:, 3:4], xt[:, i, :], ALU.mult,
                                               ALU.add).then_inc(L.sem, 1)

        block = ctx.enter_context(nc.Block())

        @block.sync
        def _(sp):
            setup_sp(sp)
            lstm2_sp(sp)
            x1_load(sp)
            f0_route_sp(sp)
            f0_sp(sp)
            f1_route_sp(sp)
            x2_load(sp)
            f1_sp(sp)
            f2_route_sp(sp)
            x3_load(sp)
            f2_sp(sp)
            f3_sp(sp)

        @block.tensor
        def _(pe):
            opened(pe, "pe")
            setup_pe(pe)
            xproj_pe(pe)
            rec_pe(pe)
            lstm2_pe(pe)
            f0_route_pe(pe)
            f0_pe(pe)
            x1_pe(pe)
            f1_route_pe(pe)
            f1_pe(pe)
            x2_pe(pe)
            f2_route_pe(pe)
            f2_pe(pe)
            x3_pe(pe)
            f3_pe(pe)

        @block.gpsimd
        def _(pool):
            opened(pool, "pool")
            rec_pool(pool)

        @block.scalar
        def _(act):
            opened(act, "act")
            setup_act(act)
            xproj_act(act)
            rec_act(act)
            lstm2_act(act)
            f0_route_act(act)
            f0_act(act)
            x1_act(act)
            f1_route_act(act)
            f1_act(act)
            x2_act(act)
            f2_route_act(act)
            f2_act(act)
            x3_act(act)
            f3_act(act)

        @block.vector
        def _(dve):
            opened(dve, "dve")
            setup_dve(dve)
            xproj_dve(dve)
            rec_dve(dve)
            lstm2_dve(dve)
            f0_route_dve(dve)
            f0_dve(dve)
            x1_dve(dve)
            f1_route_dve(dve)
            f1_dve(dve)
            x2_dve(dve)
            f2_route_dve(dve)
            f2_dve(dve)
            x3_dve(dve)
            f3_dve(dve)


def feature_major(a):
    import numpy as np
    r, c = a.shape
    return np.ascontiguousarray(a.T.reshape(c // P, P, r).transpose(1, 0, 2))


def row_tiles(a):
    import numpy as np
    r, c = a.shape
    return np.ascontiguousarray(a.reshape(r // P, P, c).transpose(1, 0, 2))


def pack(inp):
    import numpy as np
    arr = {k: np.asarray(v) for k, v in inp.items()}

    def col(a):
        return a.reshape(-1, P).T

    def rep(a):
        return np.broadcast_to(a.reshape(1, -1), (P, a.size))

    x0, x1, x2, x3 = (f"L{i}_xattn_" for i in range(4))
    f0, f1, f2, f3 = (f"L{i}_ffn_" for i in range(4))
    vecs = dict(
        b_att=col(arr[x0 + "b_att"]), v=col(arr[x0 + "v"]),
        b_ih0=col(arr[x0 + "b_ih0"]), b_hh0=col(arr[x0 + "b_hh0"]),
        b_ih1=col(arr[x0 + "b_ih1"]), b_hh1=col(arr[x0 + "b_hh1"]),
        f0_b1=col(arr[f0 + "b1"]), f0_b2=col(arr[f0 + "b2"]), f0_br=rep(arr[f0 + "br"]),
        f2_b1=col(arr[f2 + "b1"]), f2_b2=col(arr[f2 + "b2"]), f2_br=rep(arr[f2 + "br"]),
        **{n: col(arr[x1 + n]) for n in ("bq_c", "bk_s", "bv_s", "bq_s", "bk_c", "bv_c", "bg")},
        ab=col(arr[x2 + "b"]), aw=col(arr[x2 + "w"]), wcw=col(arr[x2 + "Wcw"]), wcb=col(arr[x2 + "Wcb"]),
        bcw=rep(arr[x2 + "bcw"]), bcb=rep(arr[x2 + "bcb"]), bo=col(arr[x3 + "bo"]),
        gx=rep(arr["g_xattn"]), gf=rep(arr["g_ffn"]))
    vec = np.ascontiguousarray(np.concatenate([vecs[n] for n in VECS], axis=1))

    ident = np.eye(P, dtype=np.float32)
    p = np.arange(P)
    diag_b = (p[:, None] // 32 == np.arange(B)[None]).astype(np.float32)
    i, j = np.arange(E)[:, None], np.arange(E)[None]
    before, upto = ((j < i).astype(np.float32).reshape(1, -1), (j <= i).astype(np.float32).reshape(1, -1))
    pos = np.clip((np.arange(S) + 0.5) * (C / S) - 0.5, 0.0, C - 1)
    lo = np.floor(pos).astype(int)
    hi = np.minimum(lo + 1, C - 1)
    interp = np.zeros((P, S), np.float32)
    interp[lo, np.arange(S)] += (1.0 - (pos - lo)).astype(np.float32)
    interp[hi, np.arange(S)] += (pos - lo).astype(np.float32)
    consts = dict(ident=ident, ones=np.ones((P, P), np.float32), mean=np.full((P, P), 1.0 / D, np.float32),
                  diag_b=diag_b, before=np.broadcast_to(before, (P, E * E)), upto=np.broadcast_to(upto, (P, E * E)),
                  interp=interp)
    cst = np.ascontiguousarray(np.concatenate([consts[n] for n in CONSTS], axis=1), dtype=np.float32)

    ctx = arr["ctx_1024"].reshape(B * C, D)
    ctxq = arr["ctx_1024"].reshape(B, 2, 32, D).transpose(1, 0, 2, 3).reshape(B * C, D)
    w_ih0 = arr[x0 + "W_ih0"]
    w1x = np.stack([feature_major(arr[x1 + n]) for n in ("Wq_c", "Wk_s", "Wv_s", "Wq_s", "Wk_c", "Wv_c")], axis=1)
    mask = np.ascontiguousarray(np.broadcast_to(arr["mask_BxS2_ik0"].reshape(1, B * C), (P, B * C)))
    return dict(
        vec=vec, cst=cst, ctxT=feature_major(ctx), ctxTq=feature_major(ctxq), xT=feature_major(arr["x"].reshape(N, D)),
        w_f=row_tiles(arr[x0 + "Wf"]), w_h=row_tiles(arr[x0 + "Wh"]),
        w_x=feature_major(w_ih0[:, :D]), w_at=feature_major(w_ih0[:, D:]), w_hh=feature_major(arr[x0 + "W_hh0"]),
        w_ih1=feature_major(arr[x0 + "W_ih1"]), w_hh1=feature_major(arr[x0 + "W_hh1"]),
        f0_w1=np.stack([row_tiles(a) for a in arr[f0 + "w1"]]), f0_w2=np.stack([row_tiles(a) for a in arr[f0 + "w2"]]),
        f0_wr=row_tiles(arr[f0 + "wr"]),
        f1_w1=np.stack([row_tiles(a) for a in arr[f1 + "w1"]]), f1_w3=np.stack([row_tiles(a) for a in arr[f1 + "w3"]]),
        f1_w2=np.stack([row_tiles(a) for a in arr[f1 + "w2"]]), f1_wr=row_tiles(arr[f1 + "router_w"]),
        f2_w1=np.stack([row_tiles(a) for a in arr[f2 + "W1"]]), f2_w2=np.stack([row_tiles(a) for a in arr[f2 + "W2"]]),
        f2_wr=row_tiles(arr[f2 + "Wr"]),
        x1_w=np.ascontiguousarray(w1x), x1_wg=feature_major(arr[x1 + "Wg"]),
        x2_ws=row_tiles(arr[x2 + "Ws"]), x2_w=row_tiles(arr[x2 + "W"]), mask=mask,
        x3_wq=feature_major(arr[x3 + "Wq"]), x3_wk=feature_major(arr[x3 + "Wk"]), x3_wv=feature_major(arr[x3 + "Wv"]),
        x3_wo=feature_major(arr[x3 + "Wo"]), f3_rhsT=feature_major(arr[f3 + "rhs"]))


def kernel(**inputs):
    import numpy as np
    import concourse.bacc as bacc
    from concourse.bass_utils import run_bass_kernel_spmd

    arrays = pack(inputs)
    nc = bacc.Bacc("TRN2", target_bir_lowering=False, num_devices=1)
    dram = {n: nc.dram_tensor(f"in_{n}", a.shape, mybir.dt.from_np(a.dtype), kind="ExternalInput").ap()
            for n, a in arrays.items()}
    out = nc.dram_tensor("out_x", (N, D), F32, kind="ExternalOutput").ap()
    build(nc, dram, out)
    r = run_bass_kernel_spmd(nc, [{f"in_{n}": a for n, a in arrays.items()}], core_ids=[0])
    return np.asarray(r.results[0]["out_x"]).reshape(B, S, D)
```

```python
from contextlib import ExitStack

import concourse.bass as bass
from concourse import mybir
from concourse.alu_op_type import AluOpType as ALU

F32, BF16, F16, I32 = mybir.dt.float32, mybir.dt.bfloat16, mybir.dt.float16, mybir.dt.int32
ACT = mybir.ActivationFunctionType
AX = mybir.AxisListType

P = 128
B, S, C, D = 4, 512, 64, 256
N = B * S
K = D // P
E = 8
FW = 1024
FW1 = 512
HEADS, DH = 16, 64
INNER = HEADS * DH
NG = 4 * D // P
QT = S // P
EPS = 1e-5
ROUND = 1.5 * 2.0 ** 23
NEG = 1e30
HS = 16.0
WS = 64.0
GS = 256.0

VECS = ["b_att", "v", "b_ih0", "b_hh0", "b_ih1", "b_hh1", "f0_b1", "f0_b2", "f0_br", "f2_b1", "f2_b2", "f2_br",
        "bq_c", "bk_s", "bv_s", "bq_s", "bk_c", "bv_c", "bg", "ab", "aw", "wcw", "wcb", "bcw", "bcb", "bo", "gx", "gf"]
WIDTH = dict(b_att=K, v=K, b_ih0=NG, b_hh0=NG, b_ih1=NG, b_hh1=NG, f0_b1=E * FW // P, f0_b2=E * K, f0_br=E,
             f2_b1=E * FW // P, f2_b2=E * K, f2_br=E, bq_c=K, bk_s=K, bv_s=K, bq_s=K, bk_c=K, bv_c=K, bg=K,
             ab=K, aw=K, wcw=K, wcb=K, bcw=1, bcb=1, bo=K, gx=4, gf=4)
VCOL, at = {}, 0
for name in VECS:
    VCOL[name] = at
    at += WIDTH[name]
NVEC = at
CONSTS = dict(ident=P, ones=P, mean=P, diag_b=B, before=E * E, upto=E * E, interp=S)
CCOL, at = {}, 0
for name in CONSTS:
    CCOL[name] = at
    at += CONSTS[name]
NCONST = at


class Line:

    def __init__(self, sem, steps):
        self.sem, self.n = sem, len(steps)
        self.pos = {s: i + 1 for i, s in enumerate(steps)}
        assert len(self.pos) == self.n

    def after(self, step, it=0):
        return self.sem, it * self.n + (self.pos[step] + 1)

    def before(self, it):
        return self.sem, it * self.n + 1


def build(nc, dram, out):
    ctx = ExitStack()
    with ctx:
        def sb(name, shape, dt=F32):
            return ctx.enter_context(nc.sbuf_tensor(name, shape, dt))

        def sem(name):
            return ctx.enter_context(nc.semaphore(name))

        def line(name, *steps):
            every_line[name.rsplit("_", 1)[1]].append(Line(sem(name), steps))
            return every_line[name.rsplit("_", 1)[1]][-1]

        every_line = dict(pe=[], act=[], dve=[], pool=[])

        def opened(eng, name):
            for one in every_line[name]:
                eng.sem_inc(one.sem, 1)

        xT = sb("xT", [P, K, N])
        nT = sb("nT", [P, K, N])
        big = sb("big", [P, 2, 8192])
        wbuf = sb("wbuf", [P, 2, 4096])
        hist_h = sb("hist_h", [P, K, B, S + 1])
        hist_s = sb("hist_s", [P, K, B, S + 1])
        nb = sb("nb", [P, K, S])
        sq = sb("sq", [P, K, S])
        rstd = sb("rstd", [P, S])
        cst = sb("cst", [P, NCONST])
        vec = sb("vec", [P, NVEC])
        ctxT = sb("ctxT", [P, K, B * C])
        tgx = sb("tgx", [P, 4])
        tgf = sb("tgf", [P, 4])
        tgf_w = sb("tgf_w", [P, 4])
        ws_col, eps_col = sb("ws_col", [P, 1]), sb("eps_col", [P, 1])
        fo = sb("fo", [P, K, S])
        bank = [ctx.enter_context(nc.psum_tensor(f"bank{i}", [P, 512], F32)) for i in range(8)]

        def const(name):
            return cst[:, CCOL[name]:CCOL[name] + CONSTS[name]]

        def v_(name, i=0, n=1):
            return vec[:, VCOL[name] + i:VCOL[name] + i + n]

        ident, ones, mean_w = const("ident"), const("ones"), const("mean")

        def cols(t, off, shape, dt=F32):
            n = 1
            for s in shape:
                n *= s
            words = n * (2 if dt in (BF16, F16) else 4) // 4
            a = t[:, off:off + words]
            if dt != F32:
                a = a.bitcast(dt)
            if len(shape) == 2:
                a = a.rearrange("p (a b) -> p a b", a=shape[0])
            elif len(shape) == 3:
                a = a.rearrange("p (a b c) -> p a b c", a=shape[0], b=shape[1])
            return a

        def flat(t):
            n = len(t.shape)
            return t[:, :, :].rearrange("p a b -> p (a b)") if n == 3 else \
                t[:, :, :, :].rearrange("p a b c -> p (a b c)")

        bigA, bigB, wflat = big[:, 0, :], big[:, 1, :], flat(wbuf)
        fh, fs, fn = flat(hist_h), flat(hist_s), flat(nT)

        def bcast(a, n):
            return a.unsqueeze(2).to_broadcast([a.shape[0], a.shape[1], n])

        def over(a, m):
            return a.unsqueeze(1).to_broadcast([a.shape[0], m, a.shape[1]])

        LN_PE, LN_ACT = ("mean0", "mean1", "var0", "var1"), ("sq0", "sq1", "std0", "std1")
        LN_DVE = ("cent0", "cent1", "rstd0", "normed0", "rstd1", "normed1")

        def ln_buffers(second):
            return (nb[:, :, :], sq[:, :, :], rstd[:, :]), \
                (cols(second, 0, (K, S)), cols(second, K * S, (K, S)), second[:, 2 * K * S:2 * K * S + S])

        def x_of(c):
            return xT[:, :, bass.ds(c * S, S)]

        def ln_pe(pe, L, it, bufs):
            for u in range(2):
                for k in range(K):
                    i = nc.tensor.matmul(bank[2 * u][:, :], mean_w, xT[:, k, bass.ds((2 * it + u) * S, S)], start=k == 0,
                                         stop=k == K - 1)
                i.then_inc(L["pe"].sem, 1)
            for u, (_, squares, _) in enumerate(bufs):
                pe.wait_ge(*L["act"].after(f"sq{u}", it))
                for k in range(K):
                    i = nc.tensor.matmul(bank[2 * u + 1][:, :], mean_w, squares[:, k, :], start=k == 0, stop=k == K - 1)
                i.then_inc(L["pe"].sem, 1)

        def ln_act(act, L, it, bufs):
            for u, (centered, squares, _) in enumerate(bufs):
                act.wait_ge(*L["dve"].after(f"cent{u}", it))
                nc.scalar.activation(squares, centered, ACT.Square).then_inc(L["act"].sem, 1)
            for u, (_, _, dev) in enumerate(bufs):
                act.wait_ge(*L["pe"].after(f"var{u}", it))
                nc.scalar.activation(dev, bank[2 * u + 1][:, :], ACT.Sqrt, bias=eps_col[:, :]).then_inc(L["act"].sem, 1)

        def ln_dve(dve, L, it, bufs, dst=None):
            dve.wait_ge(*L["dve"].before(it))
            for u, (centered, _, _) in enumerate(bufs):
                dve.wait_ge(*L["pe"].after(f"mean{u}", it))
                nc.vector.tensor_tensor(centered, x_of(2 * it + u), over(bank[2 * u][:, :], K),
                                        ALU.subtract).then_inc(L["dve"].sem, 1)
            for u, (centered, _, dev) in enumerate(bufs):
                dve.wait_ge(*L["act"].after(f"std{u}", it))
                nc.vector.reciprocal(dev, dev).then_inc(L["dve"].sem, 1)
                dve.wait_ge(*L["dve"].after(f"rstd{u}", it))
                nc.vector.tensor_tensor(dst(2 * it + u) if dst else centered, centered, over(dev, K),
                                        ALU.mult).then_inc(L["dve"].sem, 1)

        def ln_lines(name):
            return lines(name, pe=LN_PE, act=LN_ACT, dve=LN_DVE)

        def normed(c):
            return nT[:, :, bass.ds(c * S, S)]

        def lines(name, **steps):
            return {e: line(f"{name}_{e}", *steps[e]) for e in steps}

        def finished(eng, L, iters=1):
            for e in L:
                eng.wait_ge(*L[e].before(iters))

        in_small, in_ctx, in_x, in_rec, in_l1 = (sem(n) for n in ("in_small", "in_ctx", "in_x", "in_rec", "in_l1"))
        xp = cols(flat(big), 0, (2 * NG * B, S), F16)
        xp_hi, xp_lo = (cols(big[:, u, :], 0, (NG, B, S), F16) for u in range(2))
        ctxTq = sb("ctxTq", [P, K, 2 * P])
        w_x = cols(fn, 0, (K, 4 * D))
        w_f, w_h32 = cols(fn, 2048, (K, D)), cols(fn, 2560, (K, D))
        w_hh32, w_at32 = cols(fh, 0, (K, 4 * D)), cols(fh, 2048, (K, 4 * D))
        g32 = cols(fs, 0, (2, 4 * D))
        whh = cols(wflat, 0, (2, K, 4 * D), F16)
        gat = cols(wflat, 2048, (2, 2, 4 * D), F16)
        wh = cols(wflat, 4096, (2, K, D), F16)
        h_t, s_t = sb("h_t", [P, K, B]), sb("s_t", [P, K, B])
        ident16 = sb("ident16", [P, P], F16)
        GROUPS = dict(f=(2, 3), ig=(0, 1, 4, 5), o=(6, 7))
        SLOT = {g: n for n, g in enumerate(sum(GROUPS.values(), ()))}
        fproj = sb("fproj", [P, K, B * C])
        vrep = sb("vrep", [P, K, 32])
        b0 = sb("b0", [P, NG])
        b1 = sb("b1", [P, NG])
        hp = sb("hp", [P, K, 2 * B], F16)

        def setup_sp(sp):
            sp.dma_start(vec[:, :], dram["vec"]).then_inc(in_small, 16)
            sp.dma_start(cst[:, :], dram["cst"]).then_inc(in_small, 16)
            sp.dma_start(ctxT[:, :, :], dram["ctxT"]).then_inc(in_ctx, 16)
            sp.dma_start(ctxTq[:, :, :], dram["ctxTq"]).then_inc(in_ctx, 16)
            sp.dma_start(xT[:, :, :], dram["xT"]).then_inc(in_x, 16)
            for dst, n in ((w_f, "w_f"), (w_at32, "w_at"), (w_x, "w_x"), (w_hh32, "w_hh"), (w_h32, "w_h")):
                sp.dma_start(dst, dram[n]).then_inc(in_rec, 16)

        SU = lines("setup", pe=("fproj0", "fproj1", "g0", "g1", "g2", "g3"),
                   act=("tgx", "tgf", "fproj0", "fproj1", "g0", "g1", "g2", "g3"),
                   dve=("b0", "b1", "vrep", "zero_h", "ident16", "b0_ifo", "b0_g", "b0_o", "b1_half", "b1_half2", "half_hh",
                        "half_h", *(f"{w}{i}" for w in ("whh", "wh", "gat") for i in range(3)), "zero_h_t", "tgf_w", "b2_0", "b2_2", "ws", "eps", "done"))

        def setup_pe(pe):
            pe.wait_ge(in_ctx, 32)
            pe.wait_ge(in_rec, 80)
            for a in range(K):
                for k in range(K):
                    i = nc.tensor.matmul(bank[a][:, 0:B * C], w_f[:, k, a * P:(a + 1) * P], ctxT[:, k, :],
                                         start=k == 0, stop=k == K - 1)
                i.then_inc(SU["pe"].sem, 1)
            for j in range(2):
                for u in range(2):
                    for k in range(K):
                        i = nc.tensor.matmul(bank[2 + 2 * j + u][:, :], ctxTq[:, k, j * P:(j + 1) * P],
                                             w_at32[:, k, u * 512:(u + 1) * 512], start=k == 0, stop=k == K - 1)
                    i.then_inc(SU["pe"].sem, 1)

        def setup_act(act):
            act.wait_ge(in_small, 32)
            nc.scalar.activation(tgx[:, :], v_("gx", 0, 4), ACT.Tanh).then_inc(SU["act"].sem, 1)
            nc.scalar.activation(tgf[:, :], v_("gf", 0, 4), ACT.Tanh).then_inc(SU["act"].sem, 1)
            for a in range(K):
                act.wait_ge(*SU["pe"].after(f"fproj{a}"))
                nc.scalar.activation(fproj[:, a, :], bank[a][:, 0:B * C], ACT.Identity,
                                     bias=v_("b_att", a)).then_inc(SU["act"].sem, 1)
            for j in range(2):
                for u in range(2):
                    act.wait_ge(*SU["pe"].after(f"g{2 * j + u}"))
                    src, dst = bank[2 + 2 * j + u], g32[:, j, u * 512:(u + 1) * 512]
                    if u == 0:
                        i = nc.scalar.activation(dst, src[:, :], ACT.Copy, scale=GS / 2)
                    else:
                        nc.scalar.activation(dst[:, 0:256], src[:, 0:256], ACT.Copy, scale=GS)
                        i = nc.scalar.activation(dst[:, 256:512], src[:, 256:512], ACT.Copy, scale=GS / 2)
                    i.then_inc(SU["act"].sem, 1)

        def setup_dve(dve):
            L = SU["dve"]
            dve.wait_ge(in_small, 32)
            nc.vector.tensor_tensor(b0[:, :], v_("b_ih0", 0, NG), v_("b_hh0", 0, NG), ALU.add).then_inc(L.sem, 1)
            nc.vector.tensor_tensor(b1[:, :], v_("b_ih1", 0, NG), v_("b_hh1", 0, NG), ALU.add).then_inc(L.sem, 1)
            nc.vector.tensor_copy(vrep[:, :, :], bcast(v_("v", 0, K), 32)).then_inc(L.sem, 1)
            nc.vector.memset(hp[:, :, :], 0.0).then_inc(L.sem, 1)
            nc.vector.tensor_copy(ident16[:, :], ident).then_inc(L.sem, 1)
            dve.wait_ge(*L.after("b1"))
            for g0, g1, f in ((0, 4, GS / 2), (4, 6, GS), (6, 8, GS / 2)):
                nc.vector.tensor_scalar(b0[:, g0:g1], b0[:, g0:g1], f, None, ALU.mult).then_inc(L.sem, 1)
            nc.vector.tensor_scalar(b1[:, 0:4], b1[:, 0:4], 0.5, None, ALU.mult).then_inc(L.sem, 1)
            nc.vector.tensor_scalar(b1[:, 6:8], b1[:, 6:8], 0.5, None, ALU.mult).then_inc(L.sem, 1)
            dve.wait_ge(in_rec, 80)
            for g0, g1, f in ((0, 512, GS / HS / 2), (512, 768, GS / HS), (768, 1024, GS / HS / 2)):
                i = nc.vector.tensor_scalar(w_hh32[:, :, g0:g1], w_hh32[:, :, g0:g1], f, None, ALU.mult)
            i.then_inc(L.sem, 1)
            nc.vector.tensor_scalar(w_h32, w_h32, GS / HS, None, ALU.mult).then_inc(L.sem, 1)
            for n, src, dst in (("whh", w_hh32, whh), ("wh", w_h32, wh), ("gat", g32, gat)):
                if n == "gat":
                    dve.wait_ge(*SU["act"].after("g3"))
                else:
                    dve.wait_ge(*L.after("half_h"))
                nc.vector.tensor_copy(dst[:, 0], src).then_inc(L.sem, 1)
                dve.wait_ge(*L.after(f"{n}0"))
                nc.vector.tensor_tensor(src, src, dst[:, 0], ALU.subtract).then_inc(L.sem, 1)
                dve.wait_ge(*L.after(f"{n}1"))
                nc.vector.tensor_copy(dst[:, 1], src).then_inc(L.sem, 1)
            nc.vector.memset(h_t[:, :, :], 0.0).then_inc(L.sem, 1)
            nc.vector.tensor_scalar(tgf_w[:, :], tgf[:, :], 1 / WS, None, ALU.mult).then_inc(L.sem, 1)
            for n in (0, 2):
                nc.vector.tensor_scalar(v_(f"f{n}_b2", 0, E * K), v_(f"f{n}_b2", 0, E * K), WS, None,
                                        ALU.mult).then_inc(L.sem, 1)
            nc.vector.memset(ws_col[:, :], WS).then_inc(L.sem, 1)
            nc.vector.memset(eps_col[:, :], EPS).then_inc(L.sem, 1)
            nc.vector.memset(s_t[:, :, :], 0.0).then_inc(L.sem, 1)

        XG = [(u, g) for u in range(2) for g in range(NG)]
        XP = lines("xproj", pe=(*LN_PE, *(f"g{u}{g}" for u, g in XG)),
                   act=(*LN_ACT, *(f"{w}{u}{g}" for u, g in XG for w in ("hi", "x"))),
                   dve=(*LN_DVE, *(f"lo{u}{g}" for u, g in XG)))
        xbufs = ln_buffers(wflat[:, 2 * 2048 + 512:])

        def xproj_pe(pe):
            pe.wait_ge(in_x, 16)
            pe.wait_ge(in_small, 32)
            finished(pe, {"act": SU["act"]})
            with pe.Fori(0, B // 2) as it:
                ln_pe(pe, XP, it, xbufs)
                for n, (u, g) in enumerate(XG):
                    if g == 0:
                        pe.wait_ge(*XP["dve"].after(f"normed{u}", it))
                    if n >= 4:
                        pe.wait_ge(*XP["act"].after("x%d%d" % XG[n - 4], it))
                    for k in range(K):
                        i = nc.tensor.matmul(bank[4 + g % 4][:, :], w_x[:, k, g * P:(g + 1) * P], xbufs[u][0][:, k, :],
                                             start=k == 0, stop=k == K - 1)
                    i.then_inc(XP["pe"].sem, 1)

        def xp_out(xp_part, u, g, it):
            return xp_part[:, SLOT[g], bass.ds(2 * it + u, 1), :].rearrange("p a s -> p (a s)")

        def xproj_act(act):
            act.wait_ge(*SU["dve"].after("done"))
            with act.Fori(0, B // 2) as it:
                ln_act(act, XP, it, xbufs)
                for n, (u, g) in enumerate(XG):
                    if n >= 2:
                        act.wait_ge(*XP["dve"].after("lo%d%d" % XG[n - 2], it))
                    act.wait_ge(*XP["pe"].after(f"g{u}{g}", it))
                    for dst in (xp_out(xp_hi, u, g, it), fo[:, g % 2, :]):
                        nc.scalar.activation(dst, bank[4 + g % 4][:, :], ACT.Identity, bias=b0[:, g:g + 1],
                                             scale=GS if g in (4, 5) else GS / 2).then_inc(XP["act"].sem, 1)

        def xproj_dve(dve):
            dve.wait_ge(in_x, 16)
            with dve.Fori(0, B // 2) as it:
                ln_dve(dve, XP, it, xbufs)
                for u, g in XG:
                    dve.wait_ge(*XP["act"].after(f"x{u}{g}", it))
                    nc.vector.tensor_tensor(xp_out(xp_lo, u, g, it), fo[:, g % 2, :], xp_out(xp_hi, u, g, it),
                                            ALU.subtract).then_inc(XP["dve"].sem, 1)

        arg = sb("arg", [P, K, B * C])
        e = sb("e", [P, K, B * C])
        negmax = sb("negmax", [P, 1])
        ex = sb("ex", [P, C])
        den = sb("den", [P, 1])
        rden = sb("rden", [P, 1])
        exT = sb("exT", [P, 2, 32])
        al32 = sb("al32", [P, 2, B])
        al = sb("al", [P, 2, 2 * B], F16)
        t_f, t_o = sb("t_f", [P, K, B]), sb("t_o", [P, K, B])
        t_ig = sb("t_ig", [P, 2 * K, B])
        o1 = sb("o1", [P, K, B])
        fc = sb("fc", [P, K, B])
        ig = sb("ig", [P, K, B])
        tc = sb("tc", [P, K, B])
        query = [bank[0], bank[1]]
        score = bank[2]
        xp_t = sb("xp_t", [P, 2, NG, B], F16)
        GATE_OUT = {g: bank[3 + u][:, j * B:(j + 1) * B] for u, gs in enumerate(GROUPS.values()) for j, g in enumerate(gs)}

        R = lines("rec", pool=("xp", "hist_h", "hist_s"), pe=("query0", "query1", "scores", "gates_f", "gates_ig", "gates_o"),
                  act=("tanh0", "tanh1", "exp", "tanh_f", "tanh_ig", "tanh_o", "tanh_c"),
                  dve=("h_hi", "h", "h_lo", "arg0", "arg1", "negmax", "exT", "rden", "al_hi", "al32", "al_lo", "fc", "ig",
                       "s", "o1"))

        R_END = line("rec_end_pool", "hist_h", "hist_s")

        def rec_finished(eng):
            eng.wait_ge(*R["pe"].before(S))
            eng.wait_ge(*R["act"].before(S))
            eng.wait_ge(*R["dve"].after("h_lo", S))
            eng.wait_ge(*R_END.after("hist_s"))

        def gate_mm(g, w, moving, k, pairs):
            for part, lo in pairs:
                i = nc.tensor.matmul(GATE_OUT[g], w[:, part, k, g * P:(g + 1) * P], moving[:, k, lo * B:(lo + 1) * B],
                                     start=False, stop=False, skip_group_check=True)
            return i

        def rec_pe(pe):
            finished(pe, {"dve": SU["dve"]})
            pe.wait_ge(*XP["act"].before(B // 2))
            pe.wait_ge(*XP["dve"].before(B // 2))
            with pe.Fori(0, S) as t:
                for lo in range(2):
                    pe.wait_ge(*R["dve"].after("h_lo" if lo else "h_hi", t))
                    for a in range(K):
                        pairs = [(k, part) for k in range(K) for part in range(2 - lo)]
                        for n, (k, part) in enumerate(pairs):
                            i = nc.tensor.matmul(query[a][:, 0:B], wh[:, part, k, a * P:(a + 1) * P],
                                                 hp[:, k, lo * B:(lo + 1) * B], start=n + lo == 0,
                                                 stop=lo == 1 and n == len(pairs) - 1, skip_group_check=True)
                        if lo:
                            i.then_inc(R["pe"].sem, 1)
                pe.wait_ge(*R["pool"].after("xp", t))
                for u, gs in enumerate(GROUPS.values()):
                    for part in range(2):
                        nc.tensor.matmul(bank[3 + u][:, 0:len(gs) * B], ident16[:, :],
                                         xp_t[:, part, SLOT[gs[0]]:SLOT[gs[-1]] + 1, :].rearrange("p g b -> p (g b)"),
                                         start=part == 0, stop=False, skip_group_check=True)

                def state_part(gs):
                    for g in gs:
                        for k in range(K):
                            gate_mm(g, whh, hp, k, ((0, 0), (1, 0), (0, 1)))

                state_part(GROUPS["f"])
                for a in range(K):
                    pe.wait_ge(*R["act"].after(f"tanh{a}", t))
                    for b in range(B):
                        i = nc.tensor.matmul(score[32 * b:32 * b + 32, 0:C], vrep[:, a, :], e[:, a, b * C:(b + 1) * C],
                                             start=a == 0, stop=a == K - 1)
                i.then_inc(R["pe"].sem, 1)
                state_part(GROUPS["ig"])
                state_part(GROUPS["o"])
                fig = ("f", "ig")
                pe.wait_ge(*R["dve"].after("al_hi", t))
                for name in fig:
                    for g in GROUPS[name]:
                        for j in range(2):
                            gate_mm(g, gat, al, j, ((0, 0), (1, 0)))
                pe.wait_ge(*R["dve"].after("al_lo", t))
                for name in fig:
                    for g in GROUPS[name]:
                        for j in range(2):
                            i = gate_mm(g, gat, al, j, ((0, 1),))
                    i.then_inc(R["pe"].sem, 1)
                for g in GROUPS["o"]:
                    for j in range(2):
                        i = gate_mm(g, gat, al, j, ((0, 0), (1, 0), (0, 1)))
                i.then_inc(R["pe"].sem, 1)

        def remember(pool, L, t):
            pool.wait_ge(*R["dve"].after("h", t))
            for hist, src in ((hist_h, h_t), (hist_s, s_t)):
                nc.gpsimd.tensor_copy(hist[:, :, :, bass.ds(t, 1)].rearrange("p k b a -> p k (b a)"),
                                      src[:, :, :]).then_inc(L.sem, 1)

        def rec_pool(pool):
            pool.wait_ge(*XP["act"].before(B // 2))
            pool.wait_ge(*XP["dve"].before(B // 2))
            with pool.Fori(0, S) as t:
                pool.wait_ge(*R["dve"].after("h_hi", t))
                nc.gpsimd.tensor_copy(xp_t[:, :, :, :].rearrange("p u g b -> p (u g b)"),
                                      xp[:, :, bass.ds(t, 1)].rearrange("p c a -> p (c a)")).then_inc(R["pool"].sem, 1)
                remember(pool, R["pool"], t)
            remember(pool, R_END, S)

        def rec_act(act):
            nc.scalar.preload_act_table(ACT.Exp)
            with act.Fori(0, S) as t:
                for a in range(K):
                    act.wait_ge(*R["dve"].after(f"arg{a}", t))
                    nc.scalar.activation(e[:, a, :], arg[:, a, :], ACT.Tanh).then_inc(R["act"].sem, 1)
                act.wait_ge(*R["dve"].after("negmax", t))
                nc.scalar.activation(ex[:, :], score[:, 0:C], ACT.Exp, bias=negmax[:, :],
                                     accum_out=den[:, :]).then_inc(R["act"].sem, 1)
                for u, (name, dst) in enumerate((("f", t_f), ("ig", t_ig), ("o", t_o))):
                    act.wait_ge(*R["pe"].after(f"gates_{name}", t))
                    n = len(GROUPS[name])
                    nc.scalar.activation(dst[:, :, :].rearrange("p g b -> p (g b)"), bank[3 + u][:, 0:n * B], ACT.Tanh,
                                         scale=1 / GS).then_inc(R["act"].sem, 1)
                act.wait_ge(*R["dve"].after("s", t))
                nc.scalar.activation(tc[:, :, :], s_t[:, :, :], ACT.Tanh, scale=0.5).then_inc(R["act"].sem, 1)

        def rec_dve(dve):
            L = R["dve"]
            dve.wait_ge(*XP["act"].before(B // 2))
            dve.sem_inc(L.sem, 3)

            def attend(t):
                for a in range(K):
                    dve.wait_ge(*R["pe"].after(f"query{a}", t))
                    nc.vector.scalar_tensor_tensor(arg[:, a, :].rearrange("p (b n) -> p b n", b=B),
                                                   bcast(query[a][:, 0:B], C), 1 / GS,
                                                   fproj[:, a, :].rearrange("p (b n) -> p b n", b=B),
                                                   ALU.mult, ALU.add).then_inc(L.sem, 1)
                dve.wait_ge(*R["pe"].after("scores", t))
                nc.vector.tensor_reduce(negmax[:, :], score[:, 0:C], AX.X, ALU.max, negate=True).then_inc(L.sem, 1)
                dve.wait_ge(*R["act"].after("exp", t))
                nc.vector.transpose(exT[:, :, :].rearrange("p j c -> p (j c)"), ex[:, :]).then_inc(L.sem, 1)
                nc.vector.reciprocal(rden[:, :], den[:, :]).then_inc(L.sem, 1)
                dve.wait_ge(*L.after("rden", t))
                for dst in (al[:, :, 0:B], al32[:, :, :]):
                    nc.vector.scalar_tensor_tensor(dst, exT[:, :, 0:B], rden[:, 0:1], over(const("diag_b"), 2),
                                                   ALU.mult, ALU.mult).then_inc(L.sem, 1)
                dve.wait_ge(*L.after("al32", t))
                nc.vector.tensor_tensor(al[:, :, B:2 * B], al32[:, :, :], al[:, :, 0:B],
                                        ALU.subtract).then_inc(L.sem, 1)

            def cell(t):
                dve.wait_ge(*R["act"].after("tanh_f", t))
                nc.vector.scalar_tensor_tensor(fc[:, :, :], t_f[:, :, :], 1.0, s_t[:, :, :], ALU.add,
                                               ALU.mult).then_inc(L.sem, 1)
                dve.wait_ge(*R["act"].after("tanh_ig", t))
                nc.vector.scalar_tensor_tensor(ig[:, :, :], t_ig[:, 0:2, :], 1.0, t_ig[:, 2:4, :], ALU.add,
                                               ALU.mult).then_inc(L.sem, 1)
                dve.wait_ge(*R["pool"].after("hist_s", t))
                dve.wait_ge(*L.after("ig", t))
                nc.vector.scalar_tensor_tensor(s_t[:, :, :], fc[:, :, :], 0.5, ig[:, :, :], ALU.mult,
                                               ALU.add).then_inc(L.sem, 1)
                dve.wait_ge(*R["act"].after("tanh_o", t))
                nc.vector.tensor_scalar(o1[:, :, :], t_o[:, :, :], 1.0, HS / 2, ALU.add, ALU.mult).then_inc(L.sem, 1)
                dve.wait_ge(*L.after("o1", t))
                dve.wait_ge(*R["act"].after("tanh_c", t))
                for dst in (hp[:, :, 0:B], h_t[:, :, :]):
                    nc.vector.tensor_tensor(dst, o1[:, :, :], tc[:, :, :], ALU.mult).then_inc(L.sem, 1)
                dve.wait_ge(*L.after("h", t + 1))
                nc.vector.tensor_tensor(hp[:, :, B:2 * B], h_t[:, :, :], hp[:, :, 0:B],
                                        ALU.subtract).then_inc(L.sem, 1)

            attend(0)
            with dve.Fori(0, S - 1) as t:
                cell(t)
                attend(t + 1)
            cell(S - 1)

        w1s = cols(fn, 0, (K, 4 * D))
        w1b = cols(fn, 2048, (K, 4 * D))
        t2 = cols(bigA, 0, (NG, S))
        fc2, ig2 = cols(bigA, 4096, (K, S)), cols(bigA, 5120, (K, S))
        tc2 = cols(bigA, 6144, (K, S))
        tgh = sb("tgh", [P, 1])
        L2 = lines("lstm2", pe=tuple(f"g{g}" for g in range(NG)), act=(*(f"t{g}" for g in range(NG)), "tanh_c"),
                   dve=("fc", "ig", "c", "h", "x0", "x1"))
        L2W = line("lstm2_w_dve", "sum", "half", "tgh")

        def lstm2_sp(sp):
            finished(sp, XP, B // 2)
            finished(sp, SU)
            sp.dma_start(w1s, dram["w_ih1"]).then_inc(in_l1, 16)
            sp.dma_start(w1b, dram["w_hh1"]).then_inc(in_l1, 16)

        def lstm2_pe(pe):
            pe.wait_ge(*L2W.after("half"))
            rec_finished(pe)
            with pe.Fori(0, B) as c:
                for g in range(NG):
                    if g >= 4:
                        pe.wait_ge(*L2["act"].after(f"t{g - 4}", c))
                    else:
                        pe.wait_ge(*L2["act"].before(c))
                    for k in range(K):
                        h = hist_h[:, k, bass.ds(c, 1), 1:S + 1].rearrange("p a s -> p (a s)")
                        i = nc.tensor.matmul(bank[g % 4][:, :], w1s[:, k, g * P:(g + 1) * P], h,
                                             start=k == 0, stop=k == K - 1)
                    i.then_inc(L2["pe"].sem, 1)

        def lstm2_act(act):
            rec_finished(act)
            with act.Fori(0, B) as c:
                act.wait_ge(*L2["dve"].before(c))
                for g in range(NG):
                    act.wait_ge(*L2["pe"].after(f"g{g}", c))
                    nc.scalar.activation(t2[:, g, :], bank[g % 4][:, :], ACT.Tanh, bias=b1[:, g:g + 1],
                                         scale=1.0 if g in (4, 5) else 0.5).then_inc(L2["act"].sem, 1)
                act.wait_ge(*L2["dve"].after("c", c))
                nc.scalar.activation(tc2, fc2, ACT.Tanh, scale=0.5).then_inc(L2["act"].sem, 1)

        def lstm2_dve(dve):
            dve.wait_ge(in_l1, 32)
            nc.vector.tensor_tensor(w1s, w1s, w1b, ALU.add).then_inc(L2W.sem, 1)
            dve.wait_ge(*L2W.after("sum"))
            nc.vector.tensor_scalar(w1s, w1s, 1 / HS, None, ALU.mult).then_inc(L2W.sem, 1)
            dve.wait_ge(*SU["act"].after("tgx"))
            nc.vector.tensor_scalar(tgh[:, :], tgx[:, 0:1], 0.5, None, ALU.mult).then_inc(L2W.sem, 1)
            rec_finished(dve)
            with dve.Fori(0, B) as c:
                s0 = hist_s[:, :, bass.ds(c, 1), 1:S + 1].rearrange("p k a s -> p k (a s)")
                dve.wait_ge(*L2["act"].after("t7", c))
                nc.vector.scalar_tensor_tensor(fc2, t2[:, 2:4, :], 1.0, s0, ALU.add, ALU.mult).then_inc(L2["dve"].sem, 1)
                nc.vector.scalar_tensor_tensor(ig2, t2[:, 0:2, :], 1.0, t2[:, 4:6, :], ALU.add,
                                               ALU.mult).then_inc(L2["dve"].sem, 1)
                dve.wait_ge(*L2["dve"].after("ig", c))
                nc.vector.scalar_tensor_tensor(fc2, fc2, 0.5, ig2, ALU.mult, ALU.add).then_inc(L2["dve"].sem, 1)
                dve.wait_ge(*L2["act"].after("tanh_c", c))
                nc.vector.scalar_tensor_tensor(ig2, t2[:, 6:8, :], 1.0, tc2, ALU.add, ALU.mult).then_inc(L2["dve"].sem, 1)
                dve.wait_ge(*L2["dve"].after("h", c))
                for k in range(K):
                    xs = xT[:, k, bass.ds(c * S, S)]
                    nc.vector.scalar_tensor_tensor(xs, ig2[:, k, :], tgh[:, 0:1], xs, ALU.mult,
                                                   ALU.add).then_inc(L2["dve"].sem, 1)

        wr = sb("wr", [P, K, E])
        T = N // P
        lg = sb("lg", [P, T, E])
        gates = sb("gates", [P, T, E])
        rank = sb("rank", [P, T, E])
        m0, m1 = sb("m0", [P, T, E]), sb("m1", [P, T, E])
        r0, r1 = sb("r0", [P, T]), sb("r1", [P, T])
        in_wr, in_w, in_gate, out_gate = sem("in_wr"), [sem("in_w0"), sem("in_w1")], [sem("in_gate0"), sem("in_gate1")], \
            sem("out_gate")
        gate_dram = [nc.dram_tensor(f"gates_of_layer{i}", (E, N), F32, kind="Internal").ap() for i in range(3)]
        n16 = [cols(fn, u * N, (K, N), F16) for u in range(2)]
        silu = cols(bigA, 2048, (FW1 // P, S))
        gate_bc = [bigA[:, 4096:6144], bigA[:, 6144:8192]]
        gT = bigA[0:E, 0:N]
        pair0, pair1 = cols(bigA, 2048, (T, E * E)), cols(bigA, 3072, (T, E * E))

        RANKED = ("gt", "equal", "tie", "pairs", "rank")
        SOFTMAX = ("max", "shift", "sum", "rsum", "probs")
        BEST2 = ("first", "second", "p1", "p2", "s1", "s2")
        ROUTE = [(*SOFTMAX, *RANKED, *BEST2, "s12", "rs12", "share", "gates"),
                 (*RANKED, *BEST2, "diff", "denom", "w1", "w2", "g1", "g2", "gates"),
                 (*SOFTMAX, *RANKED, "cum_in", "cum", "low", "first", "keep", "gates")]

        def expert_layer(n, prev, prev_iters):
            F = FW1 if n == 1 else FW
            FT = F // P
            LR = lines(f"ln{n}", pe=(*LN_PE, "logits0", "logits1"), act=(*LN_ACT, "n_hi0", "n_hi1"),
                       dve=(*LN_DVE, "n_lo0", "logits0", "n_lo1", "logits1"))
            RT = lines(f"route{n}", pe=("gT0", "gT1", "gT2", "gT3"), act=("exp", "gT0", "gT1", "gT2", "gT3"),
                       dve=ROUTE[n])
            X = f"experts{n}"
            XL = dict(up=line(f"{X}_up_pe", *(f"{u}{f}" for f in range(FT) for u in (("gate", "up") if n == 1 else ("up",)))),
                      out=line(f"{X}_out_pe", "out0", "out1"),
                      act=line(f"{X}_act", *(f"{u}{f}" for f in range(FT) for u in (("silu",) if n == 1 else ("hi", "h")))),
                      hid=line(f"{X}_hid_dve", *(f"{u}{f}" for f in range(FT)
                                                 for u in (("h", "hi", "lo") if n == 1 else ("lo",)))),
                      gated=line(f"{X}_gated_dve", "gated0", "gated1"), add=line(f"{X}_add_dve", "x0", "x1"))
            SPLIT = line(f"{X}_split_pool", "hi", "scaled", "lo")
            names = ("f1_w1", "f1_w3", "f1_w2") if n == 1 else (f"f{n}_w1", f"f{n}_w2")
            w_base = 16 * (E // 2) * sum(3 if i == 1 else 2 for i in range(n))
            g_base = 16 * (E // 2) * n

            hid16 = cols(bigA, 0, (2, FT, S), F16)
            WN = (3 if n == 1 else 2) * K * F
            w16 = [cols(t, 0, (2, WN), F16) for t in (fh, fs)]

            def weights(o):
                up = [o[:, m * K * F:(m + 1) * K * F].rearrange("p (k f) -> p k f", k=K) for m in range(WN // (K * F) - 1)]
                d = o[:, WN - FT * D:WN].rearrange("p (f d) -> p f d", f=FT)
                return [*up, d]

            def load_weights(sp, e, half):
                for dst, nm in zip(weights(wbuf[:, half, :]), names):
                    sp.dma_start(dst, dram[nm][bass.ds(e, 1)].rearrange("a p k f -> p (a k) f")).then_inc(in_w[half], 16)

            def load_gates(sp, e, half):
                sp.dma_start(gate_bc[half], gate_dram[n][bass.ds(e, 1), :].to_broadcast([P, N])).then_inc(in_gate[half], 16)

            rbufs = ln_buffers(bigA)

            def n16_of(part, it, u):
                return n16[part][:, :, bass.ds((2 * it + u) * S, S)]

            def route_sp(sp):
                finished(sp, prev, prev_iters)
                sp.dma_start(wr[:, :, :], dram[f"f{n}_wr"]).then_inc(in_wr, 16)
                for half in range(2):
                    load_weights(sp, half, half)
                sp.wait_ge(*RT["act"].after("gT3"))
                sp.dma_start(gate_dram[n], gT).then_inc(out_gate, 16)
                sp.wait_ge(out_gate, 16 * (n + 1))
                for half in range(2):
                    load_gates(sp, half, half)

            def experts_sp(sp):
                with sp.Fori(1, E // 2) as ep:
                    for half in range(2):
                        e = ep * 2 + half
                        sp.wait_ge(*SPLIT.before(e - 1))
                        load_weights(sp, e, half)
                        sp.wait_ge(*XL["gated"].before((e - 1) * B))
                        load_gates(sp, e, half)

            def experts_pool(pool):
                finished(pool, prev, prev_iters)

                def split(ep, half):
                    pool.wait_ge(in_w[half], (ep + 1) * 16 * len(names) + w_base)
                    w32, hi, lo = wbuf[:, half, 0:WN], w16[half][:, 0, :], w16[half][:, 1, :]
                    ws = ws_col[:, :].to_broadcast([P, WN])
                    nc.gpsimd.tensor_tensor(hi, w32, ws, ALU.mult).then_inc(SPLIT.sem, 1)
                    nc.gpsimd.tensor_tensor(w32, w32, ws, ALU.mult).then_inc(SPLIT.sem, 1)
                    pool.wait_ge(*SPLIT.after("scaled", ep * 2 + half))
                    nc.gpsimd.tensor_tensor(lo, w32, hi, ALU.subtract).then_inc(SPLIT.sem, 1)

                for half in range(2):
                    split(0, half)
                with pool.Fori(1, E // 2) as ep:
                    for half in range(2):
                        pool.wait_ge(*XL["out"].before((ep * 2 + half - 1) * B))
                        split(ep, half)

            def route_pe(pe):
                finished(pe, prev, prev_iters)
                pe.wait_ge(in_wr, 16 * (n + 1))
                with pe.Fori(0, B // 2) as it:
                    ln_pe(pe, LR, it, rbufs)
                    for u, (n32, _, _) in enumerate(rbufs):
                        pe.wait_ge(*LR["dve"].after(f"normed{u}", it))
                        for q in range(QT):
                            for k in range(K):
                                i = nc.tensor.matmul(bank[4 + u][:, q * E:(q + 1) * E], n32[:, k, q * P:(q + 1) * P], wr[:, k, :],
                                                     start=k == 0, stop=k == K - 1)
                        i.then_inc(LR["pe"].sem, 1)
                pe.wait_ge(*RT["dve"].after("gates"))
                for b in range(B):
                    for q in range(QT):
                        i = nc.tensor.transpose(bank[3 + b][0:E, q * P:(q + 1) * P], gates[:, b * QT + q, :], ident)
                    i.then_inc(RT["pe"].sem, 1)

            def route_act(act):
                finished(act, prev, prev_iters)
                with act.Fori(0, B // 2) as it:
                    ln_act(act, LR, it, rbufs)
                    for u, (n32, _, _) in enumerate(rbufs):
                        act.wait_ge(*LR["dve"].after(f"normed{u}", it))
                        nc.scalar.activation(n16_of(0, it, u), n32, ACT.Copy).then_inc(LR["act"].sem, 1)
                if n == 1:
                    act.wait_ge(*RT["dve"].after("diff"))
                    i = nc.scalar.activation(r1[:, :], r1[:, :], ACT.Exp)
                else:
                    act.wait_ge(*RT["dve"].after("shift"))
                    i = nc.scalar.activation(gates[:, :, :], lg[:, :, :], ACT.Exp)
                i.then_inc(RT["act"].sem, 1)
                for b in range(B):
                    act.wait_ge(*RT["pe"].after(f"gT{b}"))
                    nc.scalar.activation(gT[:, b * S:(b + 1) * S], bank[3 + b][0:E, :], ACT.Copy).then_inc(RT["act"].sem, 1)

            def route_dve(dve):
                finished(dve, prev, prev_iters)
                with dve.Fori(0, B // 2) as it:
                    ln_dve(dve, LR, it, rbufs)
                    for u, (n32, _, _) in enumerate(rbufs):
                        dve.wait_ge(*LR["act"].after(f"n_hi{u}", it))
                        nc.vector.tensor_tensor(n16_of(1, it, u), n32, n16_of(0, it, u), ALU.subtract).then_inc(LR["dve"].sem, 1)
                        dve.wait_ge(*LR["pe"].after(f"logits{u}", it))
                        dst = lg[:, bass.ds((2 * it + u) * QT, QT), :]
                        src = bank[4 + u][:, 0:QT * E].rearrange("p (q e) -> p q e", e=E)
                        if n == 1:
                            i = nc.vector.tensor_copy(dst, src)
                        else:
                            i = nc.vector.tensor_tensor(dst, src, over(v_(f"f{n}_br", 0, E), QT), ALU.add)
                        i.then_inc(LR["dve"].sem, 1)
                dve.wait_ge(*LR["dve"].before(B // 2))
                L = RT["dve"]
                rank_by = lg
                if n != 1:
                    nc.vector.tensor_reduce(r0[:, :], lg[:, :, :], AX.X, ALU.max).then_inc(L.sem, 1)
                    dve.wait_ge(*L.after("max"))
                    nc.vector.tensor_tensor(lg[:, :, :], lg[:, :, :], bcast(r0[:, :], E), ALU.subtract).then_inc(L.sem, 1)
                    dve.wait_ge(*RT["act"].after("exp"))
                    nc.vector.tensor_reduce(r0[:, :], gates[:, :, :], AX.X, ALU.add).then_inc(L.sem, 1)
                    dve.wait_ge(*L.after("sum"))
                    nc.vector.reciprocal(r0[:, :], r0[:, :]).then_inc(L.sem, 1)
                    dve.wait_ge(*L.after("rsum"))
                    nc.vector.tensor_tensor(gates[:, :, :], gates[:, :, :], bcast(r0[:, :], E), ALU.mult).then_inc(L.sem, 1)
                    dve.wait_ge(*L.after("probs"))
                    rank_by = gates
                e_of = rank_by[:, :, :].unsqueeze(3).to_broadcast([P, T, E, E])
                j_of = rank_by[:, :, :].unsqueeze(2).to_broadcast([P, T, E, E])
                p0 = pair0.rearrange("p t (e j) -> p t e j", e=E)
                p1 = pair1.rearrange("p t (e j) -> p t e j", e=E)
                nc.vector.tensor_tensor(p0, j_of, e_of, ALU.is_gt).then_inc(L.sem, 1)
                nc.vector.tensor_tensor(p1, j_of, e_of, ALU.is_equal).then_inc(L.sem, 1)
                dve.wait_ge(*L.after("equal"))
                nc.vector.tensor_tensor(pair1, pair1, over(const("upto" if n == 2 else "before"), T),
                                        ALU.mult).then_inc(L.sem, 1)
                dve.wait_ge(*L.after("tie"))
                nc.vector.tensor_tensor(pair0, pair0, pair1, ALU.add).then_inc(L.sem, 1)
                dve.wait_ge(*L.after("pairs"))
                nc.vector.tensor_reduce(rank[:, :, :], p0, AX.X, ALU.add).then_inc(L.sem, 1)
                dve.wait_ge(*L.after("rank"))
                if n == 2:
                    nc.vector.tensor_tensor(p0, p0, j_of, ALU.mult).then_inc(L.sem, 1)
                    dve.wait_ge(*L.after("cum_in"))
                    nc.vector.tensor_reduce(m0[:, :, :], p0, AX.X, ALU.add).then_inc(L.sem, 1)
                    dve.wait_ge(*L.after("cum"))
                    nc.vector.tensor_scalar(m0[:, :, :], m0[:, :, :], 0.8, None, ALU.is_lt).then_inc(L.sem, 1)
                    nc.vector.tensor_scalar(m1[:, :, :], rank[:, :, :], 1.5, None, ALU.is_lt).then_inc(L.sem, 1)
                    dve.wait_ge(*L.after("first"))
                    nc.vector.tensor_tensor(m0[:, :, :], m0[:, :, :], m1[:, :, :], ALU.max).then_inc(L.sem, 1)
                    dve.wait_ge(*L.after("keep"))
                    nc.vector.tensor_tensor(gates[:, :, :], gates[:, :, :], m0[:, :, :], ALU.mult).then_inc(L.sem, 1)
                    return
                nc.vector.tensor_scalar(m0[:, :, :], rank[:, :, :], 0.0, None, ALU.is_equal).then_inc(L.sem, 1)
                nc.vector.tensor_scalar(m1[:, :, :], rank[:, :, :], 1.0, None, ALU.is_equal).then_inc(L.sem, 1)
                dve.wait_ge(*L.after("second"))
                nc.vector.tensor_tensor(pair0[:, :, 0:E], rank_by[:, :, :], m0[:, :, :], ALU.mult).then_inc(L.sem, 1)
                nc.vector.tensor_tensor(pair1[:, :, 0:E], rank_by[:, :, :], m1[:, :, :], ALU.mult).then_inc(L.sem, 1)
                dve.wait_ge(*L.after("p2"))
                nc.vector.tensor_reduce(r0[:, :], pair0[:, :, 0:E], AX.X, ALU.add).then_inc(L.sem, 1)
                nc.vector.tensor_reduce(r1[:, :], pair1[:, :, 0:E], AX.X, ALU.add).then_inc(L.sem, 1)
                dve.wait_ge(*L.after("s2"))
                if n == 0:
                    nc.vector.tensor_tensor(r1[:, :], r0[:, :], r1[:, :], ALU.add).then_inc(L.sem, 1)
                    dve.wait_ge(*L.after("s12"))
                    nc.vector.reciprocal(r1[:, :], r1[:, :]).then_inc(L.sem, 1)
                    dve.wait_ge(*L.after("rs12"))
                    nc.vector.tensor_tensor(r0[:, :], r0[:, :], r1[:, :], ALU.mult).then_inc(L.sem, 1)
                    dve.wait_ge(*L.after("share"))
                    nc.vector.tensor_tensor(gates[:, :, :], m0[:, :, :], bcast(r0[:, :], E), ALU.mult).then_inc(L.sem, 1)
                    return
                nc.vector.tensor_tensor(r1[:, :], r1[:, :], r0[:, :], ALU.subtract).then_inc(L.sem, 1)
                dve.wait_ge(*RT["act"].after("exp"))
                nc.vector.tensor_scalar(r0[:, :], r1[:, :], 1.0, None, ALU.add).then_inc(L.sem, 1)
                dve.wait_ge(*L.after("denom"))
                nc.vector.reciprocal(r0[:, :], r0[:, :]).then_inc(L.sem, 1)
                dve.wait_ge(*L.after("w1"))
                nc.vector.tensor_tensor(r1[:, :], r1[:, :], r0[:, :], ALU.mult).then_inc(L.sem, 1)
                dve.wait_ge(*L.after("w2"))
                nc.vector.tensor_tensor(m0[:, :, :], m0[:, :, :], bcast(r0[:, :], E), ALU.mult).then_inc(L.sem, 1)
                nc.vector.tensor_tensor(m1[:, :, :], m1[:, :, :], bcast(r1[:, :], E), ALU.mult).then_inc(L.sem, 1)
                dve.wait_ge(*L.after("g2"))
                nc.vector.tensor_tensor(gates[:, :, :], m0[:, :, :], m1[:, :, :], ALU.add).then_inc(L.sem, 1)

            PARTS = ((0, 0), (1, 0), (0, 1))
            UP_BANKS = 2 if n == 1 else 4

            def experts_pe(pe):
                pe.wait_ge(*RT["act"].after("gT3"))
                pe.wait_ge(*LR["dve"].before(B // 2))
                w = [[weights(w16[half][:, part, :]) for part in range(2)] for half in range(2)]

                def up(f, half, c):
                    for m in range(len(w[half][0]) - 1):
                        pairs = [(k, *p) for k in range(K) for p in PARTS]
                        for j, (k, wp, np_) in enumerate(pairs):
                            i = nc.tensor.matmul(bank[m * UP_BANKS + f % UP_BANKS][:, :], w[half][wp][m][:, k, f * P:(f + 1) * P],
                                                 n16[np_][:, k, bass.ds(c * S, S)], start=j == 0, stop=j == len(pairs) - 1)
                        i.then_inc(XL["up"].sem, 1)

                def down(f, half, it):
                    if f == 0:
                        pe.wait_ge(*XL["gated"].before(it))
                    pe.wait_ge(*XL["hid"].after(f"lo{f}", it))
                    for h in range(K):
                        for wp, hp_ in PARTS:
                            i = nc.tensor.matmul(bank[6 + h][:, :], w[half][wp][-1][:, f, h * P:(h + 1) * P], hid16[:, hp_, f, :],
                                                 start=f == 0 and wp + hp_ == 0, stop=f == FT - 1 and hp_ == 1)
                        if f == FT - 1:
                            i.then_inc(XL["out"].sem, 1)

                def chunk(it, half, c, next_half, next_c):
                    for f in range(2, FT + 2):
                        if n == 1:
                            pe.wait_ge(*XL["hid"].after(f"hi{f - 2}", it))
                        if f < FT:
                            up(f, half, c)
                        elif next_half is not None:
                            up(f - FT, next_half, next_c)
                        down(f - 2, half, it)

                def pair(ep, last):
                    for half in range(2):
                        e = ep * 2 + half
                        with pe.Fori(0, B - 1) as c:
                            chunk(e * B + c, half, c, half, c + 1)
                        if last and half == 1:
                            chunk(e * B + B - 1, half, B - 1, None, None)
                        else:
                            pe.wait_ge(*SPLIT.after("lo", e + 1))
                            chunk(e * B + B - 1, half, B - 1, 1 - half, 0)

                pe.wait_ge(*SPLIT.after("lo", 0))
                for f in range(2):
                    up(f, 0, 0)
                with pe.Fori(0, E // 2 - 1) as ep:
                    pair(ep, False)
                pair(E // 2 - 1, True)

            def experts_act(act):
                act.wait_ge(out_gate, 16 * (n + 1))
                act.wait_ge(*RT["dve"].before(1))
                nc.scalar.preload_act_table((ACT.Gelu, ACT.Silu, ACT.Relu)[n])
                with act.Fori(0, E) as ex_:
                    with act.Fori(0, B) as c:
                        it = ex_ * B + c
                        for f in range(FT):
                            ps = bank[f % UP_BANKS][:, :]
                            if n == 1:
                                act.wait_ge(*XL["up"].after(f"gate{f}", it))
                                nc.scalar.activation(silu[:, f, :], ps, ACT.Silu, scale=1 / WS).then_inc(XL["act"].sem, 1)
                                continue
                            act.wait_ge(*(XL["hid"].after(f"lo{f - 2}", it) if f >= 2 else XL["hid"].before(it)))
                            act.wait_ge(*XL["up"].after(f"up{f}", it))
                            func, col = ACT.Gelu if n == 0 else ACT.Relu, VCOL[f"f{n}_b1"] + f
                            b = vec[:, bass.ds(ex_ * FT + col, 1)]
                            for dst in (hid16[:, 0, f, :], sq[:, f % 2, :]):
                                nc.scalar.activation(dst, ps, func, bias=b, scale=1 / WS).then_inc(XL["act"].sem, 1)

            def experts_dve(dve):
                dve.wait_ge(out_gate, 16 * (n + 1))

                def low(f, it):
                    hi, lo, h = hid16[:, 0, f, :], hid16[:, 1, f, :], sq[:, f % 2, :]
                    if n == 1:
                        dve.wait_ge(*XL["act"].after(f"silu{f}", it))
                        dve.wait_ge(*XL["up"].after(f"up{f}", it))
                        for dst in (h, hi):
                            nc.vector.scalar_tensor_tensor(dst, bank[UP_BANKS + f % UP_BANKS][:, :], 1 / WS, silu[:, f, :],
                                                           ALU.mult, ALU.mult).then_inc(XL["hid"].sem, 1)
                        dve.wait_ge(*XL["hid"].after(f"hi{f}", it))
                    else:
                        dve.wait_ge(*XL["act"].after(f"h{f}", it))
                    nc.vector.tensor_tensor(lo, h, hi, ALU.subtract).then_inc(XL["hid"].sem, 1)

                def gated(ep, half, c):
                    dve.wait_ge(in_gate[half], (ep + 1) * 16 + g_base)
                    ex_ = ep * 2 + half
                    it = ex_ * B + c
                    g = gate_bc[half][:, bass.ds(c * S, S)]
                    for h in range(K):
                        dve.wait_ge(*XL["out"].after(f"out{h}", it))
                        if n == 1:
                            i = nc.vector.tensor_tensor(fo[:, h, :], bank[6 + h][:, :], g, ALU.mult)
                        else:
                            col = VCOL[f"f{n}_b2"] + h
                            i = nc.vector.scalar_tensor_tensor(fo[:, h, :], bank[6 + h][:, :],
                                                               vec[:, bass.ds(ex_ * K + col, 1)], g, ALU.add, ALU.mult)
                        i.then_inc(XL["gated"].sem, 1)

                def add(c, it):
                    for h in range(K):
                        dve.wait_ge(*XL["gated"].after(f"gated{h}", it))
                        xs = xT[:, h, bass.ds(c * S, S)]
                        nc.vector.scalar_tensor_tensor(xs, fo[:, h, :], tgf_w[:, n:n + 1], xs, ALU.mult,
                                                       ALU.add).then_inc(XL["add"].sem, 1)

                def chunk(ep, half, c, last):
                    it = (ep * 2 + half) * B + c
                    for f in range(2, FT):
                        low(f, it)
                    if not last:
                        low(0, it + 1)
                    gated(ep, half, c)
                    if not last:
                        low(1, it + 1)
                    add(c, it)

                for f in range(2):
                    low(f, 0)
                with dve.Fori(0, E // 2 - 1) as ep:
                    for half in range(2):
                        with dve.Fori(0, B) as c:
                            chunk(ep, half, c, False)
                with dve.Fori(0, B) as c:
                    chunk(E // 2 - 1, 0, c, False)
                with dve.Fori(0, B - 1) as c:
                    chunk(E // 2 - 1, 1, c, False)
                chunk(E // 2 - 1, 1, B - 1, True)

            return XL, route_sp, experts_sp, route_pe, experts_pe, route_act, experts_act, route_dve, experts_dve, experts_pool

        F0, f0_route_sp, f0_sp, f0_route_pe, f0_pe, f0_route_act, f0_act, f0_route_dve, f0_dve, f0_pool = expert_layer(0, L2, B)

        in_x1 = sem("in_x1")
        w_x1 = cols(bigB, 0, (6, K, D))
        WQC, WKS, WVS, WQS, WKC, WVC = range(6)
        w_g = cols(bigB, 3072, (2 * K, D))
        ctxb = sb("ctxb", [P, K, 2 * C])
        qcT, kcT = cols(bigA, 0, (K, S)), cols(bigA, 1024, (K, S))
        c2s, s2c = cols(bigA, 2048, (K, S)), cols(bigA, 3072, (K, S))
        vc = cols(bigA, 4096, (QT, D))
        gate1, mix = cols(bigA, 5120, (K, S)), cols(bigA, 6144, (K, S))
        ksT, qsT = cols(fh, 0, (K, C)), cols(fh, 128, (K, C))
        vs = fh[0:C, 256:512]
        s1 = cols(fh, 512, (QT, C))
        s2 = fh[0:C, 1024:1536]
        s1T = fh[0:C, 1536:2048]
        s2T = cols(fh, 2048, (QT, C))
        s2o = fh[0:C, 2304:2560]
        mx1, sum1 = sb("mx1", [P, QT]), sb("sum1", [P, QT])
        mx2, sum2 = sb("mx2", [P, 1]), sb("sum2", [P, 1])
        bgh = sb("bgh", [P, K])
        tg1h = sb("tg1h", [P, 1])
        SC1 = 1.0 / 16.0
        X1 = lines("x1", pe=("ks", "qs", "vs", "qc0", "qc1", "kc0", "kc1", "vc", "s1", "s2", "s1T", "s2T",
                             "c2s0", "c2s1", "s2o", "s2c0", "s2c1", "gate0", "gate1"),
                   act=("nb", "ks", "qs", "vs", "qc0", "qc1", "kc0", "kc1", "vc", "e1", "e2", "c2s0", "c2s1",
                        "s2c0", "s2c1", "gate0", "gate1"),
                   dve=("ctxb", "mx1", "mx2", "nmx2", "shift1", "sum1", "rsum1", "p1", "rsum2", "p2", "s1T", "s2T",
                        "s2o", "diff", "prod", "mix", "x0", "x1"))
        LN1 = ln_lines("x1_ln")
        abufs = ln_buffers(bigA)
        X1C = line("x1_consts_dve", "bgh", "tg1h")

        def ln_all(eng, L, part, *dst):
            with eng.Fori(0, B // 2) as it:
                part(eng, L, it, abufs, *dst)
            finished(eng, L, B // 2)

        def x1_load(sp):
            sp.wait_ge(*R["dve"].after("h_lo", S))
            sp.dma_start(w_x1.rearrange("p w k d -> p (w k d)"), dram["x1_w"]).then_inc(in_x1, 16)
            sp.dma_start(w_g, dram["x1_wg"]).then_inc(in_x1, 16)

        def x1_pe(pe):
            finished(pe, F0, E * B)
            ln_all(pe, LN1, ln_pe)
            pe.wait_ge(in_x1, 32)
            L = X1["pe"]

            def proj(dst, w, o, rhs):
                for k in range(K):
                    i = nc.tensor.matmul(dst, w_x1[:, w, k, o * P:(o + 1) * P], rhs[k], start=k == 0, stop=k == K - 1)
                return i

            with pe.Fori(0, B) as c:
                pe.wait_ge(*X1["dve"].before(c))
                pe.wait_ge(*X1["dve"].after("ctxb", c))
                cx = [ctxb[:, k, 0:C] for k in range(K)]
                for o in range(K):
                    i = proj(bank[2][:, o * C:(o + 1) * C], WKS, o, cx)
                i.then_inc(L.sem, 1)
                for o in range(K):
                    i = proj(bank[3][:, o * C:(o + 1) * C], WQS, o, cx)
                i.then_inc(L.sem, 1)
                for k in range(K):
                    i = nc.tensor.matmul(bank[4][0:C, 0:D], cx[k], w_x1[:, WVS, k, :], start=k == 0, stop=k == K - 1)
                i.then_inc(L.sem, 1)
                nbk = [nT[:, k, bass.ds(c * S, S)] for k in range(K)]
                proj(bank[5][:, :], WQC, 0, nbk).then_inc(L.sem, 1)
                proj(bank[6][:, :], WQC, 1, nbk).then_inc(L.sem, 1)
                proj(bank[7][:, :], WKC, 0, nbk).then_inc(L.sem, 1)
                proj(bank[0][:, :], WKC, 1, nbk).then_inc(L.sem, 1)
                pe.wait_ge(*X1["act"].after("qs", c))
                for q in range(QT):
                    for k in range(K):
                        i = nc.tensor.matmul(bank[2 + q // 2][:, q % 2 * D:q % 2 * D + D], nb[:, k, q * P:(q + 1) * P],
                                             w_x1[:, WVC, k, :], start=k == 0, stop=k == K - 1)
                i.then_inc(L.sem, 1)
                pe.wait_ge(*X1["act"].after("kc1", c))
                for q in range(QT):
                    for o in range(K):
                        i = nc.tensor.matmul(bank[1][:, q * C:(q + 1) * C], qcT[:, o, q * P:(q + 1) * P], ksT[:, o, :],
                                             start=o == 0, stop=o == K - 1)
                i.then_inc(L.sem, 1)
                for o in range(K):
                    i = nc.tensor.matmul(bank[4][0:C, :], qsT[:, o, :], kcT[:, o, :], start=o == 0, stop=o == K - 1)
                i.then_inc(L.sem, 1)
                pe.wait_ge(*X1["dve"].after("p1", c))
                for q in range(QT):
                    i = nc.tensor.matmul(bank[5][0:C, q * P:(q + 1) * P], s1[:, q, :], ident, start=True, stop=True)
                i.then_inc(L.sem, 1)
                pe.wait_ge(*X1["dve"].after("p2", c))
                for q in range(QT):
                    i = nc.tensor.matmul(bank[6][:, q * C:(q + 1) * C], s2[:, q * P:(q + 1) * P], ident[0:C, 0:C],
                                         start=True, stop=True)
                i.then_inc(L.sem, 1)
                pe.wait_ge(*X1["dve"].after("s1T", c))
                for o in range(K):
                    nc.tensor.matmul(bank[7 * (1 - o)][:, :], vs[:, o * P:(o + 1) * P], s1T, start=True,
                                     stop=True).then_inc(L.sem, 1)
                pe.wait_ge(*X1["dve"].after("s2T", c))
                pe.wait_ge(*X1["act"].after("vc", c))
                for q in range(QT):
                    i = nc.tensor.matmul(bank[2][0:C, 0:D], s2T[:, q, :], vc[:, q, :], start=q == 0, stop=q == QT - 1)
                i.then_inc(L.sem, 1)
                pe.wait_ge(*X1["dve"].after("s2o", c))
                for o in range(K):
                    nc.tensor.matmul(bank[3 + o][:, :], s2o[:, o * P:(o + 1) * P], const("interp")[0:C, :], start=True,
                                     stop=True).then_inc(L.sem, 1)
                pe.wait_ge(*X1["act"].after("s2c1", c))
                for o in range(K):
                    for m in range(2 * K):
                        r = c2s[:, m, :] if m < K else s2c[:, m - K, :]
                        i = nc.tensor.matmul(bank[5 + o][:, :], w_g[:, m, o * P:(o + 1) * P], r, start=m == 0,
                                             stop=m == 2 * K - 1)
                    i.then_inc(L.sem, 1)

        def x1_act(act):
            L = X1["act"]
            finished(act, F0, E * B)
            act.wait_ge(*X1C.before(1))
            ln_all(act, LN1, ln_act)
            with act.Fori(0, B) as c:
                nc.scalar.activation(nb[:, :, :], normed(c), ACT.Copy).then_inc(L.sem, 1)

                def evac(dst, ps, step, bias, scale=1.0, func=ACT.Identity):
                    act.wait_ge(*X1["pe"].after(step, c))
                    nc.scalar.activation(dst, ps, func, bias=bias, scale=scale).then_inc(L.sem, 1)

                def evac2(dst, b, step, bias):
                    act.wait_ge(*X1["pe"].after(step, c))
                    for o in range(K):
                        i = nc.scalar.activation(dst[:, o, :], bank[b][:, o * C:(o + 1) * C], ACT.Identity, bias=v_(bias, o))
                    i.then_inc(L.sem, 1)

                evac2(ksT, 2, "ks", "bk_s")
                evac2(qsT, 3, "qs", "bq_s")
                act.wait_ge(*X1["pe"].after("vs", c))
                nc.scalar.activation(vs, bank[4][0:C, 0:D], ACT.Copy).then_inc(L.sem, 1)
                evac(qcT[:, 0, :], bank[5][:, :], "qc0", v_("bq_c", 0))
                evac(qcT[:, 1, :], bank[6][:, :], "qc1", v_("bq_c", 1))
                evac(kcT[:, 0, :], bank[7][:, :], "kc0", v_("bk_c", 0))
                evac(kcT[:, 1, :], bank[0][:, :], "kc1", v_("bk_c", 1))
                act.wait_ge(*X1["pe"].after("vc", c))
                for u in range(2):
                    i = nc.scalar.activation(vc[:, 2 * u:2 * u + 2, :].rearrange("p q d -> p (q d)"), bank[2 + u][:, :],
                                             ACT.Copy)
                i.then_inc(L.sem, 1)
                act.wait_ge(*X1["dve"].after("shift1", c))
                nc.scalar.activation(s1, s1, ACT.Exp, scale=SC1).then_inc(L.sem, 1)
                act.wait_ge(*X1["dve"].after("nmx2", c))
                nc.scalar.activation(s2, bank[4][0:C, :], ACT.Exp, scale=SC1, bias=mx2[0:C, :],
                                     accum_out=sum2[0:C, :]).then_inc(L.sem, 1)
                evac(c2s[:, 0, :], bank[7][:, :], "c2s0", v_("bv_s", 0))
                evac(c2s[:, 1, :], bank[0][:, :], "c2s1", v_("bv_s", 1))
                evac(s2c[:, 0, :], bank[3][:, :], "s2c0", v_("bv_c", 0))
                evac(s2c[:, 1, :], bank[4][:, :], "s2c1", v_("bv_c", 1))
                evac(gate1[:, 0, :], bank[5][:, :], "gate0", bgh[:, 0:1], 0.5, ACT.Tanh)
                evac(gate1[:, 1, :], bank[6][:, :], "gate1", bgh[:, 1:2], 0.5, ACT.Tanh)

        def x1_dve(dve):
            L = X1["dve"]
            finished(dve, F0, E * B)
            nc.vector.tensor_scalar(bgh[:, :], v_("bg", 0, K), 0.5, None, ALU.mult).then_inc(X1C.sem, 1)
            nc.vector.tensor_scalar(tg1h[:, :], tgx[:, 1:2], 0.5, None, ALU.mult).then_inc(X1C.sem, 1)
            ln_all(dve, LN1, ln_dve, normed)
            with dve.Fori(0, B) as c:
                dve.wait_ge(*X1["pe"].before(c))
                nc.vector.tensor_copy(ctxb[:, :, 0:C], ctxT[:, :, bass.ds(c * C, C)]).then_inc(L.sem, 1)
                dve.wait_ge(*X1["pe"].after("s1", c))
                sc = bank[1][:, 0:QT * C].rearrange("p (q n) -> p q n", q=QT)
                nc.vector.tensor_reduce(mx1[:, :], sc, AX.X, ALU.max).then_inc(L.sem, 1)
                dve.wait_ge(*X1["pe"].after("s2", c))
                nc.vector.tensor_reduce(mx2[0:C, :], bank[4][0:C, :], AX.X, ALU.max).then_inc(L.sem, 1)
                dve.wait_ge(*L.after("mx2", c))
                nc.vector.tensor_scalar(mx2[0:C, :], mx2[0:C, :], -SC1, None, ALU.mult).then_inc(L.sem, 1)
                nc.vector.tensor_tensor(s1, sc, bcast(mx1[:, :], C), ALU.subtract).then_inc(L.sem, 1)
                dve.wait_ge(*X1["act"].after("e1", c))
                nc.vector.tensor_reduce(sum1[:, :], s1, AX.X, ALU.add).then_inc(L.sem, 1)
                dve.wait_ge(*L.after("sum1", c))
                nc.vector.reciprocal(sum1[:, :], sum1[:, :]).then_inc(L.sem, 1)
                dve.wait_ge(*L.after("rsum1", c))
                nc.vector.tensor_tensor(s1, s1, bcast(sum1[:, :], C), ALU.mult).then_inc(L.sem, 1)
                dve.wait_ge(*X1["act"].after("e2", c))
                nc.vector.reciprocal(sum2[0:C, :], sum2[0:C, :]).then_inc(L.sem, 1)
                dve.wait_ge(*L.after("rsum2", c))
                nc.vector.tensor_scalar(s2, s2, sum2[0:C, 0:1], None, ALU.mult).then_inc(L.sem, 1)
                dve.wait_ge(*X1["pe"].after("s1T", c))
                nc.vector.tensor_copy(s1T, bank[5][0:C, :]).then_inc(L.sem, 1)
                dve.wait_ge(*X1["pe"].after("s2T", c))
                nc.vector.tensor_copy(s2T, bank[6][:, 0:QT * C].rearrange("p (q n) -> p q n", q=QT)).then_inc(L.sem, 1)
                dve.wait_ge(*X1["pe"].after("s2o", c))
                nc.vector.tensor_copy(s2o, bank[2][0:C, 0:D]).then_inc(L.sem, 1)
                dve.wait_ge(*X1["act"].after("s2c1", c))
                nc.vector.tensor_tensor(mix, c2s, s2c, ALU.subtract).then_inc(L.sem, 1)
                dve.wait_ge(*X1["act"].after("gate1", c))
                dve.wait_ge(*L.after("diff", c))
                nc.vector.scalar_tensor_tensor(mix, gate1, 1.0, mix, ALU.add, ALU.mult).then_inc(L.sem, 1)
                dve.wait_ge(*L.after("prod", c))
                nc.vector.scalar_tensor_tensor(mix, s2c, 2.0, mix, ALU.mult, ALU.add).then_inc(L.sem, 1)
                dve.wait_ge(*L.after("mix", c))
                for k in range(K):
                    xs = xT[:, k, bass.ds(c * S, S)]
                    nc.vector.scalar_tensor_tensor(xs, mix[:, k, :], tg1h[:, 0:1], xs, ALU.mult, ALU.add).then_inc(L.sem, 1)

        F1, f1_route_sp, f1_sp, f1_route_pe, f1_pe, f1_route_act, f1_act, f1_route_dve, f1_dve, f1_pool = \
            expert_layer(1, X1, B)

        in_x2 = sem("in_x2")
        w_s, w_w = cols(bigB, 0, (K, D)), cols(bigB, 512, (K, D))
        mask_i = cols(bigB, 1024, (1, B * C))[:, 0, :].bitcast(I32)
        mask = bigB[:, 1280:1536]
        wcr = cols(bigB, 1536, (2, K * P))
        u2 = cols(bigB, 2048, (2, B * C))
        txtT = cols(bigB, 2560, (K, B * C))
        ones_at = bigB[:, 3072:3072 + 2 * C]
        NH2, NR2 = 4, 3
        h2 = [cols(bigA, i * 1024, (K, S)) for i in range(NH2)]
        r2 = cols(bigA, 4096, (NR2, S))
        rhoT = bigA[0:C, 5632:6144]
        rho = cols(bigA, 6144, (QT, C))
        eu = cols(bigA, 6400, (QT, C))
        diag = cols(bigA, 6656, (2, S))
        y2 = cols(bigA, 0, (K, S))
        WEIGHED = ["m0"] + [w for t in range(C) for w in ([f"m{t + 1}"] if t + 1 < C else []) + [f"r{t}"]]
        ws = sb("ws", [P, 2, QT])
        X2S = lines("x2_setup", pe=("txt0", "txt1", "u0", "u1"), act=("txt0", "txt1", "u0", "u1"),
                    dve=("mask_f", "mask", "wcr0", "wcr1", "zeros", "one"))
        LN2 = ln_lines("x2_ln")
        X2 = lines("x2", pe=("feat0", "feat1", *(f"rho{t}" for t in range(C)), "rhoT", "bc0", "bc1"),
                   act=(*(f"h{t}" for t in range(C)), "rhoT", "exp", "ws", "bs"),
                   dve=(*WEIGHED, "masked", "mx", "shift", "sum", "rsum",
                        "ew", "sw", "eb", "sb", "nw", "nb_", "diag", "scaled", "moved", "x0", "x1"))

        def x2_load(sp):
            finished(sp, X1, B)
            sp.dma_start(w_s, dram["x2_ws"]).then_inc(in_x2, 16)
            sp.dma_start(w_w, dram["x2_w"]).then_inc(in_x2, 16)
            sp.dma_start(mask_i, dram["mask"]).then_inc(in_x2, 16)

        def x2_pe(pe):
            finished(pe, F1, E * B)
            pe.wait_ge(in_x2, 48)
            pe.wait_ge(*X2S["dve"].before(1))
            for a in range(K):
                for k in range(K):
                    i = nc.tensor.matmul(bank[a][:, 0:B * C], w_s[:, k, a * P:(a + 1) * P], ctxT[:, k, :],
                                         start=k == 0, stop=k == K - 1)
                i.then_inc(X2S["pe"].sem, 1)
            for m in range(2):
                for k in range(K):
                    i = nc.tensor.matmul(bank[2 + m][:, 0:B * C], wcr[:, m, k * P:(k + 1) * P], ctxT[:, k, :],
                                         start=k == 0, stop=k == K - 1)
                i.then_inc(X2S["pe"].sem, 1)
            pe.wait_ge(*X2S["act"].before(1))
            ln_all(pe, LN2, ln_pe)
            L = X2["pe"]
            with pe.Fori(0, B) as c:
                pe.wait_ge(*X2["dve"].before(c))
                for a in range(K):
                    for k in range(K):
                        i = nc.tensor.matmul(bank[2 + a][:, :], w_w[:, k, a * P:(a + 1) * P], nT[:, k, bass.ds(c * S, S)],
                                             start=k == 0, stop=k == K - 1)
                    i.then_inc(L.sem, 1)
                for t in range(C):
                    pe.wait_ge(*X2["dve"].after(f"r{t}", c))
                    i = nc.tensor.matmul(bank[4][0:C, :], ones_at[:, C - 1 - t:2 * C - 1 - t], r2[:, t % NR2, :],
                                         start=t == 0, stop=t == C - 1)
                    i.then_inc(L.sem, 1)
                pe.wait_ge(*X2["act"].after("rhoT", c))
                for q in range(QT):
                    i = nc.tensor.matmul(bank[5][:, q * C:(q + 1) * C], rhoT[:, q * P:(q + 1) * P], ident[0:C, 0:C],
                                         start=True, stop=True)
                i.then_inc(L.sem, 1)
                pe.wait_ge(*X2["dve"].after("diag", c))
                for m in range(2):
                    i = nc.tensor.matmul(bank[6 + m][:, :], ones, diag[:, m, :], start=True, stop=True)
                    i.then_inc(L.sem, 1)

        def x2_act(act):
            finished(act, F1, E * B)
            L = X2S["act"]
            for a in range(K):
                act.wait_ge(*X2S["pe"].after(f"txt{a}"))
                nc.scalar.activation(txtT[:, a, :], bank[a][:, 0:B * C], ACT.Identity, bias=v_("ab", a)).then_inc(L.sem, 1)
            for m in range(2):
                act.wait_ge(*X2S["pe"].after(f"u{m}"))
                nc.scalar.activation(u2[:, m, :], bank[2 + m][:, 0:B * C], ACT.Copy).then_inc(L.sem, 1)
            act.wait_ge(*L.before(1))
            ln_all(act, LN2, ln_act)
            L = X2["act"]
            with act.Fori(0, B) as c:
                act.wait_ge(*X2["pe"].after("feat1", c))
                for t in range(C):
                    if t >= NH2:
                        act.wait_ge(*X2["dve"].after(f"r{t - NH2}", c))
                    for a in range(K):
                        i = nc.scalar.activation(h2[t % NH2][:, a, :], bank[2 + a][:, :], ACT.Tanh,
                                                 bias=txtT[:, a, bass.ds(c * C + t, 1)])
                    i.then_inc(L.sem, 1)
                act.wait_ge(*X2["pe"].after(f"rho{C - 1}", c))
                nc.scalar.activation(rhoT, bank[4][0:C, :], ACT.Copy).then_inc(L.sem, 1)
                act.wait_ge(*X2["dve"].after("shift", c))
                nc.scalar.activation(rho, rho, ACT.Exp).then_inc(L.sem, 1)
                act.wait_ge(*X2["dve"].after("nb_", c))
                nc.scalar.activation(ws[:, 0, :], ws[:, 0, :], ACT.Tanh, bias=v_("bcw")).then_inc(L.sem, 1)
                nc.scalar.activation(ws[:, 1, :], ws[:, 1, :], ACT.Tanh, bias=v_("bcb")).then_inc(L.sem, 1)

        def x2_dve(dve):
            finished(dve, F1, E * B)
            dve.wait_ge(in_x2, 48)
            L = X2S["dve"]
            nc.vector.tensor_copy(mask, mask_i).then_inc(L.sem, 1)
            dve.wait_ge(*L.after("mask_f"))
            nc.vector.tensor_scalar(mask, mask, NEG, NEG, ALU.mult, ALU.subtract).then_inc(L.sem, 1)
            for m, n in enumerate(("wcw", "wcb")):
                nc.vector.tensor_copy(wcr[:, m, :].rearrange("p (k a) -> p k a", k=K), bcast(v_(n, 0, K), P)).then_inc(L.sem, 1)
            nc.vector.memset(ones_at, 0.0).then_inc(L.sem, 1)
            dve.wait_ge(*L.after("zeros"))
            nc.vector.memset(ones_at[:, C - 1:C], 1.0).then_inc(L.sem, 1)
            dve.wait_ge(*X2S["act"].before(1))
            dve.wait_ge(*L.before(1))
            ln_all(dve, LN2, ln_dve, normed)
            L = X2["dve"]
            with dve.Fori(0, B) as c:

                def weigh(t):
                    dve.wait_ge(*X2["act"].after(f"h{t}", c))
                    if t >= NR2:
                        dve.wait_ge(*X2["pe"].after(f"rho{t - NR2}", c))
                    nc.vector.tensor_scalar(r2[:, t % NR2, :], h2[t % NH2][:, 0, :], v_("aw", 0), None,
                                            ALU.mult).then_inc(L.sem, 1)

                weigh(0)
                for t in range(C):
                    if t + 1 < C:
                        weigh(t + 1)
                    dve.wait_ge(*L.after(f"m{t}", c))
                    nc.vector.scalar_tensor_tensor(r2[:, t % NR2, :], h2[t % NH2][:, 1, :], v_("aw", 1), r2[:, t % NR2, :],
                                                   ALU.mult, ALU.add).then_inc(L.sem, 1)
                dve.wait_ge(*X2["pe"].after("rhoT", c))
                nc.vector.tensor_tensor(rho, bank[5][:, 0:QT * C].rearrange("p (q n) -> p q n", q=QT),
                                        over(mask[:, bass.ds(c * C, C)], QT), ALU.add).then_inc(L.sem, 1)
                dve.wait_ge(*L.after("masked", c))
                nc.vector.tensor_reduce(mx1[:, :], rho, AX.X, ALU.max).then_inc(L.sem, 1)
                dve.wait_ge(*L.after("mx", c))
                nc.vector.tensor_tensor(rho, rho, bcast(mx1[:, :], C), ALU.subtract).then_inc(L.sem, 1)
                dve.wait_ge(*X2["act"].after("exp", c))
                nc.vector.tensor_reduce(sum1[:, :], rho, AX.X, ALU.add).then_inc(L.sem, 1)
                dve.wait_ge(*L.after("sum", c))
                nc.vector.reciprocal(sum1[:, :], sum1[:, :]).then_inc(L.sem, 1)
                for m, (w, s_) in enumerate((("ew", "sw"), ("eb", "sb"))):
                    if m:
                        dve.wait_ge(*L.after("sw", c))
                    nc.vector.tensor_tensor(eu, rho, over(u2[:, m, bass.ds(c * C, C)], QT), ALU.mult).then_inc(L.sem, 1)
                    dve.wait_ge(*L.after(w, c))
                    nc.vector.tensor_reduce(ws[:, m, :], eu, AX.X, ALU.add).then_inc(L.sem, 1)
                dve.wait_ge(*L.after("sb", c))
                nc.vector.tensor_tensor(ws[:, 0, :], ws[:, 0, :], sum1[:, :], ALU.mult).then_inc(L.sem, 1)
                nc.vector.tensor_tensor(ws[:, 1, :], ws[:, 1, :], sum1[:, :], ALU.mult).then_inc(L.sem, 1)
                dve.wait_ge(*X2["act"].after("bs", c))
                for m in range(2):
                    for q in range(QT):
                        i = nc.vector.tensor_scalar(diag[:, m, q * P:(q + 1) * P], ident, ws[:, m, q:q + 1], None, ALU.mult)
                i.then_inc(L.sem, 1)
                dve.wait_ge(*X2["pe"].after("bc0", c))
                nc.vector.tensor_tensor(y2, normed(c), over(bank[6][:, :], K), ALU.mult).then_inc(L.sem, 1)
                dve.wait_ge(*X2["pe"].after("bc1", c))
                dve.wait_ge(*L.after("scaled", c))
                nc.vector.tensor_tensor(y2, y2, over(bank[7][:, :], K), ALU.add).then_inc(L.sem, 1)
                dve.wait_ge(*L.after("moved", c))
                for k in range(K):
                    xs = xT[:, k, bass.ds(c * S, S)]
                    nc.vector.scalar_tensor_tensor(xs, y2[:, k, :], tgx[:, 2:3], xs, ALU.mult, ALU.add).then_inc(L.sem, 1)

        F2, f2_route_sp, f2_sp, f2_route_pe, f2_pe, f2_route_act, f2_act, f2_route_dve, f2_dve, f2_pool = \
            expert_layer(2, X2, B)

        in_x3 = sem("in_x3")
        HP = HEADS // 2
        w_q3, w_k3, w_v3 = (cols(bigB, 2048 * i, (K, INNER)) for i in range(3))
        w_o3 = cols(bigB, 6144, (HP, D))
        q3, p3T = cols(bigA, 0, (HP, S)), cols(bigA, 4096, (HP, S))
        o3 = cols(fh, 0, (HP, S))
        kbd = cols(fs, 0, (HP, 2 * C))
        vbd = cols(fs, 1024, (HP, 2 * DH))
        NP3 = 3
        p3_of = [cols(wflat, 4096 + i * HEADS * C, (HEADS, C)) for i in range(NP3)]
        mx3, sum3 = sb("mx3", [P, 2, HEADS]), sb("sum3", [P, HEADS])
        SC3 = DH ** -0.5
        TQ = range(QT)

        def staggered(first, second):
            order = []
            for q in range(QT + 1):
                order += ([(first, q)] if q < QT else []) + ([(second, q - 1)] if q else [])
            return order

        def staggered_names(first, second):
            return [f"{w}{q}" for ws, q in staggered(first, second) for w in ws]

        X3 = lines("x3", pe=("k", "v", *(f"q{i}" for i in range(HP)),
                             *staggered_names(("s",), ("pT",)), *(f"o{i}" for i in range(HP)), "y0", "y1"),
                   act=("k", "v", *(f"q{i}" for i in range(HP)), *staggered_names(("exp",), ("pT",)),
                        *(f"o{i}" for i in range(HP)), "y0", "y1"),
                   dve=("ctx0", "ctx1", *staggered_names(("mx", "shift"), ("sum", "rsum", "p")),
                        "x0", "x1"))
        LN3 = ln_lines("x3_ln")
        X3Z = line("x3_zero_dve", "k", "v")

        def x3_load(sp):
            finished(sp, X2, B)
            for dst, n in ((w_q3, "x3_wq"), (w_k3, "x3_wk"), (w_v3, "x3_wv"), (w_o3, "x3_wo")):
                sp.dma_start(dst, dram[n]).then_inc(in_x3, 16)

        def x3_pe(pe):
            finished(pe, F2, E * B)
            ln_all(pe, LN3, ln_pe)
            pe.wait_ge(in_x3, 64)
            L = X3["pe"]
            with pe.Fori(0, B) as c:
                pe.wait_ge(*X3["dve"].before(c))
                pe.wait_ge(*X3["dve"].after("ctx1", c))
                for h in range(HP):
                    for k in range(K):
                        i = nc.tensor.matmul(bank[2][:, h * C:(h + 1) * C], w_k3[:, k, h * P:(h + 1) * P], ctxb[:, k, 0:C],
                                             start=k == 0, stop=k == K - 1)
                i.then_inc(L.sem, 1)
                for u in range(2):
                    for k in range(K):
                        i = nc.tensor.matmul(bank[3 + u][:, :], ctxb[:, k, :], w_v3[:, k, u * 512:(u + 1) * 512],
                                             start=k == 0, stop=k == K - 1)
                i.then_inc(L.sem, 1)
                for h in range(HP):
                    if h >= 3:
                        pe.wait_ge(*X3["act"].after(f"q{h - 3}", c))
                    for k in range(K):
                        i = nc.tensor.matmul(bank[5 + h % 3][:, :], w_q3[:, k, h * P:(h + 1) * P], nT[:, k, bass.ds(c * S, S)],
                                             start=k == 0, stop=k == K - 1)
                    i.then_inc(L.sem, 1)
                pe.wait_ge(*X3["act"].after(f"q{HP - 1}", c))

                def scores(q):
                    for h in range(HP):
                        i = nc.tensor.matmul(bank[q % 2 * 2 + h // 4][:, h % 4 * P:(h % 4 + 1) * P],
                                             q3[:, h, q * P:(q + 1) * P], kbd[:, h, :], start=True, stop=True)
                    i.then_inc(L.sem, 1)

                def turned(q):
                    pe.wait_ge(*X3["dve"].after(f"p{q}", c))
                    if q:
                        pe.wait_ge(*X3["act"].after(f"pT{q - 1}", c))
                    for h in range(HP):
                        i = nc.tensor.transpose(bank[4 + h // 4][:, h % 4 * P:(h % 4 + 1) * P],
                                                p3_of[q % NP3][:, 2 * h:2 * h + 2, :].rearrange("p h n -> p (h n)"), ident)
                    i.then_inc(L.sem, 1)

                for step, q in staggered(scores, turned):
                    step(q)
                pe.wait_ge(*X3["act"].after(f"pT{QT - 1}", c))
                for h in range(HP):
                    if h >= 2:
                        pe.wait_ge(*X3["act"].after(f"o{h - 2}", c))
                    nc.tensor.matmul(bank[6 + h % 2][:, :], vbd[:, h, :], p3T[:, h, :], start=True, stop=True).then_inc(L.sem, 1)
                pe.wait_ge(*X3["act"].after(f"o{HP - 1}", c))
                for k in range(K):
                    for h in range(HP):
                        i = nc.tensor.matmul(bank[k][:, :], w_o3[:, h, k * P:(k + 1) * P], o3[:, h, :], start=h == 0,
                                             stop=h == HP - 1)
                    i.then_inc(L.sem, 1)

        def x3_act(act):
            finished(act, F2, E * B)
            act.wait_ge(*X3Z.before(1))
            ln_all(act, LN3, ln_act)
            L = X3["act"]
            with act.Fori(0, B) as c:
                act.wait_ge(*X3["pe"].after("k", c))
                for u in range(2):
                    i = nc.scalar.activation(kbd[u * 64:(u + 1) * 64, :, u * C:(u + 1) * C],
                                             bank[2][u * 64:(u + 1) * 64, :].rearrange("p (h n) -> p h n", h=HP), ACT.Copy)
                i.then_inc(L.sem, 1)
                act.wait_ge(*X3["pe"].after("v", c))
                for u in range(2):
                    for g in range(2):
                        src = bank[3 + g][u * 64:(u + 1) * 64, :].rearrange("p (h d) -> p h d", d=2 * DH)
                        i = nc.scalar.activation(vbd[u * 64:(u + 1) * 64, 4 * g:4 * g + 4, u * DH:(u + 1) * DH],
                                                 src[:, :, u * DH:(u + 1) * DH], ACT.Copy)
                i.then_inc(L.sem, 1)
                for h in range(HP):
                    act.wait_ge(*X3["pe"].after(f"q{h}", c))
                    nc.scalar.activation(q3[:, h, :], bank[5 + h % 3][:, :], ACT.Copy).then_inc(L.sem, 1)

                def exponentials(q):
                    act.wait_ge(*X3["dve"].after(f"shift{q}", c))
                    nc.scalar.activation(p3_of[q % NP3], p3_of[q % NP3], ACT.Exp, scale=SC3).then_inc(L.sem, 1)

                def keep_turned(q):
                    act.wait_ge(*X3["pe"].after(f"pT{q}", c))
                    for u in range(2):
                        i = nc.scalar.activation(p3T[:, 4 * u:4 * u + 4, q * P:(q + 1) * P],
                                                 bank[4 + u][:, :].rearrange("p (h q) -> p h q", h=4), ACT.Copy)
                    i.then_inc(L.sem, 1)

                for step, q in staggered(exponentials, keep_turned):
                    step(q)
                for h in range(HP):
                    act.wait_ge(*X3["pe"].after(f"o{h}", c))
                    nc.scalar.activation(o3[:, h, :], bank[6 + h % 2][:, :], ACT.Copy).then_inc(L.sem, 1)
                for k in range(K):
                    act.wait_ge(*X3["pe"].after(f"y{k}", c))
                    nc.scalar.activation(sq[:, k, :], bank[k][:, :], ACT.Identity, bias=v_("bo", k)).then_inc(L.sem, 1)

        def x3_dve(dve):
            finished(dve, F2, E * B)
            nc.vector.memset(kbd, 0.0).then_inc(X3Z.sem, 1)
            nc.vector.memset(vbd, 0.0).then_inc(X3Z.sem, 1)
            ln_all(dve, LN3, ln_dve, normed)
            L = X3["dve"]
            with dve.Fori(0, B) as c:
                dve.wait_ge(*X3["pe"].before(c))
                for u in range(2):
                    nc.vector.tensor_copy(ctxb[:, :, u * C:(u + 1) * C], ctxT[:, :, bass.ds(c * C, C)]).then_inc(L.sem, 1)

                def shifted(q):
                    p3, mx = p3_of[q % NP3], mx3[:, q % 2, :]
                    if q >= NP3:
                        dve.wait_ge(*X3["pe"].after(f"pT{q - NP3}", c))
                    dve.wait_ge(*X3["pe"].after(f"s{q}", c))
                    sc = [bank[q % 2 * 2 + u][:, :].rearrange("p (h n) -> p h n", n=C) for u in range(2)]
                    for u in range(2):
                        i = nc.vector.tensor_reduce(mx[:, 8 * u:8 * u + 8], sc[u], AX.X, ALU.max)
                    i.then_inc(L.sem, 1)
                    dve.wait_ge(*L.after(f"mx{q}", c))
                    for u in range(2):
                        i = nc.vector.tensor_tensor(p3[:, 8 * u:8 * u + 8, :], sc[u], bcast(mx[:, 8 * u:8 * u + 8], C), ALU.subtract)
                    i.then_inc(L.sem, 1)

                def probabilities(q):
                    p3 = p3_of[q % NP3]
                    if q:
                        dve.wait_ge(*L.after(f"p{q - 1}", c))
                    dve.wait_ge(*X3["act"].after(f"exp{q}", c))
                    nc.vector.tensor_reduce(sum3[:, :], p3, AX.X, ALU.add).then_inc(L.sem, 1)
                    dve.wait_ge(*L.after(f"sum{q}", c))
                    nc.vector.reciprocal(sum3[:, :], sum3[:, :]).then_inc(L.sem, 1)
                    dve.wait_ge(*L.after(f"rsum{q}", c))
                    nc.vector.tensor_tensor(p3, p3, bcast(sum3[:, :], C), ALU.mult).then_inc(L.sem, 1)

                for step, q in staggered(shifted, probabilities):
                    step(q)
                for k in range(K):
                    dve.wait_ge(*X3["act"].after(f"y{k}", c))
                    xs = xT[:, k, bass.ds(c * S, S)]
                    nc.vector.scalar_tensor_tensor(xs, sq[:, k, :], tgx[:, 3:4], xs, ALU.mult, ALU.add).then_inc(L.sem, 1)

        in_f3, sent = sem("in_f3"), sem("sent")
        rhsT = cols(wflat, 0, (K, D))
        rq32 = cols(wflat, 512, (K, D))
        rqT = cols(wflat, 1024, (K, D), BF16)
        rq = cols(wflat, 1280, (K, D), BF16)
        identb = cols(wflat, 1536, (1, P), BF16)[:, 0, :]
        rdiag = cols(wflat, 1600, (1, D))[:, 0, :]
        rsb = cols(wflat, 1856, (1, D))[:, 0, :]
        rs, rinv = sb("rs", [P, K]), sb("rinv", [P, K])
        xt = cols(bigA, 0, (T, D))
        xn = cols(bigA, 4096, (T, D))
        q_tok = cols(fn, 0, (T, D), BF16)
        q_f = cols(fh, 0, (K, N), BF16)
        yo = cols(bigB, 0, (T, D))
        stats, mv = sb("stats", [P, T, 6]), sb("mv", [P, T, 2])
        std = sb("std", [P, T])
        ls, linv = sb("ls", [P, T]), sb("linv", [P, T])
        F3 = lines("f3", pe=(*(f"x{i}" for i in range(T)), "rq", "rsb", *(f"q{i}" for i in range(T)), *(f"y{i}" for i in range(T))),
                   act=(*(f"x{i}" for i in range(T)), "std", *(f"q{i}" for i in range(T))),
                   dve=("identb", "rmax", "rs", "rinv", "rmul", "rround", "rclip", "rq", "rdiag0", "rdiag1", "rsb",
                        *(f"stats{i}" for i in range(T)), *(f"mv{i}" for i in range(T)),
                        "eps", "rstd", *(f"n{i}" for i in range(T)), "amax", "ls", "linv", *(f"mul{i}" for i in range(T)), "round", "clip",
                        *(f"{w}{i}" for i in range(T) for w in ("y", "x"))))

        def f3_sp(sp):
            finished(sp, F2, E * B)
            sp.dma_start(rhsT, dram["f3_rhsT"]).then_inc(in_f3, 16)
            for i in range(T):
                sp.wait_ge(*F3["dve"].after(f"x{i}"))
                sp.dma_start(out[i * P:(i + 1) * P, :], yo[:, i, :]).then_inc(sent, 16)
            sp.wait_ge(sent, 16 * T)

        def f3_pe(pe):
            finished(pe, X3, B)
            L = F3["pe"]
            for i in range(T):
                if i >= 4:
                    pe.wait_ge(*F3["act"].after(f"x{i - 4}"))
                for k in range(K):
                    m = nc.tensor.transpose(bank[i % 4][:, k * P:(k + 1) * P], xT[:, k, i * P:(i + 1) * P], ident)
                m.then_inc(L.sem, 1)
            pe.wait_ge(*F3["dve"].after("rclip"))
            b16 = bank[4][:, 0:2 * P].bitcast(BF16)
            for k in range(K):
                for o in range(K):
                    m = nc.tensor.transpose(b16[:, (k * K + o) * P:(k * K + o + 1) * P], rqT[:, o, k * P:(k + 1) * P], identb)
            m.then_inc(L.sem, 1)
            pe.wait_ge(*F3["dve"].after("rdiag1"))
            nc.tensor.matmul(bank[5][:, 0:D], ones, rdiag, start=True, stop=True).then_inc(L.sem, 1)
            pe.wait_ge(*F3["dve"].after("clip"))
            for i in range(T):
                if i >= 2:
                    pe.wait_ge(*F3["act"].after(f"q{i - 2}"))
                bq = bank[6 + i % 2][:, 0:P].bitcast(BF16)
                for k in range(K):
                    m = nc.tensor.transpose(bq[:, k * P:(k + 1) * P], q_tok[:, i, k * P:(k + 1) * P], identb)
                m.then_inc(L.sem, 1)
            for i in range(T):
                pe.wait_ge(*F3["act"].after(f"q{i}"))
                if i >= 4:
                    pe.wait_ge(*F3["dve"].after(f"y{i - 4}"))
                for k in range(K):
                    m = nc.tensor.matmul(bank[i % 4][:, 0:D], q_f[:, k, i * P:(i + 1) * P], rq[:, k, :], start=k == 0,
                                         stop=k == K - 1)
                m.then_inc(L.sem, 1)

        def f3_act(act):
            finished(act, X3, B)
            L = F3["act"]
            for i in range(T):
                act.wait_ge(*F3["pe"].after(f"x{i}"))
                nc.scalar.activation(xt[:, i, :], bank[i % 4][:, 0:D], ACT.Copy).then_inc(L.sem, 1)
            act.wait_ge(*F3["dve"].after("eps"))
            nc.scalar.activation(std[:, :], std[:, :], ACT.Sqrt).then_inc(L.sem, 1)
            for i in range(T):
                act.wait_ge(*F3["pe"].after(f"q{i}"))
                bq = bank[6 + i % 2][:, 0:P].bitcast(BF16)
                nc.scalar.activation(q_f[:, :, i * P:(i + 1) * P], bq.rearrange("p (k q) -> p k q", k=K),
                                     ACT.Copy).then_inc(L.sem, 1)

        def f3_dve(dve):
            finished(dve, X3, B)
            dve.wait_ge(in_f3, 16)
            L = F3["dve"]
            nc.vector.tensor_copy(identb, ident).then_inc(L.sem, 1)
            nc.vector.tensor_reduce(rs[:, :], rhsT, AX.X, ALU.max, apply_absolute_value=True).then_inc(L.sem, 1)
            dve.wait_ge(*L.after("rmax"))
            nc.vector.tensor_scalar(rs[:, :], rs[:, :], 1e-12, 1.0 / 127.0, ALU.max, ALU.mult).then_inc(L.sem, 1)
            dve.wait_ge(*L.after("rs"))
            nc.vector.reciprocal(rinv[:, :], rs[:, :]).then_inc(L.sem, 1)
            dve.wait_ge(*L.after("rinv"))
            for k in range(K):
                i = nc.vector.tensor_scalar(rq32[:, k, :], rhsT[:, k, :], rinv[:, k:k + 1], ROUND, ALU.mult, ALU.add)
            i.then_inc(L.sem, 1)
            dve.wait_ge(*L.after("rmul"))
            nc.vector.tensor_scalar(rq32, rq32, ROUND, 127.0, ALU.subtract, ALU.min).then_inc(L.sem, 1)
            dve.wait_ge(*L.after("rround"))
            nc.vector.tensor_scalar(rqT, rq32, -127.0, None, ALU.max).then_inc(L.sem, 1)
            dve.wait_ge(*F3["pe"].after("rq"))
            nc.vector.tensor_copy(rq.rearrange("p k d -> p (k d)"), bank[4][:, 0:2 * P].bitcast(BF16)).then_inc(L.sem, 1)
            for k in range(K):
                nc.vector.tensor_scalar(rdiag[:, k * P:(k + 1) * P], ident, rs[:, k:k + 1], None, ALU.mult).then_inc(L.sem, 1)
            dve.wait_ge(*F3["pe"].after("rsb"))
            nc.vector.tensor_copy(rsb, bank[5][:, 0:D]).then_inc(L.sem, 1)
            for i in range(T):
                dve.wait_ge(*F3["act"].after(f"x{i}"))
                nc.vector.bn_stats(stats[:, i, :], xt[:, i, :]).then_inc(L.sem, 1)
            for i in range(T):
                dve.wait_ge(*L.after(f"stats{i}"))
                nc.vector.bn_aggr(mv[:, i, :], stats[:, i, :]).then_inc(L.sem, 1)
            dve.wait_ge(*L.after(f"mv{T - 1}"))
            nc.vector.tensor_scalar(std[:, :], mv[:, :, 1], EPS, None, ALU.add).then_inc(L.sem, 1)
            dve.wait_ge(*F3["act"].after("std"))
            nc.vector.reciprocal(std[:, :], std[:, :]).then_inc(L.sem, 1)
            dve.wait_ge(*L.after("rstd"))
            for i in range(T):
                nc.vector.tensor_scalar(xn[:, i, :], xt[:, i, :], mv[:, i, 0:1], std[:, i:i + 1], ALU.subtract,
                                        ALU.mult).then_inc(L.sem, 1)
            dve.wait_ge(*L.after(f"n{T - 1}"))
            nc.vector.tensor_reduce(ls[:, :], xn, AX.X, ALU.max, apply_absolute_value=True).then_inc(L.sem, 1)
            dve.wait_ge(*L.after("amax"))
            nc.vector.tensor_scalar(ls[:, :], ls[:, :], 1e-12, 1.0 / 127.0, ALU.max, ALU.mult).then_inc(L.sem, 1)
            dve.wait_ge(*L.after("ls"))
            nc.vector.reciprocal(linv[:, :], ls[:, :]).then_inc(L.sem, 1)
            dve.wait_ge(*L.after("linv"))
            for i in range(T):
                nc.vector.tensor_scalar(xn[:, i, :], xn[:, i, :], linv[:, i:i + 1], ROUND, ALU.mult, ALU.add).then_inc(L.sem, 1)
            dve.wait_ge(*L.after(f"mul{T - 1}"))
            nc.vector.tensor_scalar(xn, xn, ROUND, 127.0, ALU.subtract, ALU.min).then_inc(L.sem, 1)
            dve.wait_ge(*L.after("round"))
            nc.vector.tensor_scalar(q_tok, xn, -127.0, None, ALU.max).then_inc(L.sem, 1)
            for i in range(T):
                dve.wait_ge(*F3["pe"].after(f"y{i}"))
                nc.vector.scalar_tensor_tensor(yo[:, i, :], bank[i % 4][:, 0:D], ls[:, i:i + 1], rsb, ALU.mult,
                                               ALU.mult).then_inc(L.sem, 1)
                dve.wait_ge(*L.after(f"y{i}"))
                nc.vector.scalar_tensor_tensor(yo[:, i, :], yo[:, i, :], tgf[:, 3:4], xt[:, i, :], ALU.mult,
                                               ALU.add).then_inc(L.sem, 1)

        block = ctx.enter_context(nc.Block())

        @block.sync
        def _(sp):
            setup_sp(sp)
            lstm2_sp(sp)
            x1_load(sp)
            f0_route_sp(sp)
            f0_sp(sp)
            f1_route_sp(sp)
            x2_load(sp)
            f1_sp(sp)
            f2_route_sp(sp)
            x3_load(sp)
            f2_sp(sp)
            f3_sp(sp)

        @block.tensor
        def _(pe):
            opened(pe, "pe")
            setup_pe(pe)
            xproj_pe(pe)
            rec_pe(pe)
            lstm2_pe(pe)
            f0_route_pe(pe)
            f0_pe(pe)
            x1_pe(pe)
            f1_route_pe(pe)
            f1_pe(pe)
            x2_pe(pe)
            f2_route_pe(pe)
            f2_pe(pe)
            x3_pe(pe)
            f3_pe(pe)

        @block.gpsimd
        def _(pool):
            opened(pool, "pool")
            rec_pool(pool)
            f0_pool(pool)
            f1_pool(pool)
            f2_pool(pool)

        @block.scalar
        def _(act):
            opened(act, "act")
            setup_act(act)
            xproj_act(act)
            rec_act(act)
            lstm2_act(act)
            f0_route_act(act)
            f0_act(act)
            x1_act(act)
            f1_route_act(act)
            f1_act(act)
            x2_act(act)
            f2_route_act(act)
            f2_act(act)
            x3_act(act)
            f3_act(act)

        @block.vector
        def _(dve):
            opened(dve, "dve")
            setup_dve(dve)
            xproj_dve(dve)
            rec_dve(dve)
            lstm2_dve(dve)
            f0_route_dve(dve)
            f0_dve(dve)
            x1_dve(dve)
            f1_route_dve(dve)
            f1_dve(dve)
            x2_dve(dve)
            f2_route_dve(dve)
            f2_dve(dve)
            x3_dve(dve)
            f3_dve(dve)


def feature_major(a):
    import numpy as np
    r, c = a.shape
    return np.ascontiguousarray(a.T.reshape(c // P, P, r).transpose(1, 0, 2))


def row_tiles(a):
    import numpy as np
    r, c = a.shape
    return np.ascontiguousarray(a.reshape(r // P, P, c).transpose(1, 0, 2))


def pack(inp):
    import numpy as np
    arr = {k: np.asarray(v) for k, v in inp.items()}

    def col(a):
        return a.reshape(-1, P).T

    def rep(a):
        return np.broadcast_to(a.reshape(1, -1), (P, a.size))

    x0, x1, x2, x3 = (f"L{i}_xattn_" for i in range(4))
    f0, f1, f2, f3 = (f"L{i}_ffn_" for i in range(4))
    vecs = dict(
        b_att=col(arr[x0 + "b_att"]), v=col(arr[x0 + "v"]),
        b_ih0=col(arr[x0 + "b_ih0"]), b_hh0=col(arr[x0 + "b_hh0"]),
        b_ih1=col(arr[x0 + "b_ih1"]), b_hh1=col(arr[x0 + "b_hh1"]),
        f0_b1=col(arr[f0 + "b1"]), f0_b2=col(arr[f0 + "b2"]), f0_br=rep(arr[f0 + "br"]),
        f2_b1=col(arr[f2 + "b1"]), f2_b2=col(arr[f2 + "b2"]), f2_br=rep(arr[f2 + "br"]),
        **{n: col(arr[x1 + n]) for n in ("bq_c", "bk_s", "bv_s", "bq_s", "bk_c", "bv_c", "bg")},
        ab=col(arr[x2 + "b"]), aw=col(arr[x2 + "w"]), wcw=col(arr[x2 + "Wcw"]), wcb=col(arr[x2 + "Wcb"]),
        bcw=rep(arr[x2 + "bcw"]), bcb=rep(arr[x2 + "bcb"]), bo=col(arr[x3 + "bo"]),
        gx=rep(arr["g_xattn"]), gf=rep(arr["g_ffn"]))
    vec = np.ascontiguousarray(np.concatenate([vecs[n] for n in VECS], axis=1))

    ident = np.eye(P, dtype=np.float32)
    p = np.arange(P)
    diag_b = (p[:, None] // 32 == np.arange(B)[None]).astype(np.float32)
    i, j = np.arange(E)[:, None], np.arange(E)[None]
    before, upto = ((j < i).astype(np.float32).reshape(1, -1), (j <= i).astype(np.float32).reshape(1, -1))
    pos = np.clip((np.arange(S) + 0.5) * (C / S) - 0.5, 0.0, C - 1)
    lo = np.floor(pos).astype(int)
    hi = np.minimum(lo + 1, C - 1)
    interp = np.zeros((P, S), np.float32)
    interp[lo, np.arange(S)] += (1.0 - (pos - lo)).astype(np.float32)
    interp[hi, np.arange(S)] += (pos - lo).astype(np.float32)
    consts = dict(ident=ident, ones=np.ones((P, P), np.float32), mean=np.full((P, P), 1.0 / D, np.float32),
                  diag_b=diag_b, before=np.broadcast_to(before, (P, E * E)), upto=np.broadcast_to(upto, (P, E * E)),
                  interp=interp)
    cst = np.ascontiguousarray(np.concatenate([consts[n] for n in CONSTS], axis=1), dtype=np.float32)

    ctx = arr["ctx_1024"].reshape(B * C, D)
    ctxq = arr["ctx_1024"].reshape(B, 2, 32, D).transpose(1, 0, 2, 3).reshape(B * C, D)
    w_ih0 = arr[x0 + "W_ih0"]
    w1x = np.stack([feature_major(arr[x1 + n]) for n in ("Wq_c", "Wk_s", "Wv_s", "Wq_s", "Wk_c", "Wv_c")], axis=1)
    mask = np.ascontiguousarray(np.broadcast_to(arr["mask_BxS2_ik0"].reshape(1, B * C), (P, B * C)))
    return dict(
        vec=vec, cst=cst, ctxT=feature_major(ctx), ctxTq=feature_major(ctxq), xT=feature_major(arr["x"].reshape(N, D)),
        w_f=row_tiles(arr[x0 + "Wf"]), w_h=row_tiles(arr[x0 + "Wh"]),
        w_x=feature_major(w_ih0[:, :D]), w_at=feature_major(w_ih0[:, D:]), w_hh=feature_major(arr[x0 + "W_hh0"]),
        w_ih1=feature_major(arr[x0 + "W_ih1"]), w_hh1=feature_major(arr[x0 + "W_hh1"]),
        f0_w1=np.stack([row_tiles(a) for a in arr[f0 + "w1"]]), f0_w2=np.stack([row_tiles(a) for a in arr[f0 + "w2"]]),
        f0_wr=row_tiles(arr[f0 + "wr"]),
        f1_w1=np.stack([row_tiles(a) for a in arr[f1 + "w1"]]), f1_w3=np.stack([row_tiles(a) for a in arr[f1 + "w3"]]),
        f1_w2=np.stack([row_tiles(a) for a in arr[f1 + "w2"]]), f1_wr=row_tiles(arr[f1 + "router_w"]),
        f2_w1=np.stack([row_tiles(a) for a in arr[f2 + "W1"]]), f2_w2=np.stack([row_tiles(a) for a in arr[f2 + "W2"]]),
        f2_wr=row_tiles(arr[f2 + "Wr"]),
        x1_w=np.ascontiguousarray(w1x), x1_wg=feature_major(arr[x1 + "Wg"]),
        x2_ws=row_tiles(arr[x2 + "Ws"]), x2_w=row_tiles(arr[x2 + "W"]), mask=mask,
        x3_wq=feature_major(arr[x3 + "Wq"]), x3_wk=feature_major(arr[x3 + "Wk"]), x3_wv=feature_major(arr[x3 + "Wv"]),
        x3_wo=feature_major(arr[x3 + "Wo"]), f3_rhsT=feature_major(arr[f3 + "rhs"]))


def kernel(**inputs):
    import numpy as np
    import concourse.bacc as bacc
    from concourse.bass_utils import run_bass_kernel_spmd

    arrays = pack(inputs)
    nc = bacc.Bacc("TRN2", target_bir_lowering=False, num_devices=1)
    dram = {n: nc.dram_tensor(f"in_{n}", a.shape, mybir.dt.from_np(a.dtype), kind="ExternalInput").ap()
            for n, a in arrays.items()}
    out = nc.dram_tensor("out_x", (N, D), F32, kind="ExternalOutput").ap()
    build(nc, dram, out)
    r = run_bass_kernel_spmd(nc, [{f"in_{n}": a for n, a in arrays.items()}], core_ids=[0])
    return np.asarray(r.results[0]["out_x"]).reshape(B, S, D)
```

```python
from contextlib import ExitStack

import concourse.bass as bass
from concourse import mybir
from concourse.alu_op_type import AluOpType as ALU

F32, BF16, F16, I32 = mybir.dt.float32, mybir.dt.bfloat16, mybir.dt.float16, mybir.dt.int32
ACT = mybir.ActivationFunctionType
AX = mybir.AxisListType

P = 128
B, S, C, D = 4, 512, 64, 256
N = B * S
K = D // P
E = 8
FW = 1024
FW1 = 512
HEADS, DH = 16, 64
INNER = HEADS * DH
NG = 4 * D // P
QT = S // P
EPS = 1e-5
ROUND = 1.5 * 2.0 ** 23
NEG = 1e30
HS = 16.0
WS = 64.0
GS = 256.0

VECS = ["b_att", "v", "b_ih0", "b_hh0", "b_ih1", "b_hh1", "f0_b1", "f0_b2", "f0_br", "f2_b1", "f2_b2", "f2_br",
        "bq_c", "bk_s", "bv_s", "bq_s", "bk_c", "bv_c", "bg", "ab", "aw", "wcw", "wcb", "bcw", "bcb", "bo", "gx", "gf"]
WIDTH = dict(b_att=K, v=K, b_ih0=NG, b_hh0=NG, b_ih1=NG, b_hh1=NG, f0_b1=E * FW // P, f0_b2=E * K, f0_br=E,
             f2_b1=E * FW // P, f2_b2=E * K, f2_br=E, bq_c=K, bk_s=K, bv_s=K, bq_s=K, bk_c=K, bv_c=K, bg=K,
             ab=K, aw=K, wcw=K, wcb=K, bcw=1, bcb=1, bo=K, gx=4, gf=4)
VCOL, at = {}, 0
for name in VECS:
    VCOL[name] = at
    at += WIDTH[name]
NVEC = at
CONSTS = dict(ident=P, ones=P, mean=P, diag_b=B, before=E * E, upto=E * E, interp=S)
CCOL, at = {}, 0
for name in CONSTS:
    CCOL[name] = at
    at += CONSTS[name]
NCONST = at


class Line:

    def __init__(self, sem, steps):
        self.sem, self.n = sem, len(steps)
        self.pos = {s: i + 1 for i, s in enumerate(steps)}
        assert len(self.pos) == self.n

    def after(self, step, it=0):
        return self.sem, it * self.n + (self.pos[step] + 1)

    def before(self, it):
        return self.sem, it * self.n + 1


def build(nc, dram, out):
    ctx = ExitStack()
    with ctx:
        def sb(name, shape, dt=F32):
            return ctx.enter_context(nc.sbuf_tensor(name, shape, dt))

        def sem(name):
            return ctx.enter_context(nc.semaphore(name))

        def line(name, *steps):
            every_line[name.rsplit("_", 1)[1]].append(Line(sem(name), steps))
            return every_line[name.rsplit("_", 1)[1]][-1]

        every_line = dict(pe=[], act=[], dve=[], pool=[])

        def opened(eng, name):
            for one in every_line[name]:
                eng.sem_inc(one.sem, 1)

        xT = sb("xT", [P, K, N])
        nT = sb("nT", [P, K, N])
        big = sb("big", [P, 2, 8192])
        wbuf = sb("wbuf", [P, 2, 4096])
        hist_h = sb("hist_h", [P, K, B, S + 1])
        hist_s = sb("hist_s", [P, K, B, S + 1])
        nb = sb("nb", [P, K, S])
        sq = sb("sq", [P, K, S])
        rstd = sb("rstd", [P, S])
        cst = sb("cst", [P, NCONST])
        vec = sb("vec", [P, NVEC])
        ctxT = sb("ctxT", [P, K, B * C])
        tgx = sb("tgx", [P, 4])
        tgf = sb("tgf", [P, 4])
        tgf_w = sb("tgf_w", [P, 4])
        ws_col, eps_col = sb("ws_col", [P, 1]), sb("eps_col", [P, 1])
        fo = sb("fo", [P, K, S])
        bank = [ctx.enter_context(nc.psum_tensor(f"bank{i}", [P, 512], F32)) for i in range(8)]

        def const(name):
            return cst[:, CCOL[name]:CCOL[name] + CONSTS[name]]

        def v_(name, i=0, n=1):
            return vec[:, VCOL[name] + i:VCOL[name] + i + n]

        ident, ones, mean_w = const("ident"), const("ones"), const("mean")

        def cols(t, off, shape, dt=F32):
            n = 1
            for s in shape:
                n *= s
            words = n * (2 if dt in (BF16, F16) else 4) // 4
            a = t[:, off:off + words]
            if dt != F32:
                a = a.bitcast(dt)
            if len(shape) == 2:
                a = a.rearrange("p (a b) -> p a b", a=shape[0])
            elif len(shape) == 3:
                a = a.rearrange("p (a b c) -> p a b c", a=shape[0], b=shape[1])
            return a

        def flat(t):
            n = len(t.shape)
            return t[:, :, :].rearrange("p a b -> p (a b)") if n == 3 else \
                t[:, :, :, :].rearrange("p a b c -> p (a b c)")

        bigA, bigB, wflat = big[:, 0, :], big[:, 1, :], flat(wbuf)
        fh, fs, fn = flat(hist_h), flat(hist_s), flat(nT)

        def bcast(a, n):
            return a.unsqueeze(2).to_broadcast([a.shape[0], a.shape[1], n])

        def over(a, m):
            return a.unsqueeze(1).to_broadcast([a.shape[0], m, a.shape[1]])

        quadrant = sb("quadrant", [P, QT, P])
        LN_PE, LN_ACT = ("mean0", "mean1", "var0", "var1", "rep0", "rep1"), ("sq0", "sq1", "std0", "std1")
        LN_DVE = ("cent0", "cent1", "rstd0", "rstd1", "normed0", "normed1")

        def ln_buffers(second):
            return (nb[:, :, :], sq[:, :, :], rstd[:, :]), \
                (cols(second, 0, (K, S)), cols(second, K * S, (K, S)), second[:, 2 * K * S:2 * K * S + S])

        def x_of(c):
            return xT[:, :, bass.ds(c * S, S)]

        def ln_pe(pe, L, it, bufs):
            for u in range(2):
                for k in range(K):
                    i = nc.tensor.matmul(bank[2 * u][:, :], mean_w, xT[:, k, bass.ds((2 * it + u) * S, S)], start=k == 0,
                                         stop=k == K - 1)
                i.then_inc(L["pe"].sem, 1)
            for u, (_, squares, _) in enumerate(bufs):
                pe.wait_ge(*L["act"].after(f"sq{u}", it))
                for q in range(QT):
                    for k in range(K):
                        i = nc.tensor.matmul(bank[2 * u + 1][q * 32:(q + 1) * 32, 0:P], mean_w[:, 0:32],
                                             squares[:, k, q * P:(q + 1) * P], start=k == 0, stop=k == K - 1,
                                             tile_position=(0, q * 32))
                i.then_inc(L["pe"].sem, 1)
            for u, (_, _, dev) in enumerate(bufs):
                pe.wait_ge(*L["dve"].after(f"rstd{u}", it))
                for q in range(QT):
                    i = nc.tensor.matmul(bank[2 * u + 1][:, q * P:(q + 1) * P], quadrant[:, q, :], dev[:, 0:P],
                                         start=True, stop=True)
                i.then_inc(L["pe"].sem, 1)

        def ln_act(act, L, it, bufs):
            nc.scalar.preload_act_table(ACT.Sqrt)
            for u, (centered, squares, _) in enumerate(bufs):
                act.wait_ge(*L["dve"].after(f"cent{u}", it))
                nc.scalar.activation(squares, centered, ACT.Square).then_inc(L["act"].sem, 1)
            for u, (_, _, dev) in enumerate(bufs):
                act.wait_ge(*L["pe"].after(f"var{u}", it))
                nc.scalar.activation(dev[:, 0:P], bank[2 * u + 1][:, 0:P], ACT.Sqrt, bias=eps_col[:, :]).then_inc(L["act"].sem, 1)

        def ln_dve(dve, L, it, bufs, dst=None):
            dve.wait_ge(*L["dve"].before(it))
            for u, (centered, _, _) in enumerate(bufs):
                dve.wait_ge(*L["pe"].after(f"mean{u}", it))
                nc.vector.tensor_tensor(centered, x_of(2 * it + u), over(bank[2 * u][:, :], K),
                                        ALU.subtract).then_inc(L["dve"].sem, 1)
            for u, (centered, _, dev) in enumerate(bufs):
                dve.wait_ge(*L["act"].after(f"std{u}", it))
                nc.vector.reciprocal(dev[:, 0:P], dev[:, 0:P]).then_inc(L["dve"].sem, 1)
            for u, (centered, _, _) in enumerate(bufs):
                dve.wait_ge(*L["pe"].after(f"rep{u}", it))
                nc.vector.tensor_tensor(dst(2 * it + u) if dst else centered, centered,
                                        over(bank[2 * u + 1][:, :], K),
                                        ALU.mult).then_inc(L["dve"].sem, 1)

        def ln_lines(name):
            return lines(name, pe=LN_PE, act=LN_ACT, dve=LN_DVE)

        def normed(c):
            return nT[:, :, bass.ds(c * S, S)]

        def lines(name, **steps):
            return {e: line(f"{name}_{e}", *steps[e]) for e in steps}

        def finished(eng, L, iters=1):
            for e in L:
                eng.wait_ge(*L[e].before(iters))

        in_small, in_ctx, in_x, in_rec, in_l1 = (sem(n) for n in ("in_small", "in_ctx", "in_x", "in_rec", "in_l1"))
        xp = cols(flat(big), 0, (2 * NG * B, S), F16)
        xp_hi, xp_lo = (cols(big[:, u, :], 0, (NG, B, S), F16) for u in range(2))
        ctxTq = sb("ctxTq", [P, K, 2 * P])
        w_x = cols(fn, 0, (K, 4 * D))
        w_f, w_h32 = cols(fn, 2048, (K, D)), cols(fn, 2560, (K, D))
        w_hh32, w_at32 = cols(fh, 0, (K, 4 * D)), cols(fh, 2048, (K, 4 * D))
        g32 = cols(fs, 0, (2, 4 * D))
        whh = cols(wflat, 0, (2, K, 4 * D), F16)
        gat = cols(wflat, 2048, (2, 2, 4 * D), F16)
        wh = cols(wflat, 4096, (2, K, D), F16)
        h_t, s_t = sb("h_t", [P, K, B]), sb("s_t", [P, K, B])
        ident16 = sb("ident16", [P, P], F16)
        GROUPS = dict(f=(2, 3), ig=(0, 1, 4, 5), o=(6, 7))
        SLOT = {g: n for n, g in enumerate(sum(GROUPS.values(), ()))}
        fproj = sb("fproj", [P, K, B * C])
        vrep = sb("vrep", [P, K, 32])
        b0 = sb("b0", [P, NG])
        b1 = sb("b1", [P, NG])
        hp = sb("hp", [P, K, 2 * B], F16)

        def setup_sp(sp):
            sp.dma_start(vec[:, :], dram["vec"]).then_inc(in_small, 16)
            sp.dma_start(cst[:, :], dram["cst"]).then_inc(in_small, 16)
            sp.dma_start(ctxT[:, :, :], dram["ctxT"]).then_inc(in_ctx, 16)
            sp.dma_start(ctxTq[:, :, :], dram["ctxTq"]).then_inc(in_ctx, 16)
            sp.dma_start(xT[:, :, :], dram["xT"]).then_inc(in_x, 16)
            for dst, n in ((w_f, "w_f"), (w_at32, "w_at"), (w_x, "w_x"), (w_hh32, "w_hh"), (w_h32, "w_h")):
                sp.dma_start(dst, dram[n]).then_inc(in_rec, 16)

        SU = lines("setup", pe=("fproj0", "fproj1", "g0", "g1", "g2", "g3"),
                   act=("tgx", "tgf", "fproj0", "fproj1", "g0", "g1", "g2", "g3"),
                   dve=("b0", "b1", "vrep", "zero_h", "ident16", "b0_ifo", "b0_g", "b0_o", "b1_half", "b1_half2", "half_hh",
                        "half_h", "zero_h_t", "tgf_w", "b2_0", "b2_2", "ws", "eps", "no_quadrant", "quadrant", "done"),
                   pool=tuple(f"{w}_{i}" for w in ("whh", "wh", "gat") for i in ("hi", "rest", "lo")))

        def setup_pe(pe):
            pe.wait_ge(in_ctx, 32)
            pe.wait_ge(in_rec, 80)
            for a in range(K):
                for k in range(K):
                    i = nc.tensor.matmul(bank[a][:, 0:B * C], w_f[:, k, a * P:(a + 1) * P], ctxT[:, k, :],
                                         start=k == 0, stop=k == K - 1)
                i.then_inc(SU["pe"].sem, 1)
            for j in range(2):
                for u in range(2):
                    for k in range(K):
                        i = nc.tensor.matmul(bank[2 + 2 * j + u][:, :], ctxTq[:, k, j * P:(j + 1) * P],
                                             w_at32[:, k, u * 512:(u + 1) * 512], start=k == 0, stop=k == K - 1)
                    i.then_inc(SU["pe"].sem, 1)

        def setup_act(act):
            act.wait_ge(in_small, 32)
            nc.scalar.activation(tgx[:, :], v_("gx", 0, 4), ACT.Tanh).then_inc(SU["act"].sem, 1)
            nc.scalar.activation(tgf[:, :], v_("gf", 0, 4), ACT.Tanh).then_inc(SU["act"].sem, 1)
            for a in range(K):
                act.wait_ge(*SU["pe"].after(f"fproj{a}"))
                nc.scalar.activation(fproj[:, a, :], bank[a][:, 0:B * C], ACT.Identity,
                                     bias=v_("b_att", a)).then_inc(SU["act"].sem, 1)
            for j in range(2):
                for u in range(2):
                    act.wait_ge(*SU["pe"].after(f"g{2 * j + u}"))
                    src, dst = bank[2 + 2 * j + u], g32[:, j, u * 512:(u + 1) * 512]
                    if u == 0:
                        i = nc.scalar.activation(dst, src[:, :], ACT.Copy, scale=GS / 2)
                    else:
                        nc.scalar.activation(dst[:, 0:256], src[:, 0:256], ACT.Copy, scale=GS)
                        i = nc.scalar.activation(dst[:, 256:512], src[:, 256:512], ACT.Copy, scale=GS / 2)
                    i.then_inc(SU["act"].sem, 1)

        def setup_dve(dve):
            L = SU["dve"]
            dve.wait_ge(in_small, 32)
            nc.vector.tensor_tensor(b0[:, :], v_("b_ih0", 0, NG), v_("b_hh0", 0, NG), ALU.add).then_inc(L.sem, 1)
            nc.vector.tensor_tensor(b1[:, :], v_("b_ih1", 0, NG), v_("b_hh1", 0, NG), ALU.add).then_inc(L.sem, 1)
            nc.vector.tensor_copy(vrep[:, :, :], bcast(v_("v", 0, K), 32)).then_inc(L.sem, 1)
            nc.vector.memset(hp[:, :, :], 0.0).then_inc(L.sem, 1)
            nc.vector.tensor_copy(ident16[:, :], ident).then_inc(L.sem, 1)
            dve.wait_ge(*L.after("b1"))
            for g0, g1, f in ((0, 4, GS / 2), (4, 6, GS), (6, 8, GS / 2)):
                nc.vector.tensor_scalar(b0[:, g0:g1], b0[:, g0:g1], f, None, ALU.mult).then_inc(L.sem, 1)
            nc.vector.tensor_scalar(b1[:, 0:4], b1[:, 0:4], 0.5, None, ALU.mult).then_inc(L.sem, 1)
            nc.vector.tensor_scalar(b1[:, 6:8], b1[:, 6:8], 0.5, None, ALU.mult).then_inc(L.sem, 1)
            dve.wait_ge(in_rec, 80)
            for g0, g1, f in ((0, 512, GS / HS / 2), (512, 768, GS / HS), (768, 1024, GS / HS / 2)):
                i = nc.vector.tensor_scalar(w_hh32[:, :, g0:g1], w_hh32[:, :, g0:g1], f, None, ALU.mult)
            i.then_inc(L.sem, 1)
            nc.vector.tensor_scalar(w_h32, w_h32, GS / HS, None, ALU.mult).then_inc(L.sem, 1)
            nc.vector.memset(h_t[:, :, :], 0.0).then_inc(L.sem, 1)
            dve.wait_ge(*SU["act"].after("tgf"))
            nc.vector.tensor_scalar(tgf_w[:, :], tgf[:, :], 1 / WS, None, ALU.mult).then_inc(L.sem, 1)
            for n in (0, 2):
                nc.vector.tensor_scalar(v_(f"f{n}_b2", 0, E * K), v_(f"f{n}_b2", 0, E * K), WS, None,
                                        ALU.mult).then_inc(L.sem, 1)
            nc.vector.memset(ws_col[:, :], WS).then_inc(L.sem, 1)
            nc.vector.memset(eps_col[:, :], EPS).then_inc(L.sem, 1)
            nc.vector.memset(quadrant[:, :, :], 0.0).then_inc(L.sem, 1)
            dve.wait_ge(*L.after("no_quadrant"))
            for q in range(QT):
                i = nc.vector.memset(quadrant[q * 32:(q + 1) * 32, q, :], 1 / 32)
            i.then_inc(L.sem, 1)
            nc.vector.memset(s_t[:, :, :], 0.0).then_inc(L.sem, 1)

        def setup_pool(pool):
            L = SU["pool"]
            for n, src, dst in (("whh", w_hh32, whh), ("wh", w_h32, wh), ("gat", g32, gat)):
                if n == "gat":
                    pool.wait_ge(*SU["act"].after("g3"))
                else:
                    pool.wait_ge(*SU["dve"].after("half_h"))
                nc.gpsimd.tensor_copy(dst[:, 0], src).then_inc(L.sem, 1)
                pool.wait_ge(*L.after(f"{n}_hi"))
                nc.gpsimd.tensor_tensor(src, src, dst[:, 0], ALU.subtract).then_inc(L.sem, 1)
                pool.wait_ge(*L.after(f"{n}_rest"))
                nc.gpsimd.tensor_copy(dst[:, 1], src).then_inc(L.sem, 1)

        XG = [(u, g) for u in range(2) for g in range(NG)]
        XP = lines("xproj", pe=(*LN_PE, *(f"g{u}{g}" for u, g in XG)),
                   act=(*LN_ACT, *(f"{w}{u}{g}" for u, g in XG for w in ("hi", "x"))),
                   dve=(*LN_DVE, *(f"lo{u}{g}" for u, g in XG)))
        xbufs = ln_buffers(wflat[:, 2 * 2048 + 512:])

        def xproj_pe(pe):
            pe.wait_ge(in_x, 16)
            pe.wait_ge(in_small, 32)
            finished(pe, {e: SU[e] for e in ("act", "dve")})
            with pe.Fori(0, B // 2) as it:
                ln_pe(pe, XP, it, xbufs)
                for n, (u, g) in enumerate(XG):
                    if g == 0:
                        pe.wait_ge(*XP["dve"].after(f"normed{u}", it))
                    if n >= 4:
                        pe.wait_ge(*XP["act"].after("x%d%d" % XG[n - 4], it))
                    for k in range(K):
                        i = nc.tensor.matmul(bank[4 + g % 4][:, :], w_x[:, k, g * P:(g + 1) * P], xbufs[u][0][:, k, :],
                                             start=k == 0, stop=k == K - 1)
                    i.then_inc(XP["pe"].sem, 1)

        def xp_out(xp_part, u, g, it):
            return xp_part[:, SLOT[g], bass.ds(2 * it + u, 1), :].rearrange("p a s -> p (a s)")

        def xproj_act(act):
            act.wait_ge(*SU["dve"].after("done"))
            with act.Fori(0, B // 2) as it:
                ln_act(act, XP, it, xbufs)
                for n, (u, g) in enumerate(XG):
                    if n >= 2:
                        act.wait_ge(*XP["dve"].after("lo%d%d" % XG[n - 2], it))
                    act.wait_ge(*XP["pe"].after(f"g{u}{g}", it))
                    for dst in (xp_out(xp_hi, u, g, it), fo[:, g % 2, :]):
                        nc.scalar.activation(dst, bank[4 + g % 4][:, :], ACT.Identity, bias=b0[:, g:g + 1],
                                             scale=GS if g in (4, 5) else GS / 2).then_inc(XP["act"].sem, 1)

        def xproj_dve(dve):
            dve.wait_ge(in_x, 16)
            with dve.Fori(0, B // 2) as it:
                ln_dve(dve, XP, it, xbufs)
                for u, g in XG:
                    dve.wait_ge(*XP["act"].after(f"x{u}{g}", it))
                    nc.vector.tensor_tensor(xp_out(xp_lo, u, g, it), fo[:, g % 2, :], xp_out(xp_hi, u, g, it),
                                            ALU.subtract).then_inc(XP["dve"].sem, 1)

        arg = sb("arg", [P, K, B * C])
        e = sb("e", [P, K, B * C])
        negmax = sb("negmax", [P, 1])
        ex = sb("ex", [P, C])
        den = sb("den", [P, 1])
        rden = sb("rden", [P, 1])
        exT = sb("exT", [P, 2, 32])
        al32 = sb("al32", [P, 2, B])
        al = sb("al", [P, 2, 2 * B], F16)
        t_f, t_o = sb("t_f", [P, K, B]), sb("t_o", [P, K, B])
        t_ig = sb("t_ig", [P, 2 * K, B])
        o1 = sb("o1", [P, K, B])
        fc = sb("fc", [P, K, B])
        ig = sb("ig", [P, K, B])
        tc = sb("tc", [P, K, B])
        query = [bank[0], bank[1]]
        score = bank[2]
        xp_t = sb("xp_t", [P, 2, NG, B], F16)
        GATE_OUT = {g: bank[3 + u][:, j * B:(j + 1) * B] for u, gs in enumerate(GROUPS.values()) for j, g in enumerate(gs)}

        R = lines("rec", pool=("xp", "hist_h", "hist_s"), pe=("query0", "query1", "scores", "gates_f", "gates_ig", "gates_o"),
                  act=("tanh0", "tanh1", "exp", "tanh_f", "tanh_ig", "tanh_o", "tanh_c"),
                  dve=("h_hi", "h", "h_lo", "arg0", "arg1", "negmax", "exT", "rden", "al_hi", "al32", "al_lo", "fc", "ig",
                       "s", "o1"))

        R_END = line("rec_end_pool", "hist_h", "hist_s")

        def rec_finished(eng):
            eng.wait_ge(*R["pe"].before(S))
            eng.wait_ge(*R["act"].before(S))
            eng.wait_ge(*R["dve"].after("h_lo", S))
            eng.wait_ge(*R_END.after("hist_s"))

        def gate_mm(g, w, moving, k, pairs):
            for part, lo in pairs:
                i = nc.tensor.matmul(GATE_OUT[g], w[:, part, k, g * P:(g + 1) * P], moving[:, k, lo * B:(lo + 1) * B],
                                     start=False, stop=False, skip_group_check=True)
            return i

        def rec_pe(pe):
            finished(pe, {e: SU[e] for e in ("dve", "pool")})
            pe.wait_ge(*XP["act"].before(B // 2))
            pe.wait_ge(*XP["dve"].before(B // 2))
            with pe.Fori(0, S) as t:
                for lo in range(2):
                    pe.wait_ge(*R["dve"].after("h_lo" if lo else "h_hi", t))
                    for a in range(K):
                        pairs = [(k, part) for k in range(K) for part in range(2 - lo)]
                        for n, (k, part) in enumerate(pairs):
                            i = nc.tensor.matmul(query[a][:, 0:B], wh[:, part, k, a * P:(a + 1) * P],
                                                 hp[:, k, lo * B:(lo + 1) * B], start=n + lo == 0,
                                                 stop=lo == 1 and n == len(pairs) - 1, skip_group_check=True)
                        if lo:
                            i.then_inc(R["pe"].sem, 1)
                pe.wait_ge(*R["pool"].after("xp", t))
                for u, gs in enumerate(GROUPS.values()):
                    for part in range(2):
                        nc.tensor.matmul(bank[3 + u][:, 0:len(gs) * B], ident16[:, :],
                                         xp_t[:, part, SLOT[gs[0]]:SLOT[gs[-1]] + 1, :].rearrange("p g b -> p (g b)"),
                                         start=part == 0, stop=False, skip_group_check=True)

                def state_part(gs):
                    for g in gs:
                        for k in range(K):
                            gate_mm(g, whh, hp, k, ((0, 0), (1, 0), (0, 1)))

                state_part(GROUPS["f"])
                for a in range(K):
                    pe.wait_ge(*R["act"].after(f"tanh{a}", t))
                    for b in range(B):
                        i = nc.tensor.matmul(score[32 * b:32 * b + 32, 0:C], vrep[:, a, :], e[:, a, b * C:(b + 1) * C],
                                             start=a == 0, stop=a == K - 1)
                i.then_inc(R["pe"].sem, 1)
                state_part(GROUPS["ig"])
                state_part(GROUPS["o"])
                fig = ("f", "ig")
                pe.wait_ge(*R["dve"].after("al_hi", t))
                for name in fig:
                    for g in GROUPS[name]:
                        for j in range(2):
                            gate_mm(g, gat, al, j, ((0, 0), (1, 0)))
                pe.wait_ge(*R["dve"].after("al_lo", t))
                for name in fig:
                    for g in GROUPS[name]:
                        for j in range(2):
                            i = gate_mm(g, gat, al, j, ((0, 1),))
                    i.then_inc(R["pe"].sem, 1)
                for g in GROUPS["o"]:
                    for j in range(2):
                        i = gate_mm(g, gat, al, j, ((0, 0), (1, 0), (0, 1)))
                i.then_inc(R["pe"].sem, 1)

        def remember(pool, L, t):
            pool.wait_ge(*R["dve"].after("h", t))
            for hist, src in ((hist_h, h_t), (hist_s, s_t)):
                nc.gpsimd.tensor_copy(hist[:, :, :, bass.ds(t, 1)].rearrange("p k b a -> p k (b a)"),
                                      src[:, :, :]).then_inc(L.sem, 1)

        def rec_pool(pool):
            finished(pool, {"pool": SU["pool"]})
            pool.wait_ge(*XP["act"].before(B // 2))
            pool.wait_ge(*XP["dve"].before(B // 2))
            with pool.Fori(0, S) as t:
                pool.wait_ge(*R["dve"].after("h_hi", t))
                nc.gpsimd.tensor_copy(xp_t[:, :, :, :].rearrange("p u g b -> p (u g b)"),
                                      xp[:, :, bass.ds(t, 1)].rearrange("p c a -> p (c a)")).then_inc(R["pool"].sem, 1)
                remember(pool, R["pool"], t)
            remember(pool, R_END, S)

        def rec_act(act):
            nc.scalar.preload_act_table(ACT.Exp)
            with act.Fori(0, S) as t:
                for a in range(K):
                    act.wait_ge(*R["dve"].after(f"arg{a}", t))
                    nc.scalar.activation(e[:, a, :], arg[:, a, :], ACT.Tanh).then_inc(R["act"].sem, 1)
                act.wait_ge(*R["dve"].after("negmax", t))
                nc.scalar.activation(ex[:, :], score[:, 0:C], ACT.Exp, bias=negmax[:, :],
                                     accum_out=den[:, :]).then_inc(R["act"].sem, 1)
                for u, (name, dst) in enumerate((("f", t_f), ("ig", t_ig), ("o", t_o))):
                    act.wait_ge(*R["pe"].after(f"gates_{name}", t))
                    n = len(GROUPS[name])
                    nc.scalar.activation(dst[:, :, :].rearrange("p g b -> p (g b)"), bank[3 + u][:, 0:n * B], ACT.Tanh,
                                         scale=1 / GS).then_inc(R["act"].sem, 1)
                act.wait_ge(*R["dve"].after("s", t))
                nc.scalar.activation(tc[:, :, :], s_t[:, :, :], ACT.Tanh, scale=0.5).then_inc(R["act"].sem, 1)

        def rec_dve(dve):
            L = R["dve"]
            dve.wait_ge(*XP["act"].before(B // 2))
            dve.sem_inc(L.sem, 3)

            def attend(t):
                for a in range(K):
                    dve.wait_ge(*R["pe"].after(f"query{a}", t))
                    nc.vector.scalar_tensor_tensor(arg[:, a, :].rearrange("p (b n) -> p b n", b=B),
                                                   bcast(query[a][:, 0:B], C), 1 / GS,
                                                   fproj[:, a, :].rearrange("p (b n) -> p b n", b=B),
                                                   ALU.mult, ALU.add).then_inc(L.sem, 1)
                dve.wait_ge(*R["pe"].after("scores", t))
                nc.vector.tensor_reduce(negmax[:, :], score[:, 0:C], AX.X, ALU.max, negate=True).then_inc(L.sem, 1)
                dve.wait_ge(*R["act"].after("exp", t))
                nc.vector.transpose(exT[:, :, :].rearrange("p j c -> p (j c)"), ex[:, :]).then_inc(L.sem, 1)
                nc.vector.reciprocal(rden[:, :], den[:, :]).then_inc(L.sem, 1)
                dve.wait_ge(*L.after("rden", t))
                for dst in (al[:, :, 0:B], al32[:, :, :]):
                    nc.vector.scalar_tensor_tensor(dst, exT[:, :, 0:B], rden[:, 0:1], over(const("diag_b"), 2),
                                                   ALU.mult, ALU.mult).then_inc(L.sem, 1)
                dve.wait_ge(*L.after("al32", t))
                nc.vector.tensor_tensor(al[:, :, B:2 * B], al32[:, :, :], al[:, :, 0:B],
                                        ALU.subtract).then_inc(L.sem, 1)

            def cell(t):
                dve.wait_ge(*R["act"].after("tanh_f", t))
                nc.vector.scalar_tensor_tensor(fc[:, :, :], t_f[:, :, :], 1.0, s_t[:, :, :], ALU.add,
                                               ALU.mult).then_inc(L.sem, 1)
                dve.wait_ge(*R["act"].after("tanh_ig", t))
                nc.vector.scalar_tensor_tensor(ig[:, :, :], t_ig[:, 0:2, :], 1.0, t_ig[:, 2:4, :], ALU.add,
                                               ALU.mult).then_inc(L.sem, 1)
                dve.wait_ge(*R["pool"].after("hist_s", t))
                dve.wait_ge(*L.after("ig", t))
                nc.vector.scalar_tensor_tensor(s_t[:, :, :], fc[:, :, :], 0.5, ig[:, :, :], ALU.mult,
                                               ALU.add).then_inc(L.sem, 1)
                dve.wait_ge(*R["act"].after("tanh_o", t))
                nc.vector.tensor_scalar(o1[:, :, :], t_o[:, :, :], 1.0, HS / 2, ALU.add, ALU.mult).then_inc(L.sem, 1)
                dve.wait_ge(*L.after("o1", t))
                dve.wait_ge(*R["act"].after("tanh_c", t))
                for dst in (hp[:, :, 0:B], h_t[:, :, :]):
                    nc.vector.tensor_tensor(dst, o1[:, :, :], tc[:, :, :], ALU.mult).then_inc(L.sem, 1)
                dve.wait_ge(*L.after("h", t + 1))
                nc.vector.tensor_tensor(hp[:, :, B:2 * B], h_t[:, :, :], hp[:, :, 0:B],
                                        ALU.subtract).then_inc(L.sem, 1)

            attend(0)
            with dve.Fori(0, S - 1) as t:
                cell(t)
                attend(t + 1)
            cell(S - 1)

        w1s = cols(fn, 0, (K, 4 * D))
        w1b = cols(fn, 2048, (K, 4 * D))
        t2_of = [cols(bigA, 0, (NG, S)), cols(bigB, 4096, (NG, S))]
        fc2, ig2 = cols(bigA, 4096, (K, S)), cols(bigA, 5120, (K, S))
        tc2 = cols(bigA, 6144, (K, S))
        tgh = sb("tgh", [P, 1])
        L2 = lines("lstm2", pe=tuple(f"g{g}" for g in range(NG)), act=(*(f"t{g}" for g in range(NG)), "tanh_c"),
                   dve=("fc", "ig", "c", "h", "x0", "x1"))
        L2W = line("lstm2_w_dve", "sum", "half", "tgh")

        def lstm2_sp(sp):
            finished(sp, XP, B // 2)
            finished(sp, SU)
            sp.dma_start(w1s, dram["w_ih1"]).then_inc(in_l1, 16)
            sp.dma_start(w1b, dram["w_hh1"]).then_inc(in_l1, 16)

        def lstm2_pe(pe):
            pe.wait_ge(*L2W.after("half"))
            rec_finished(pe)
            with pe.Fori(0, B // 2) as it:
                for u in range(2):
                    c = 2 * it + u
                    for g in range(NG):
                        pe.wait_ge(*(L2["act"].after(f"t{g}", c - 1) if u else L2["act"].before(c)))
                        for k in range(K):
                            h = hist_h[:, k, bass.ds(c, 1), 1:S + 1].rearrange("p a s -> p (a s)")
                            i = nc.tensor.matmul(bank[g][:, :], w1s[:, k, g * P:(g + 1) * P], h,
                                                 start=k == 0, stop=k == K - 1)
                        i.then_inc(L2["pe"].sem, 1)

        def lstm2_act(act):
            rec_finished(act)
            with act.Fori(0, B // 2) as it:
                for u in range(2):
                    c = 2 * it + u
                    for g in range(NG):
                        act.wait_ge(*L2["pe"].after(f"g{g}", c))
                        nc.scalar.activation(t2_of[u][:, g, :], bank[g][:, :], ACT.Tanh, bias=b1[:, g:g + 1],
                                             scale=1.0 if g in (4, 5) else 0.5).then_inc(L2["act"].sem, 1)
                    act.wait_ge(*L2["dve"].after("c", c))
                    nc.scalar.activation(tc2, fc2, ACT.Tanh, scale=0.5).then_inc(L2["act"].sem, 1)

        def lstm2_dve(dve):
            dve.wait_ge(in_l1, 32)
            nc.vector.tensor_tensor(w1s, w1s, w1b, ALU.add).then_inc(L2W.sem, 1)
            dve.wait_ge(*L2W.after("sum"))
            nc.vector.tensor_scalar(w1s, w1s, 1 / HS, None, ALU.mult).then_inc(L2W.sem, 1)
            dve.wait_ge(*SU["act"].after("tgx"))
            nc.vector.tensor_scalar(tgh[:, :], tgx[:, 0:1], 0.5, None, ALU.mult).then_inc(L2W.sem, 1)
            rec_finished(dve)
            with dve.Fori(0, B // 2) as it:
                for u in range(2):
                    c, t2 = 2 * it + u, t2_of[u]
                    s0 = hist_s[:, :, bass.ds(c, 1), 1:S + 1].rearrange("p k a s -> p k (a s)")
                    dve.wait_ge(*L2["dve"].before(c))
                    dve.wait_ge(*L2["act"].after("t7", c))
                    nc.vector.scalar_tensor_tensor(fc2, t2[:, 2:4, :], 1.0, s0, ALU.add, ALU.mult).then_inc(L2["dve"].sem, 1)
                    nc.vector.scalar_tensor_tensor(ig2, t2[:, 0:2, :], 1.0, t2[:, 4:6, :], ALU.add,
                                                   ALU.mult).then_inc(L2["dve"].sem, 1)
                    dve.wait_ge(*L2["dve"].after("ig", c))
                    nc.vector.scalar_tensor_tensor(fc2, fc2, 0.5, ig2, ALU.mult, ALU.add).then_inc(L2["dve"].sem, 1)
                    dve.wait_ge(*L2["act"].after("tanh_c", c))
                    nc.vector.scalar_tensor_tensor(ig2, t2[:, 6:8, :], 1.0, tc2, ALU.add, ALU.mult).then_inc(L2["dve"].sem, 1)
                    dve.wait_ge(*L2["dve"].after("h", c))
                    for k in range(K):
                        xs = xT[:, k, bass.ds(c * S, S)]
                        nc.vector.scalar_tensor_tensor(xs, ig2[:, k, :], tgh[:, 0:1], xs, ALU.mult,
                                                       ALU.add).then_inc(L2["dve"].sem, 1)

        wr = sb("wr", [P, K, E])
        T = N // P
        lg = sb("lg", [P, T, E])
        gates = sb("gates", [P, T, E])
        rank = sb("rank", [P, T, E])
        m0, m1 = sb("m0", [P, T, E]), sb("m1", [P, T, E])
        r0, r1 = sb("r0", [P, T]), sb("r1", [P, T])
        in_wr, in_w, in_gate, out_gate = sem("in_wr"), [sem("in_w0"), sem("in_w1")], [sem("in_gate0"), sem("in_gate1")], \
            sem("out_gate")
        gate_dram = [nc.dram_tensor(f"gates_of_layer{i}", (E, N), F32, kind="Internal").ap() for i in range(3)]
        n16 = [cols(fn, u * N, (K, N), F16) for u in range(2)]
        silu = cols(bigA, 2048, (FW1 // P, S))
        gate_bc = [bigA[:, 4096:6144], bigA[:, 6144:8192]]
        gT = bigB[0:E, 4096:4096 + N]
        pair0, pair1 = cols(bigA, 2048, (T, E * E)), cols(bigA, 3072, (T, E * E))

        RANKED = ("gt", "equal", "tie", "pairs", "rank")
        SOFTMAX = ("max", "shift", "sum", "rsum", "probs")
        BEST2 = ("first", "second", "p1", "p2", "s1", "s2")
        ROUTE = [(*SOFTMAX, *RANKED, *BEST2, "s12", "rs12", "share", "gates"),
                 (*RANKED, *BEST2, "diff", "denom", "w1", "w2", "g1", "g2", "gates"),
                 (*SOFTMAX, *RANKED, "cum_in", "cum", "low", "first", "keep", "gates")]

        def expert_layer(n, prev, prev_iters):
            F = FW1 if n == 1 else FW
            FT = F // P
            LR = lines(f"ln{n}", pe=(*LN_PE, "logits0", "logits1"), act=(*LN_ACT, "n_hi0", "n_hi1"),
                       dve=(*LN_DVE, "n_lo0", "logits0", "n_lo1", "logits1"))
            RT = lines(f"route{n}", pe=("gT0", "gT1", "gT2", "gT3"), act=("exp", "gT0", "gT1", "gT2", "gT3"),
                       dve=ROUTE[n])
            X = f"experts{n}"
            XL = dict(up=line(f"{X}_up_pe", *(f"{u}{f}" for f in range(FT) for u in (("gate", "up") if n == 1 else ("up",)))),
                      out=line(f"{X}_out_pe", "out0", "out1"),
                      act=line(f"{X}_act", *(f"{u}{f}" for f in range(FT) for u in (("silu",) if n == 1 else ("hi", "h")))),
                      hid=line(f"{X}_hid_dve", *(f"{u}{f}" for f in range(FT)
                                                 for u in (("h", "hi", "lo") if n == 1 else ("lo",)))),
                      gated=line(f"{X}_gated_dve", "gated0", "gated1"), add=line(f"{X}_add_dve", "x0", "x1"))
            SPLIT = line(f"{X}_split_pool", "hi", "scaled", "lo")
            names = ("f1_w1", "f1_w3", "f1_w2") if n == 1 else (f"f{n}_w1", f"f{n}_w2")
            w_base = 16 * (E // 2) * sum(3 if i == 1 else 2 for i in range(n))
            g_base = 16 * (E // 2) * n

            hid16 = cols(bigA, 0, (2, FT, S), F16)
            WN = (3 if n == 1 else 2) * K * F
            w16 = [cols(t, 0, (2, WN), F16) for t in (fh, fs)]

            def weights(o):
                up = [o[:, m * K * F:(m + 1) * K * F].rearrange("p (k f) -> p k f", k=K) for m in range(WN // (K * F) - 1)]
                d = o[:, WN - FT * D:WN].rearrange("p (f d) -> p f d", f=FT)
                return [*up, d]

            def load_weights(sp, e, half):
                for dst, nm in zip(weights(wbuf[:, half, :]), names):
                    sp.dma_start(dst, dram[nm][bass.ds(e, 1)].rearrange("a p k f -> p (a k) f")).then_inc(in_w[half], 16)

            def load_gates(sp, e, half):
                sp.dma_start(gate_bc[half], gate_dram[n][bass.ds(e, 1), :].to_broadcast([P, N])).then_inc(in_gate[half], 16)

            rbufs = ln_buffers(bigA)

            def n16_of(part, it, u):
                return n16[part][:, :, bass.ds((2 * it + u) * S, S)]

            def route_sp(sp):
                finished(sp, prev, prev_iters)
                sp.dma_start(wr[:, :, :], dram[f"f{n}_wr"]).then_inc(in_wr, 16)
                for half in range(2):
                    load_weights(sp, half, half)
                sp.wait_ge(*RT["act"].after("gT3"))
                sp.dma_start(gate_dram[n], gT).then_inc(out_gate, 16)
                sp.wait_ge(out_gate, 16 * (n + 1))
                for half in range(2):
                    load_gates(sp, half, half)

            def experts_sp(sp):
                with sp.Fori(1, E // 2) as ep:
                    for half in range(2):
                        e = ep * 2 + half
                        sp.wait_ge(*SPLIT.before(e - 1))
                        load_weights(sp, e, half)
                        sp.wait_ge(*XL["gated"].before((e - 1) * B))
                        load_gates(sp, e, half)

            def experts_pool(pool):
                finished(pool, prev, prev_iters)

                def split(ep, half):
                    pool.wait_ge(in_w[half], (ep + 1) * 16 * len(names) + w_base)
                    w32, hi, lo = wbuf[:, half, 0:WN], w16[half][:, 0, :], w16[half][:, 1, :]
                    ws = ws_col[:, :].to_broadcast([P, WN])
                    nc.gpsimd.tensor_tensor(hi, w32, ws, ALU.mult).then_inc(SPLIT.sem, 1)
                    nc.gpsimd.tensor_tensor(w32, w32, ws, ALU.mult).then_inc(SPLIT.sem, 1)
                    pool.wait_ge(*SPLIT.after("scaled", ep * 2 + half))
                    nc.gpsimd.tensor_tensor(lo, w32, hi, ALU.subtract).then_inc(SPLIT.sem, 1)

                for half in range(2):
                    split(0, half)
                with pool.Fori(1, E // 2) as ep:
                    for half in range(2):
                        pool.wait_ge(*XL["out"].before((ep * 2 + half - 1) * B))
                        split(ep, half)

            def route_pe(pe):
                finished(pe, prev, prev_iters)
                pe.wait_ge(in_wr, 16 * (n + 1))
                with pe.Fori(0, B // 2) as it:
                    ln_pe(pe, LR, it, rbufs)
                    for u, (n32, _, _) in enumerate(rbufs):
                        pe.wait_ge(*LR["dve"].after(f"normed{u}", it))
                        for q in range(QT):
                            for k in range(K):
                                i = nc.tensor.matmul(bank[4 + u][:, q * E:(q + 1) * E], n32[:, k, q * P:(q + 1) * P], wr[:, k, :],
                                                     start=k == 0, stop=k == K - 1)
                        i.then_inc(LR["pe"].sem, 1)

            def route_act(act):
                finished(act, prev, prev_iters)
                with act.Fori(0, B // 2) as it:
                    ln_act(act, LR, it, rbufs)
                    for u, (n32, _, _) in enumerate(rbufs):
                        act.wait_ge(*LR["dve"].after(f"normed{u}", it))
                        nc.scalar.activation(n16_of(0, it, u), n32, ACT.Copy).then_inc(LR["act"].sem, 1)
                if n == 1:
                    act.wait_ge(*RT["dve"].after("diff"))
                    i = nc.scalar.activation(r1[:, :], r1[:, :], ACT.Exp)
                else:
                    act.wait_ge(*RT["dve"].after("shift"))
                    i = nc.scalar.activation(gates[:, :, :], lg[:, :, :], ACT.Exp)
                i.then_inc(RT["act"].sem, 1)
                for b in range(B):
                    act.wait_ge(*RT["pe"].after(f"gT{b}"))
                    nc.scalar.activation(gT[:, b * S:(b + 1) * S], bank[4 + b][0:E, :], ACT.Copy).then_inc(RT["act"].sem, 1)

            def route_dve(dve):
                finished(dve, prev, prev_iters)
                with dve.Fori(0, B // 2) as it:
                    ln_dve(dve, LR, it, rbufs)
                    for u, (n32, _, _) in enumerate(rbufs):
                        dve.wait_ge(*LR["act"].after(f"n_hi{u}", it))
                        nc.vector.tensor_tensor(n16_of(1, it, u), n32, n16_of(0, it, u), ALU.subtract).then_inc(LR["dve"].sem, 1)
                        dve.wait_ge(*LR["pe"].after(f"logits{u}", it))
                        dst = lg[:, bass.ds((2 * it + u) * QT, QT), :]
                        src = bank[4 + u][:, 0:QT * E].rearrange("p (q e) -> p q e", e=E)
                        if n == 1:
                            i = nc.vector.tensor_copy(dst, src)
                        else:
                            i = nc.vector.tensor_tensor(dst, src, over(v_(f"f{n}_br", 0, E), QT), ALU.add)
                        i.then_inc(LR["dve"].sem, 1)
                dve.wait_ge(*LR["dve"].before(B // 2))
                L = RT["dve"]
                rank_by = lg
                if n != 1:
                    nc.vector.tensor_reduce(r0[:, :], lg[:, :, :], AX.X, ALU.max).then_inc(L.sem, 1)
                    dve.wait_ge(*L.after("max"))
                    nc.vector.tensor_tensor(lg[:, :, :], lg[:, :, :], bcast(r0[:, :], E), ALU.subtract).then_inc(L.sem, 1)
                    dve.wait_ge(*RT["act"].after("exp"))
                    nc.vector.tensor_reduce(r0[:, :], gates[:, :, :], AX.X, ALU.add).then_inc(L.sem, 1)
                    dve.wait_ge(*L.after("sum"))
                    nc.vector.reciprocal(r0[:, :], r0[:, :]).then_inc(L.sem, 1)
                    dve.wait_ge(*L.after("rsum"))
                    nc.vector.tensor_tensor(gates[:, :, :], gates[:, :, :], bcast(r0[:, :], E), ALU.mult).then_inc(L.sem, 1)
                    dve.wait_ge(*L.after("probs"))
                    rank_by = gates
                e_of = rank_by[:, :, :].unsqueeze(3).to_broadcast([P, T, E, E])
                j_of = rank_by[:, :, :].unsqueeze(2).to_broadcast([P, T, E, E])
                p0 = pair0.rearrange("p t (e j) -> p t e j", e=E)
                p1 = pair1.rearrange("p t (e j) -> p t e j", e=E)
                nc.vector.tensor_tensor(p0, j_of, e_of, ALU.is_gt).then_inc(L.sem, 1)
                nc.vector.tensor_tensor(p1, j_of, e_of, ALU.is_equal).then_inc(L.sem, 1)
                dve.wait_ge(*L.after("equal"))
                nc.vector.tensor_tensor(pair1, pair1, over(const("upto" if n == 2 else "before"), T),
                                        ALU.mult).then_inc(L.sem, 1)
                dve.wait_ge(*L.after("tie"))
                nc.vector.tensor_tensor(pair0, pair0, pair1, ALU.add).then_inc(L.sem, 1)
                dve.wait_ge(*L.after("pairs"))
                nc.vector.tensor_reduce(rank[:, :, :], p0, AX.X, ALU.add).then_inc(L.sem, 1)
                dve.wait_ge(*L.after("rank"))
                if n == 2:
                    nc.vector.tensor_tensor(p0, p0, j_of, ALU.mult).then_inc(L.sem, 1)
                    dve.wait_ge(*L.after("cum_in"))
                    nc.vector.tensor_reduce(m0[:, :, :], p0, AX.X, ALU.add).then_inc(L.sem, 1)
                    dve.wait_ge(*L.after("cum"))
                    nc.vector.tensor_scalar(m0[:, :, :], m0[:, :, :], 0.8, None, ALU.is_lt).then_inc(L.sem, 1)
                    nc.vector.tensor_scalar(m1[:, :, :], rank[:, :, :], 1.5, None, ALU.is_lt).then_inc(L.sem, 1)
                    dve.wait_ge(*L.after("first"))
                    nc.vector.tensor_tensor(m0[:, :, :], m0[:, :, :], m1[:, :, :], ALU.max).then_inc(L.sem, 1)
                    dve.wait_ge(*L.after("keep"))
                    nc.vector.tensor_tensor(gates[:, :, :], gates[:, :, :], m0[:, :, :], ALU.mult).then_inc(L.sem, 1)
                    return
                nc.vector.tensor_scalar(m0[:, :, :], rank[:, :, :], 0.0, None, ALU.is_equal).then_inc(L.sem, 1)
                nc.vector.tensor_scalar(m1[:, :, :], rank[:, :, :], 1.0, None, ALU.is_equal).then_inc(L.sem, 1)
                dve.wait_ge(*L.after("second"))
                nc.vector.tensor_tensor(pair0[:, :, 0:E], rank_by[:, :, :], m0[:, :, :], ALU.mult).then_inc(L.sem, 1)
                nc.vector.tensor_tensor(pair1[:, :, 0:E], rank_by[:, :, :], m1[:, :, :], ALU.mult).then_inc(L.sem, 1)
                dve.wait_ge(*L.after("p2"))
                nc.vector.tensor_reduce(r0[:, :], pair0[:, :, 0:E], AX.X, ALU.add).then_inc(L.sem, 1)
                nc.vector.tensor_reduce(r1[:, :], pair1[:, :, 0:E], AX.X, ALU.add).then_inc(L.sem, 1)
                dve.wait_ge(*L.after("s2"))
                if n == 0:
                    nc.vector.tensor_tensor(r1[:, :], r0[:, :], r1[:, :], ALU.add).then_inc(L.sem, 1)
                    dve.wait_ge(*L.after("s12"))
                    nc.vector.reciprocal(r1[:, :], r1[:, :]).then_inc(L.sem, 1)
                    dve.wait_ge(*L.after("rs12"))
                    nc.vector.tensor_tensor(r0[:, :], r0[:, :], r1[:, :], ALU.mult).then_inc(L.sem, 1)
                    dve.wait_ge(*L.after("share"))
                    nc.vector.tensor_tensor(gates[:, :, :], m0[:, :, :], bcast(r0[:, :], E), ALU.mult).then_inc(L.sem, 1)
                    return
                nc.vector.tensor_tensor(r1[:, :], r1[:, :], r0[:, :], ALU.subtract).then_inc(L.sem, 1)
                dve.wait_ge(*RT["act"].after("exp"))
                nc.vector.tensor_scalar(r0[:, :], r1[:, :], 1.0, None, ALU.add).then_inc(L.sem, 1)
                dve.wait_ge(*L.after("denom"))
                nc.vector.reciprocal(r0[:, :], r0[:, :]).then_inc(L.sem, 1)
                dve.wait_ge(*L.after("w1"))
                nc.vector.tensor_tensor(r1[:, :], r1[:, :], r0[:, :], ALU.mult).then_inc(L.sem, 1)
                dve.wait_ge(*L.after("w2"))
                nc.vector.tensor_tensor(m0[:, :, :], m0[:, :, :], bcast(r0[:, :], E), ALU.mult).then_inc(L.sem, 1)
                nc.vector.tensor_tensor(m1[:, :, :], m1[:, :, :], bcast(r1[:, :], E), ALU.mult).then_inc(L.sem, 1)
                dve.wait_ge(*L.after("g2"))
                nc.vector.tensor_tensor(gates[:, :, :], m0[:, :, :], m1[:, :, :], ALU.add).then_inc(L.sem, 1)

            PARTS = ((0, 0), (1, 0), (0, 1))
            UP_BANKS = 2 if n == 1 else 4

            def experts_pe(pe):
                pe.wait_ge(*LR["dve"].before(B // 2))
                w = [[weights(w16[half][:, part, :]) for part in range(2)] for half in range(2)]

                def up(f, half, c):
                    for m in range(len(w[half][0]) - 1):
                        pairs = [(k, *p) for k in range(K) for p in PARTS]
                        for j, (k, wp, np_) in enumerate(pairs):
                            i = nc.tensor.matmul(bank[m * UP_BANKS + f % UP_BANKS][:, :], w[half][wp][m][:, k, f * P:(f + 1) * P],
                                                 n16[np_][:, k, bass.ds(c * S, S)], start=j == 0, stop=j == len(pairs) - 1)
                        i.then_inc(XL["up"].sem, 1)

                def down(f, half, it):
                    if f == 0:
                        pe.wait_ge(*XL["gated"].before(it))
                    pe.wait_ge(*XL["hid"].after(f"lo{f}", it))
                    for h in range(K):
                        for wp, hp_ in PARTS:
                            i = nc.tensor.matmul(bank[6 + h][:, :], w[half][wp][-1][:, f, h * P:(h + 1) * P], hid16[:, hp_, f, :],
                                                 start=f == 0 and wp + hp_ == 0, stop=f == FT - 1 and hp_ == 1)
                        if f == FT - 1:
                            i.then_inc(XL["out"].sem, 1)

                def chunk(it, half, c, next_half, next_c):
                    for f in range(2, FT + 2):
                        if n == 1:
                            pe.wait_ge(*XL["hid"].after(f"hi{f - 2}", it))
                        if f < FT:
                            up(f, half, c)
                        elif next_half is not None:
                            up(f - FT, next_half, next_c)
                        down(f - 2, half, it)

                def pair(ep, last):
                    for half in range(2):
                        e = ep * 2 + half
                        with pe.Fori(0, B - 1) as c:
                            chunk(e * B + c, half, c, half, c + 1)
                        if last and half == 1:
                            chunk(e * B + B - 1, half, B - 1, None, None)
                        else:
                            pe.wait_ge(*SPLIT.after("lo", e + 1))
                            chunk(e * B + B - 1, half, B - 1, 1 - half, 0)

                pe.wait_ge(*SPLIT.after("lo", 0))
                for f in range(2):
                    up(f, 0, 0)
                pe.wait_ge(*RT["dve"].after("gates"))
                for b in range(B):
                    for q in range(QT):
                        i = nc.tensor.transpose(bank[4 + b][0:E, q * P:(q + 1) * P], gates[:, b * QT + q, :], ident)
                    i.then_inc(RT["pe"].sem, 1)
                pe.wait_ge(*RT["act"].after("gT3"))
                with pe.Fori(0, E // 2 - 1) as ep:
                    pair(ep, False)
                pair(E // 2 - 1, True)

            def experts_act(act):
                nc.scalar.preload_act_table((ACT.Gelu, ACT.Silu, ACT.Relu)[n])
                act.wait_ge(*RT["dve"].before(1))
                with act.Fori(0, E) as ex_:
                    with act.Fori(0, B) as c:
                        it = ex_ * B + c
                        for f in range(FT):
                            ps = bank[f % UP_BANKS][:, :]
                            if n == 1:
                                act.wait_ge(*XL["up"].after(f"gate{f}", it))
                                nc.scalar.activation(silu[:, f, :], ps, ACT.Silu, scale=1 / WS).then_inc(XL["act"].sem, 1)
                                continue
                            act.wait_ge(*(XL["hid"].after(f"lo{f - 2}", it) if f >= 2 else XL["hid"].before(it)))
                            act.wait_ge(*XL["up"].after(f"up{f}", it))
                            func, col = ACT.Gelu if n == 0 else ACT.Relu, VCOL[f"f{n}_b1"] + f
                            b = vec[:, bass.ds(ex_ * FT + col, 1)]
                            for dst in (hid16[:, 0, f, :], sq[:, f % 2, :]):
                                nc.scalar.activation(dst, ps, func, bias=b, scale=1 / WS).then_inc(XL["act"].sem, 1)

            def experts_dve(dve):
                def low(f, it):
                    hi, lo, h = hid16[:, 0, f, :], hid16[:, 1, f, :], sq[:, f % 2, :]
                    if n == 1:
                        dve.wait_ge(*XL["act"].after(f"silu{f}", it))
                        dve.wait_ge(*XL["up"].after(f"up{f}", it))
                        for dst in (h, hi):
                            nc.vector.scalar_tensor_tensor(dst, bank[UP_BANKS + f % UP_BANKS][:, :], 1 / WS, silu[:, f, :],
                                                           ALU.mult, ALU.mult).then_inc(XL["hid"].sem, 1)
                        dve.wait_ge(*XL["hid"].after(f"hi{f}", it))
                    else:
                        dve.wait_ge(*XL["act"].after(f"h{f}", it))
                    nc.vector.tensor_tensor(lo, h, hi, ALU.subtract).then_inc(XL["hid"].sem, 1)

                def gated(ep, half, c):
                    dve.wait_ge(in_gate[half], (ep + 1) * 16 + g_base)
                    ex_ = ep * 2 + half
                    it = ex_ * B + c
                    g = gate_bc[half][:, bass.ds(c * S, S)]
                    for h in range(K):
                        dve.wait_ge(*XL["out"].after(f"out{h}", it))
                        if n == 1:
                            i = nc.vector.tensor_tensor(fo[:, h, :], bank[6 + h][:, :], g, ALU.mult)
                        else:
                            col = VCOL[f"f{n}_b2"] + h
                            i = nc.vector.scalar_tensor_tensor(fo[:, h, :], bank[6 + h][:, :],
                                                               vec[:, bass.ds(ex_ * K + col, 1)], g, ALU.add, ALU.mult)
                        i.then_inc(XL["gated"].sem, 1)

                def add(c, it):
                    for h in range(K):
                        dve.wait_ge(*XL["gated"].after(f"gated{h}", it))
                        xs = xT[:, h, bass.ds(c * S, S)]
                        nc.vector.scalar_tensor_tensor(xs, fo[:, h, :], tgf_w[:, n:n + 1], xs, ALU.mult,
                                                       ALU.add).then_inc(XL["add"].sem, 1)

                def chunk(ep, half, c, last):
                    it = (ep * 2 + half) * B + c
                    for f in range(2, FT):
                        low(f, it)
                    if not last:
                        low(0, it + 1)
                    gated(ep, half, c)
                    if not last:
                        low(1, it + 1)
                    add(c, it)

                for f in range(2):
                    low(f, 0)
                with dve.Fori(0, E // 2 - 1) as ep:
                    for half in range(2):
                        with dve.Fori(0, B) as c:
                            chunk(ep, half, c, False)
                with dve.Fori(0, B) as c:
                    chunk(E // 2 - 1, 0, c, False)
                with dve.Fori(0, B - 1) as c:
                    chunk(E // 2 - 1, 1, c, False)
                chunk(E // 2 - 1, 1, B - 1, True)

            return XL, route_sp, experts_sp, route_pe, experts_pe, route_act, experts_act, route_dve, experts_dve, experts_pool

        F0, f0_route_sp, f0_sp, f0_route_pe, f0_pe, f0_route_act, f0_act, f0_route_dve, f0_dve, f0_pool = expert_layer(0, L2, B)

        in_x1 = sem("in_x1")
        w_x1 = cols(bigB, 0, (6, K, D))
        WQC, WKS, WVS, WQS, WKC, WVC = range(6)
        w_g = cols(bigB, 3072, (2 * K, D))
        ctxb = sb("ctxb", [P, K, 2 * C])
        qcT, kcT = cols(bigA, 0, (K, S)), cols(bigA, 1024, (K, S))
        c2s, s2c = cols(bigA, 2048, (K, S)), cols(bigA, 3072, (K, S))
        vc = cols(bigA, 4096, (QT, D))
        gate1, mix = cols(bigA, 5120, (K, S)), cols(bigA, 6144, (K, S))
        ksT, qsT = cols(fh, 0, (K, C)), cols(fh, 128, (K, C))
        vs = fh[0:C, 256:512]
        s1 = cols(fh, 512, (QT, C))
        s2 = fh[0:C, 1024:1536]
        s1T = fh[0:C, 1536:2048]
        s2T = cols(fh, 2048, (QT, C))
        s2o = fh[0:C, 2304:2560]
        mx1, sum1 = sb("mx1", [P, QT]), sb("sum1", [P, QT])
        mx2, sum2 = sb("mx2", [P, 1]), sb("sum2", [P, 1])
        bgh = sb("bgh", [P, K])
        tg1h = sb("tg1h", [P, 1])
        SC1 = 1.0 / 16.0
        X1 = lines("x1", pe=("ks", "qs", "vs", "qc0", "qc1", "kc0", "kc1", "s1", "s2", "vc", "s1T", "s2T",
                             "c2s0", "c2s1", "s2o", "s2c0", "s2c1", "gate0", "gate1"),
                   act=("ctxb", "nb", "ks", "qs", "vs", "qc0", "qc1", "kc0", "kc1", "e1", "e2", "vc", "c2s0", "c2s1",
                        "s2c0", "s2c1", "gate0", "gate1"),
                   dve=("mx1", "mx2", "nmx2", "shift1", "sum1", "rsum1", "p1", "rsum2", "p2", "s1T", "s2T",
                        "s2o", "diff", "prod", "mix", "x0", "x1"))
        LN1 = ln_lines("x1_ln")
        abufs = ln_buffers(bigA)
        X1C = line("x1_consts_dve", "bgh", "tg1h")

        def ln_all(eng, L, part, *dst):
            with eng.Fori(0, B // 2) as it:
                part(eng, L, it, abufs, *dst)
            finished(eng, L, B // 2)

        def x1_load(sp):
            sp.wait_ge(*R["dve"].after("h_lo", S))
            sp.dma_start(w_x1.rearrange("p w k d -> p (w k d)"), dram["x1_w"]).then_inc(in_x1, 16)
            sp.dma_start(w_g, dram["x1_wg"]).then_inc(in_x1, 16)

        def x1_pe(pe):
            finished(pe, F0, E * B)
            ln_all(pe, LN1, ln_pe)
            pe.wait_ge(in_x1, 32)
            L = X1["pe"]

            def proj(dst, w, o, rhs):
                for k in range(K):
                    i = nc.tensor.matmul(dst, w_x1[:, w, k, o * P:(o + 1) * P], rhs[k], start=k == 0, stop=k == K - 1)
                return i

            with pe.Fori(0, B) as c:
                pe.wait_ge(*X1["act"].after("ctxb", c))
                cx = [ctxb[:, k, 0:C] for k in range(K)]
                for o in range(K):
                    i = proj(bank[2][:, o * C:(o + 1) * C], WKS, o, cx)
                i.then_inc(L.sem, 1)
                for o in range(K):
                    i = proj(bank[3][:, o * C:(o + 1) * C], WQS, o, cx)
                i.then_inc(L.sem, 1)
                for k in range(K):
                    i = nc.tensor.matmul(bank[4][0:C, 0:D], cx[k], w_x1[:, WVS, k, :], start=k == 0, stop=k == K - 1)
                i.then_inc(L.sem, 1)
                nbk = [nT[:, k, bass.ds(c * S, S)] for k in range(K)]
                proj(bank[5][:, :], WQC, 0, nbk).then_inc(L.sem, 1)
                proj(bank[6][:, :], WQC, 1, nbk).then_inc(L.sem, 1)
                proj(bank[7][:, :], WKC, 0, nbk).then_inc(L.sem, 1)
                proj(bank[0][:, :], WKC, 1, nbk).then_inc(L.sem, 1)
                pe.wait_ge(*X1["act"].after("qc1", c))

                def values(q):
                    for k in range(K):
                        i = nc.tensor.matmul(bank[2 + q // 2][:, q % 2 * D:q % 2 * D + D], nb[:, k, q * P:(q + 1) * P],
                                             w_x1[:, WVC, k, :], start=k == 0, stop=k == K - 1)
                    return i

                for q in range(QT):
                    for o in range(K):
                        i = nc.tensor.matmul(bank[1][:, q * C:(q + 1) * C], qcT[:, o, q * P:(q + 1) * P], ksT[:, o, :],
                                             start=o == 0, stop=o == K - 1)
                i.then_inc(L.sem, 1)
                for q in range(QT // 2):
                    values(q)
                pe.wait_ge(*X1["act"].after("kc1", c))
                for o in range(K):
                    i = nc.tensor.matmul(bank[4][0:C, :], qsT[:, o, :], kcT[:, o, :], start=o == 0, stop=o == K - 1)
                i.then_inc(L.sem, 1)
                for q in range(QT // 2, QT):
                    i = values(q)
                i.then_inc(L.sem, 1)
                pe.wait_ge(*X1["dve"].after("p1", c))
                for q in range(QT):
                    i = nc.tensor.matmul(bank[5][0:C, q * P:(q + 1) * P], s1[:, q, :], ident, start=True, stop=True)
                i.then_inc(L.sem, 1)
                pe.wait_ge(*X1["dve"].after("p2", c))
                for q in range(QT):
                    i = nc.tensor.matmul(bank[6][:, q * C:(q + 1) * C], s2[:, q * P:(q + 1) * P], ident[0:C, 0:C],
                                         start=True, stop=True)
                i.then_inc(L.sem, 1)
                pe.wait_ge(*X1["dve"].after("s1T", c))
                for o in range(K):
                    nc.tensor.matmul(bank[7 * (1 - o)][:, :], vs[:, o * P:(o + 1) * P], s1T, start=True,
                                     stop=True).then_inc(L.sem, 1)
                pe.wait_ge(*X1["dve"].after("s2T", c))
                pe.wait_ge(*X1["act"].after("vc", c))
                for q in range(QT):
                    i = nc.tensor.matmul(bank[2][0:C, 0:D], s2T[:, q, :], vc[:, q, :], start=q == 0, stop=q == QT - 1)
                i.then_inc(L.sem, 1)

                def gate(o, m, r):
                    return nc.tensor.matmul(bank[5 + o][:, :], w_g[:, m, o * P:(o + 1) * P], r, start=m == 0,
                                            stop=m == 2 * K - 1)

                pe.wait_ge(*X1["act"].after("c2s1", c))
                for o in range(K):
                    for m in range(K):
                        gate(o, m, c2s[:, m, :])
                pe.wait_ge(*X1["dve"].after("s2o", c))
                for o in range(K):
                    nc.tensor.matmul(bank[3 + o][:, :], s2o[:, o * P:(o + 1) * P], const("interp")[0:C, :], start=True,
                                     stop=True).then_inc(L.sem, 1)
                pe.wait_ge(*X1["act"].after("s2c1", c))
                for o in range(K):
                    for m in range(K):
                        i = gate(o, K + m, s2c[:, m, :])
                    i.then_inc(L.sem, 1)

        def x1_act(act):
            L = X1["act"]
            finished(act, F0, E * B)
            act.wait_ge(*X1C.before(1))
            ln_all(act, LN1, ln_act)
            with act.Fori(0, B) as c:
                nc.scalar.activation(ctxb[:, :, 0:C], ctxT[:, :, bass.ds(c * C, C)], ACT.Copy).then_inc(L.sem, 1)
                nc.scalar.activation(nb[:, :, :], normed(c), ACT.Copy).then_inc(L.sem, 1)

                def evac(dst, ps, step, bias, scale=1.0, func=ACT.Identity):
                    act.wait_ge(*X1["pe"].after(step, c))
                    nc.scalar.activation(dst, ps, func, bias=bias, scale=scale).then_inc(L.sem, 1)

                def evac2(dst, b, step, bias):
                    act.wait_ge(*X1["pe"].after(step, c))
                    for o in range(K):
                        i = nc.scalar.activation(dst[:, o, :], bank[b][:, o * C:(o + 1) * C], ACT.Identity, bias=v_(bias, o))
                    i.then_inc(L.sem, 1)

                evac2(ksT, 2, "ks", "bk_s")
                evac2(qsT, 3, "qs", "bq_s")
                act.wait_ge(*X1["pe"].after("vs", c))
                nc.scalar.activation(vs, bank[4][0:C, 0:D], ACT.Copy).then_inc(L.sem, 1)
                evac(qcT[:, 0, :], bank[5][:, :], "qc0", v_("bq_c", 0))
                evac(qcT[:, 1, :], bank[6][:, :], "qc1", v_("bq_c", 1))
                evac(kcT[:, 0, :], bank[7][:, :], "kc0", v_("bk_c", 0))
                evac(kcT[:, 1, :], bank[0][:, :], "kc1", v_("bk_c", 1))
                act.wait_ge(*X1["dve"].after("shift1", c))
                nc.scalar.activation(s1, s1, ACT.Exp, scale=SC1).then_inc(L.sem, 1)
                act.wait_ge(*X1["dve"].after("nmx2", c))
                nc.scalar.activation(s2, bank[4][0:C, :], ACT.Exp, scale=SC1, bias=mx2[0:C, :],
                                     accum_out=sum2[0:C, :]).then_inc(L.sem, 1)
                act.wait_ge(*X1["pe"].after("vc", c))
                for u in range(2):
                    i = nc.scalar.activation(vc[:, 2 * u:2 * u + 2, :].rearrange("p q d -> p (q d)"), bank[2 + u][:, :],
                                             ACT.Copy)
                i.then_inc(L.sem, 1)
                evac(c2s[:, 0, :], bank[7][:, :], "c2s0", v_("bv_s", 0))
                evac(c2s[:, 1, :], bank[0][:, :], "c2s1", v_("bv_s", 1))
                evac(s2c[:, 0, :], bank[3][:, :], "s2c0", v_("bv_c", 0))
                evac(s2c[:, 1, :], bank[4][:, :], "s2c1", v_("bv_c", 1))
                evac(gate1[:, 0, :], bank[5][:, :], "gate0", bgh[:, 0:1], 0.5, ACT.Tanh)
                evac(gate1[:, 1, :], bank[6][:, :], "gate1", bgh[:, 1:2], 0.5, ACT.Tanh)

        def x1_dve(dve):
            L = X1["dve"]
            finished(dve, F0, E * B)
            nc.vector.tensor_scalar(bgh[:, :], v_("bg", 0, K), 0.5, None, ALU.mult).then_inc(X1C.sem, 1)
            nc.vector.tensor_scalar(tg1h[:, :], tgx[:, 1:2], 0.5, None, ALU.mult).then_inc(X1C.sem, 1)
            ln_all(dve, LN1, ln_dve, normed)
            with dve.Fori(0, B) as c:
                dve.wait_ge(*X1["pe"].after("s1", c))
                sc = bank[1][:, 0:QT * C].rearrange("p (q n) -> p q n", q=QT)
                nc.vector.tensor_reduce(mx1[:, :], sc, AX.X, ALU.max).then_inc(L.sem, 1)
                dve.wait_ge(*X1["pe"].after("s2", c))
                nc.vector.tensor_reduce(mx2[0:C, :], bank[4][0:C, :], AX.X, ALU.max).then_inc(L.sem, 1)
                dve.wait_ge(*L.after("mx2", c))
                nc.vector.tensor_scalar(mx2[0:C, :], mx2[0:C, :], -SC1, None, ALU.mult).then_inc(L.sem, 1)
                nc.vector.tensor_tensor(s1, sc, bcast(mx1[:, :], C), ALU.subtract).then_inc(L.sem, 1)
                dve.wait_ge(*X1["act"].after("e1", c))
                nc.vector.tensor_reduce(sum1[:, :], s1, AX.X, ALU.add).then_inc(L.sem, 1)
                dve.wait_ge(*L.after("sum1", c))
                nc.vector.reciprocal(sum1[:, :], sum1[:, :]).then_inc(L.sem, 1)
                dve.wait_ge(*L.after("rsum1", c))
                nc.vector.tensor_tensor(s1, s1, bcast(sum1[:, :], C), ALU.mult).then_inc(L.sem, 1)
                dve.wait_ge(*X1["act"].after("e2", c))
                nc.vector.reciprocal(sum2[0:C, :], sum2[0:C, :]).then_inc(L.sem, 1)
                dve.wait_ge(*L.after("rsum2", c))
                nc.vector.tensor_scalar(s2, s2, sum2[0:C, 0:1], None, ALU.mult).then_inc(L.sem, 1)
                dve.wait_ge(*X1["pe"].after("s1T", c))
                nc.vector.tensor_copy(s1T, bank[5][0:C, :]).then_inc(L.sem, 1)
                dve.wait_ge(*X1["pe"].after("s2T", c))
                nc.vector.tensor_copy(s2T, bank[6][:, 0:QT * C].rearrange("p (q n) -> p q n", q=QT)).then_inc(L.sem, 1)
                dve.wait_ge(*X1["pe"].after("s2o", c))
                nc.vector.tensor_copy(s2o, bank[2][0:C, 0:D]).then_inc(L.sem, 1)
                dve.wait_ge(*X1["act"].after("s2c1", c))
                nc.vector.tensor_tensor(mix, c2s, s2c, ALU.subtract).then_inc(L.sem, 1)
                dve.wait_ge(*X1["act"].after("gate1", c))
                dve.wait_ge(*L.after("diff", c))
                nc.vector.scalar_tensor_tensor(mix, gate1, 1.0, mix, ALU.add, ALU.mult).then_inc(L.sem, 1)
                dve.wait_ge(*L.after("prod", c))
                nc.vector.scalar_tensor_tensor(mix, s2c, 2.0, mix, ALU.mult, ALU.add).then_inc(L.sem, 1)
                dve.wait_ge(*L.after("mix", c))
                for k in range(K):
                    xs = xT[:, k, bass.ds(c * S, S)]
                    nc.vector.scalar_tensor_tensor(xs, mix[:, k, :], tg1h[:, 0:1], xs, ALU.mult, ALU.add).then_inc(L.sem, 1)

        F1, f1_route_sp, f1_sp, f1_route_pe, f1_pe, f1_route_act, f1_act, f1_route_dve, f1_dve, f1_pool = \
            expert_layer(1, X1, B)

        in_x2 = sem("in_x2")
        w_s, w_w = cols(bigB, 0, (K, D)), cols(bigB, 512, (K, D))
        mask_i = cols(bigB, 1024, (1, B * C))[:, 0, :].bitcast(I32)
        mask = bigB[:, 1280:1536]
        wcr = cols(bigB, 1536, (2, K * P))
        u2 = cols(bigB, 2048, (2, B * C))
        txtT = cols(bigB, 2560, (K, B * C))
        ones_at = bigB[:, 3072:3072 + 2 * C]
        NH2, NR2 = 4, 3
        h2 = [cols(bigA, i * 1024, (K, S)) for i in range(NH2)]
        r2 = cols(bigA, 4096, (NR2, S))
        rhoT = bigA[0:C, 5632:6144]
        rho = cols(bigA, 6144, (QT, C))
        eu = cols(bigA, 6400, (QT, C))
        diag = cols(bigA, 6656, (2, S))
        y2 = fo[:, :, :]
        WEIGHED = ["m0"] + [w for t in range(C) for w in ([f"m{t + 1}"] if t + 1 < C else []) + [f"r{t}"]]
        ws = sb("ws", [P, 2, QT])
        X2S = lines("x2_setup", pe=("txt0", "txt1", "u0", "u1"), act=("txt0", "txt1", "u0", "u1"),
                    dve=("mask_f", "mask", "wcr0", "wcr1", "zeros", "one"))
        LN2 = ln_lines("x2_ln")
        X2 = lines("x2", pe=("feat0", "feat1", *(f"rho{t}" for t in range(C))), act=tuple(f"h{t}" for t in range(C)),
                   dve=WEIGHED)
        X2T = lines("x2_tail", pe=("rhoT", "bc0", "bc1"), act=("rhoT", "exp", "ws", "bs"),
                    dve=("masked", "mx", "shift", "sum", "rsum", "ew", "sw", "eb", "sb", "nw", "nb", "diag", "scaled", "moved",
                         "x0", "x1"))
        TAIL_PE = {2: "rhoT", 28: "bc"}
        TAIL_ACT = {1: "rhoT", 9: "exp", 22: "ws"}
        TAIL_DVE = {4: "masked", 5: "mx", 6: "shift", 11: "sum", 12: "ew", 13: "sw", 14: "eb", 15: "sb", 16: "nw", 25: "diag",
                    31: "scaled", 32: "moved", 33: "x0", 34: "x1"}

        def x2_batches(eng, rows, tail_step, slots):
            rows(0, False)
            with eng.Fori(1, B) as c:
                rows(c, True)
            for step in slots.values():
                tail_step(step, B - 1)

        def x2_load(sp):
            finished(sp, X1, B)
            sp.dma_start(w_s, dram["x2_ws"]).then_inc(in_x2, 16)
            sp.dma_start(w_w, dram["x2_w"]).then_inc(in_x2, 16)
            sp.dma_start(mask_i, dram["mask"]).then_inc(in_x2, 16)

        def x2_pe(pe):
            finished(pe, F1, E * B)
            pe.wait_ge(in_x2, 48)
            pe.wait_ge(*X2S["dve"].before(1))
            for a in range(K):
                for k in range(K):
                    i = nc.tensor.matmul(bank[a][:, 0:B * C], w_s[:, k, a * P:(a + 1) * P], ctxT[:, k, :],
                                         start=k == 0, stop=k == K - 1)
                i.then_inc(X2S["pe"].sem, 1)
            for m in range(2):
                for k in range(K):
                    i = nc.tensor.matmul(bank[2 + m][:, 0:B * C], wcr[:, m, k * P:(k + 1) * P], ctxT[:, k, :],
                                         start=k == 0, stop=k == K - 1)
                i.then_inc(X2S["pe"].sem, 1)
            pe.wait_ge(*X2S["act"].before(1))
            ln_all(pe, LN2, ln_pe)

            def tail_step(step, c):
                if step == "rhoT":
                    pe.wait_ge(*X2T["act"].after("rhoT", c))
                    for q in range(QT):
                        i = nc.tensor.matmul(bank[5][:, q * C:(q + 1) * C], rhoT[:, q * P:(q + 1) * P], ident[0:C, 0:C],
                                             start=True, stop=True)
                    i.then_inc(X2T["pe"].sem, 1)
                else:
                    pe.wait_ge(*X2T["dve"].after("diag", c))
                    for m in range(2):
                        nc.tensor.matmul(bank[6 + m][:, :], ones, diag[:, m, :], start=True,
                                         stop=True).then_inc(X2T["pe"].sem, 1)

            def rows(c, with_tail):
                if with_tail:
                    pe.wait_ge(*X2["act"].before(c))
                for a in range(K):
                    for k in range(K):
                        i = nc.tensor.matmul(bank[2 + a][:, :], w_w[:, k, a * P:(a + 1) * P], nT[:, k, bass.ds(c * S, S)],
                                             start=k == 0, stop=k == K - 1)
                    i.then_inc(X2["pe"].sem, 1)
                for t in range(C):
                    if with_tail and t == 0:
                        pe.wait_ge(*X2T["act"].after("rhoT", c - 1))
                    pe.wait_ge(*X2["dve"].after(f"r{t}", c))
                    i = nc.tensor.matmul(bank[4][0:C, :], ones_at[:, C - 1 - t:2 * C - 1 - t], r2[:, t % NR2, :],
                                         start=t == 0, stop=t == C - 1)
                    i.then_inc(X2["pe"].sem, 1)
                    if with_tail and t in TAIL_PE:
                        tail_step(TAIL_PE[t], c - 1)

            x2_batches(pe, rows, tail_step, TAIL_PE)

        def x2_act(act):
            finished(act, F1, E * B)
            L = X2S["act"]
            for a in range(K):
                act.wait_ge(*X2S["pe"].after(f"txt{a}"))
                nc.scalar.activation(txtT[:, a, :], bank[a][:, 0:B * C], ACT.Identity, bias=v_("ab", a)).then_inc(L.sem, 1)
            for m in range(2):
                act.wait_ge(*X2S["pe"].after(f"u{m}"))
                nc.scalar.activation(u2[:, m, :], bank[2 + m][:, 0:B * C], ACT.Copy).then_inc(L.sem, 1)
            act.wait_ge(*L.before(1))
            ln_all(act, LN2, ln_act)

            def tail_step(step, c):
                if step == "rhoT":
                    act.wait_ge(*X2["pe"].after(f"rho{C - 1}", c))
                    nc.scalar.activation(rhoT, bank[4][0:C, :], ACT.Copy).then_inc(X2T["act"].sem, 1)
                elif step == "exp":
                    act.wait_ge(*X2T["dve"].after("shift", c))
                    nc.scalar.activation(rho, rho, ACT.Exp).then_inc(X2T["act"].sem, 1)
                else:
                    act.wait_ge(*X2T["dve"].after("nb", c))
                    nc.scalar.activation(ws[:, 0, :], ws[:, 0, :], ACT.Tanh, bias=v_("bcw")).then_inc(X2T["act"].sem, 1)
                    nc.scalar.activation(ws[:, 1, :], ws[:, 1, :], ACT.Tanh, bias=v_("bcb")).then_inc(X2T["act"].sem, 1)

            def rows(c, with_tail):
                act.wait_ge(*X2["pe"].after("feat1", c))
                for t in range(C):
                    if t >= NH2:
                        act.wait_ge(*X2["dve"].after(f"r{t - NH2}", c))
                    elif with_tail:
                        act.wait_ge(*X2["dve"].after(f"r{C + t - NH2}", c - 1))
                    for a in range(K):
                        i = nc.scalar.activation(h2[t % NH2][:, a, :], bank[2 + a][:, :], ACT.Tanh,
                                                 bias=txtT[:, a, bass.ds(c * C + t, 1)])
                    i.then_inc(X2["act"].sem, 1)
                    if with_tail and t in TAIL_ACT:
                        tail_step(TAIL_ACT[t], c - 1)

            nc.scalar.preload_act_table(ACT.Exp)
            x2_batches(act, rows, tail_step, TAIL_ACT)

        def x2_dve(dve):
            finished(dve, F1, E * B)
            dve.wait_ge(in_x2, 48)
            L = X2S["dve"]
            nc.vector.tensor_copy(mask, mask_i).then_inc(L.sem, 1)
            dve.wait_ge(*L.after("mask_f"))
            nc.vector.tensor_scalar(mask, mask, NEG, NEG, ALU.mult, ALU.subtract).then_inc(L.sem, 1)
            for m, n in enumerate(("wcw", "wcb")):
                nc.vector.tensor_copy(wcr[:, m, :].rearrange("p (k a) -> p k a", k=K), bcast(v_(n, 0, K), P)).then_inc(L.sem, 1)
            nc.vector.memset(ones_at, 0.0).then_inc(L.sem, 1)
            dve.wait_ge(*L.after("zeros"))
            nc.vector.memset(ones_at[:, C - 1:C], 1.0).then_inc(L.sem, 1)
            dve.wait_ge(*X2S["act"].before(1))
            dve.wait_ge(*L.before(1))
            ln_all(dve, LN2, ln_dve, normed)
            L = X2T["dve"]

            def tail_step(step, c):
                m = 0 if step in ("ew", "sw", "x0") else 1
                if step == "masked":
                    dve.wait_ge(*X2T["pe"].after("rhoT", c))
                    nc.vector.tensor_tensor(rho, bank[5][:, 0:QT * C].rearrange("p (q n) -> p q n", q=QT),
                                            over(mask[:, bass.ds(c * C, C)], QT), ALU.add).then_inc(L.sem, 1)
                elif step == "mx":
                    dve.wait_ge(*L.after("masked", c))
                    nc.vector.tensor_reduce(mx1[:, :], rho, AX.X, ALU.max).then_inc(L.sem, 1)
                elif step == "shift":
                    dve.wait_ge(*L.after("mx", c))
                    nc.vector.tensor_tensor(rho, rho, bcast(mx1[:, :], C), ALU.subtract).then_inc(L.sem, 1)
                elif step == "sum":
                    dve.wait_ge(*X2T["act"].after("exp", c))
                    nc.vector.tensor_reduce(sum1[:, :], rho, AX.X, ALU.add).then_inc(L.sem, 1)
                    dve.wait_ge(*L.after("sum", c))
                    nc.vector.reciprocal(sum1[:, :], sum1[:, :]).then_inc(L.sem, 1)
                elif step in ("ew", "eb"):
                    if m:
                        dve.wait_ge(*L.after("sw", c))
                    nc.vector.tensor_tensor(eu, rho, over(u2[:, m, bass.ds(c * C, C)], QT), ALU.mult).then_inc(L.sem, 1)
                elif step in ("sw", "sb"):
                    dve.wait_ge(*L.after("eb" if m else "ew", c))
                    nc.vector.tensor_reduce(ws[:, m, :], eu, AX.X, ALU.add).then_inc(L.sem, 1)
                elif step == "nw":
                    dve.wait_ge(*L.after("sb", c))
                    for i in range(2):
                        nc.vector.tensor_tensor(ws[:, i, :], ws[:, i, :], sum1[:, :], ALU.mult).then_inc(L.sem, 1)
                elif step == "diag":
                    dve.wait_ge(*X2T["act"].after("bs", c))
                    for n in range(2 * QT):
                        i = nc.vector.tensor_scalar(diag[:, n // QT, n % QT * P:(n % QT + 1) * P], ident,
                                                    ws[:, n // QT, n % QT:n % QT + 1], None, ALU.mult)
                    i.then_inc(L.sem, 1)
                elif step == "scaled":
                    dve.wait_ge(*X2T["pe"].after("bc0", c))
                    nc.vector.tensor_tensor(y2, normed(c), over(bank[6][:, :], K), ALU.mult).then_inc(L.sem, 1)
                elif step == "moved":
                    dve.wait_ge(*X2T["pe"].after("bc1", c))
                    dve.wait_ge(*L.after("scaled", c))
                    nc.vector.tensor_tensor(y2, y2, over(bank[7][:, :], K), ALU.add).then_inc(L.sem, 1)
                else:
                    dve.wait_ge(*L.after("moved", c))
                    xs = xT[:, m, bass.ds(c * S, S)]
                    nc.vector.scalar_tensor_tensor(xs, y2[:, m, :], tgx[:, 2:3], xs, ALU.mult, ALU.add).then_inc(L.sem, 1)

            def rows(c, with_tail):
                def weigh(t):
                    dve.wait_ge(*X2["act"].after(f"h{t}", c))
                    if t >= NR2:
                        dve.wait_ge(*X2["pe"].after(f"rho{t - NR2}", c))
                    elif with_tail:
                        dve.wait_ge(*X2["pe"].after(f"rho{C - 1 - (C - 1 - t) % NR2}", c - 1))
                    nc.vector.tensor_scalar(r2[:, t % NR2, :], h2[t % NH2][:, 0, :], v_("aw", 0), None,
                                            ALU.mult).then_inc(X2["dve"].sem, 1)

                weigh(0)
                for t in range(C):
                    if t + 1 < C:
                        weigh(t + 1)
                    dve.wait_ge(*X2["dve"].after(f"m{t}", c))
                    nc.vector.scalar_tensor_tensor(r2[:, t % NR2, :], h2[t % NH2][:, 1, :], v_("aw", 1), r2[:, t % NR2, :],
                                                   ALU.mult, ALU.add).then_inc(X2["dve"].sem, 1)
                    if with_tail and t in TAIL_DVE:
                        tail_step(TAIL_DVE[t], c - 1)

            x2_batches(dve, rows, tail_step, TAIL_DVE)

        F2, f2_route_sp, f2_sp, f2_route_pe, f2_pe, f2_route_act, f2_act, f2_route_dve, f2_dve, f2_pool = \
            expert_layer(2, {**X2, **{f"tail_{e}": one for e, one in X2T.items()}}, B)

        in_x3 = sem("in_x3")
        HP = HEADS // 2
        w_q3, w_k3, w_v3 = (cols(bigB, 2048 * i, (K, INNER)) for i in range(3))
        w_o3 = cols(bigB, 6144, (HP, D))
        q3_of = [cols(bigA, 0, (HP, S)), cols(bigB, 2048, (HP, S))]
        p3T = cols(bigA, 4096, (HP, S))
        o3 = cols(fh, 0, (HP, S))
        kbd = wflat[:, 4096:8192].rearrange("p (b h n) -> p b h n", b=B, h=HP)
        vbd = fs[:, 0:4096].rearrange("p (b h n) -> p b h n", b=B, h=HP)
        vbd_c = cols(wflat, 1024, (HP, 2 * DH))
        ctx2 = fo[:, :, :].rearrange("p k (b u n) -> p k b u n", b=B, u=2)
        NP3 = 3
        p3_of = [cols(flat(t), 0, (HEADS, C)) for t in (fo, nb)] + [cols(wflat, 2048, (HEADS, C))]
        mx3, sum3 = sb("mx3", [P, 2, HEADS]), sb("sum3", [P, HEADS])
        SC3 = DH ** -0.5
        TQ = range(QT)

        def staggered(first, second):
            order = []
            for q in range(QT + 1):
                order += ([(first, q)] if q < QT else []) + ([(second, q - 1)] if q else [])
            return order

        def staggered_names(first, second):
            return [f"{w}{q}" for ws, q in staggered(first, second) for w in ws]

        KV3 = lines("x3_kv", pe=("k", *(f"v{b}" for b in range(B))), act=("k", *(f"v{b}" for b in range(B))),
                    dve=("zero_k", "zero_v", "ctx0", "ctx1"))
        Q3 = dict(pe=line("x3_q_pe", *(f"q{h}" for h in range(HP))), act=line("x3_q_act", *(f"q{h}" for h in range(HP))))
        X3 = lines("x3", pe=(*staggered_names(("s",), ("pT",)), *(f"o{i}" for i in range(HP)), "y0", "y1"),
                   act=(*staggered_names(("exp",), ("pT",)), *(f"o{i}" for i in range(HP)), "y0", "y1"),
                   dve=(*staggered_names(("mx", "shift"), ("sum", "rsum", "p")), "x0", "x1"))
        LN3 = ln_lines("x3_ln")
        X3V = line("x3_values_pool", "copied")

        def x3_loop(eng, batch):
            with eng.Fori(0, B // 2 - 1) as it:
                for u in range(2):
                    batch(2 * it + u, u, True)
            for u in range(2):
                batch(B - 2 + u, u, u == 0)

        def x3_load(sp):
            finished(sp, X2, B)
            finished(sp, X2T, B)
            for dst, n in ((w_q3, "x3_wq"), (w_k3, "x3_wk"), (w_v3, "x3_wv"), (w_o3, "x3_wo")):
                sp.dma_start(dst, dram[n]).then_inc(in_x3, 16)

        def x3_pe(pe):
            finished(pe, F2, E * B)
            pe.wait_ge(in_x3, 64)
            L = X3["pe"]
            ln_pe(pe, LN3, 0, abufs)
            for h in range(HP):
                for k in range(K):
                    i = nc.tensor.matmul(bank[4 + h // 2][:, h % 2 * B * C:(h % 2 + 1) * B * C], w_k3[:, k, h * P:(h + 1) * P],
                                         ctxT[:, k, :], start=k == 0, stop=k == K - 1)
            i.then_inc(KV3["pe"].sem, 1)
            ln_pe(pe, LN3, 1, abufs)
            pe.wait_ge(*KV3["dve"].before(1))
            for b in range(B):
                pe.wait_ge(*KV3["act"].after(f"v{b - 2}" if b >= 2 else "k"))
                for u in range(2):
                    for k in range(K):
                        i = nc.tensor.matmul(bank[4 + b % 2 * 2 + u][:, :], ctx2[:, k, b, :, :].rearrange("p u n -> p (u n)"),
                                             w_v3[:, k, u * 512:(u + 1) * 512], start=k == 0, stop=k == K - 1)
                i.then_inc(KV3["pe"].sem, 1)
            finished(pe, LN3, B // 2)
            finished(pe, {"act": KV3["act"]})

            def queries(h, c):
                if h >= 2:
                    pe.wait_ge(*Q3["act"].after(f"q{h - 2}", c))
                for k in range(K):
                    i = nc.tensor.matmul(bank[6 + h % 2][:, :], w_q3[:, k, h * P:(h + 1) * P], nT[:, k, bass.ds(c * S, S)],
                                         start=k == 0, stop=k == K - 1)
                i.then_inc(Q3["pe"].sem, 1)

            def batch(c, u, ahead):
                pe.wait_ge(*Q3["act"].after(f"q{HP - 1}", c))
                pe.wait_ge(*X3["act"].before(c))

                def scores(q):
                    for h in range(HP):
                        i = nc.tensor.matmul(bank[q % 2 * 2 + h // 4][:, h % 4 * P:(h % 4 + 1) * P],
                                             q3_of[u][:, h, q * P:(q + 1) * P],
                                             kbd[:, bass.ds(c, 1), h, :].rearrange("p b n -> p (b n)"), start=True, stop=True)
                    i.then_inc(L.sem, 1)
                    if ahead:
                        for h in (2 * q, 2 * q + 1):
                            queries(h, c + 1)

                def turned(q):
                    pe.wait_ge(*X3["dve"].after(f"p{q}", c))
                    if q:
                        pe.wait_ge(*X3["act"].after(f"pT{q - 1}", c))
                    for h in range(HP):
                        i = nc.tensor.transpose(bank[4 + h // 4][:, h % 4 * P:(h % 4 + 1) * P],
                                                p3_of[q % NP3][:, 2 * h:2 * h + 2, :].rearrange("p h n -> p (h n)"), ident)
                    i.then_inc(L.sem, 1)

                for step, q in staggered(scores, turned):
                    step(q)
                pe.wait_ge(*X3["act"].after(f"pT{QT - 1}", c))
                pe.wait_ge(*X3V.after("copied", c))
                for h in range(HP):
                    if h >= 2:
                        pe.wait_ge(*X3["act"].after(f"o{h - 2}", c))
                    elif ahead:
                        pe.wait_ge(*Q3["act"].after(f"q{HP - 2 + h}", c + 1))
                    nc.tensor.matmul(bank[6 + h % 2][:, :], vbd_c[:, h, :], p3T[:, h, :], start=True, stop=True).then_inc(L.sem, 1)
                pe.wait_ge(*X3["act"].after(f"o{HP - 1}", c))
                for k in range(K):
                    for h in range(HP):
                        i = nc.tensor.matmul(bank[k][:, :], w_o3[:, h, k * P:(k + 1) * P], o3[:, h, :], start=h == 0,
                                             stop=h == HP - 1)
                    i.then_inc(L.sem, 1)

            for h in range(HP):
                queries(h, 0)
            x3_loop(pe, batch)

        def x3_pool(pool):
            finished(pool, {"act": KV3["act"]})
            with pool.Fori(0, B) as c:
                pool.wait_ge(*X3["pe"].before(c))
                nc.gpsimd.tensor_copy(vbd_c.rearrange("p h n -> p (h n)"),
                                      vbd[:, bass.ds(c, 1), :, :].rearrange("p b h n -> p (b h n)")).then_inc(X3V.sem, 1)

        def x3_act(act):
            finished(act, F2, E * B)
            L = X3["act"]
            ln_act(act, LN3, 0, abufs)
            act.wait_ge(*KV3["dve"].before(1))
            act.wait_ge(*KV3["pe"].after("k"))
            for j in range(HP // 2):
                for u in range(2):
                    i = nc.scalar.activation(kbd[u * 64:(u + 1) * 64, :, 2 * j:2 * j + 2, u * C:(u + 1) * C],
                                             bank[4 + j][u * 64:(u + 1) * 64, :].rearrange("p (h b n) -> p b h n", h=2, b=B),
                                             ACT.Copy)
            i.then_inc(KV3["act"].sem, 1)
            ln_act(act, LN3, 1, abufs)
            for b in range(B):
                act.wait_ge(*KV3["pe"].after(f"v{b}"))
                for u in range(2):
                    for g in range(2):
                        src = bank[4 + b % 2 * 2 + g][u * 64:(u + 1) * 64, :].rearrange("p (h d) -> p h d", d=2 * DH)
                        i = nc.scalar.activation(vbd[u * 64:(u + 1) * 64, b, 4 * g:4 * g + 4, u * DH:(u + 1) * DH],
                                                 src[:, :, u * DH:(u + 1) * DH], ACT.Copy)
                i.then_inc(KV3["act"].sem, 1)

            def queries(h, c, u):
                act.wait_ge(*Q3["pe"].after(f"q{h}", c))
                nc.scalar.activation(q3_of[u][:, h, :], bank[6 + h % 2][:, :], ACT.Copy).then_inc(Q3["act"].sem, 1)

            def batch(c, u, ahead):
                def exponentials(q):
                    act.wait_ge(*X3["dve"].after(f"shift{q}", c))
                    nc.scalar.activation(p3_of[q % NP3], p3_of[q % NP3], ACT.Exp, scale=SC3).then_inc(L.sem, 1)
                    if ahead:
                        for h in (2 * q, 2 * q + 1):
                            queries(h, c + 1, 1 - u)

                def keep_turned(q):
                    act.wait_ge(*X3["pe"].after(f"pT{q}", c))
                    for u in range(2):
                        i = nc.scalar.activation(p3T[:, 4 * u:4 * u + 4, q * P:(q + 1) * P],
                                                 bank[4 + u][:, :].rearrange("p (h q) -> p h q", h=4), ACT.Copy)
                    i.then_inc(L.sem, 1)

                for step, q in staggered(exponentials, keep_turned):
                    step(q)
                for h in range(HP):
                    act.wait_ge(*X3["pe"].after(f"o{h}", c))
                    nc.scalar.activation(o3[:, h, :], bank[6 + h % 2][:, :], ACT.Copy).then_inc(L.sem, 1)
                for k in range(K):
                    act.wait_ge(*X3["pe"].after(f"y{k}", c))
                    nc.scalar.activation(sq[:, k, :], bank[k][:, :], ACT.Identity, bias=v_("bo", k)).then_inc(L.sem, 1)

            for h in range(HP):
                queries(h, 0, 0)
            x3_loop(act, batch)

        def x3_dve(dve):
            finished(dve, F2, E * B)
            nc.vector.memset(wflat[:, 4096:8192], 0.0).then_inc(KV3["dve"].sem, 1)
            nc.vector.memset(fs[:, 0:4096], 0.0).then_inc(KV3["dve"].sem, 1)
            for u in range(2):
                nc.vector.tensor_copy(ctx2[:, :, :, u, :], ctxT[:, :, :].rearrange("p k (b n) -> p k b n", b=B)
                                      ).then_inc(KV3["dve"].sem, 1)
            ln_all(dve, LN3, ln_dve, normed)
            L = X3["dve"]

            def batch(c, u, ahead):
                dve.wait_ge(*X3["dve"].before(c))

                def shifted(q):
                    p3, mx = p3_of[q % NP3], mx3[:, q % 2, :]
                    if q >= NP3:
                        dve.wait_ge(*X3["pe"].after(f"pT{q - NP3}", c))
                    dve.wait_ge(*X3["pe"].after(f"s{q}", c))
                    sc = [bank[q % 2 * 2 + u][:, :].rearrange("p (h n) -> p h n", n=C) for u in range(2)]
                    for u in range(2):
                        i = nc.vector.tensor_reduce(mx[:, 8 * u:8 * u + 8], sc[u], AX.X, ALU.max)
                    i.then_inc(L.sem, 1)
                    dve.wait_ge(*L.after(f"mx{q}", c))
                    for u in range(2):
                        i = nc.vector.tensor_tensor(p3[:, 8 * u:8 * u + 8, :], sc[u], bcast(mx[:, 8 * u:8 * u + 8], C), ALU.subtract)
                    i.then_inc(L.sem, 1)

                def probabilities(q):
                    p3 = p3_of[q % NP3]
                    if q:
                        dve.wait_ge(*L.after(f"p{q - 1}", c))
                    dve.wait_ge(*X3["act"].after(f"exp{q}", c))
                    nc.vector.tensor_reduce(sum3[:, :], p3, AX.X, ALU.add).then_inc(L.sem, 1)
                    dve.wait_ge(*L.after(f"sum{q}", c))
                    nc.vector.reciprocal(sum3[:, :], sum3[:, :]).then_inc(L.sem, 1)
                    dve.wait_ge(*L.after(f"rsum{q}", c))
                    nc.vector.tensor_tensor(p3, p3, bcast(sum3[:, :], C), ALU.mult).then_inc(L.sem, 1)

                for step, q in staggered(shifted, probabilities):
                    step(q)
                for k in range(K):
                    dve.wait_ge(*X3["act"].after(f"y{k}", c))
                    xs = xT[:, k, bass.ds(c * S, S)]
                    nc.vector.scalar_tensor_tensor(xs, sq[:, k, :], tgx[:, 3:4], xs, ALU.mult, ALU.add).then_inc(L.sem, 1)

            x3_loop(dve, batch)

        in_f3, sent = sem("in_f3"), sem("sent")
        rhsT = cols(wflat, 0, (K, D))
        rq32 = cols(wflat, 512, (K, D))
        rqT = cols(wflat, 1024, (K, D), BF16)
        rq = cols(wflat, 1280, (K, D), BF16)
        identb = cols(wflat, 1536, (1, P), BF16)[:, 0, :]
        rdiag = cols(wflat, 1600, (1, D))[:, 0, :]
        rsb = cols(wflat, 1856, (1, D))[:, 0, :]
        rs, rinv = sb("rs", [P, K]), sb("rinv", [P, K])
        xt = cols(bigA, 0, (T, D))
        xn = cols(bigA, 4096, (T, D))
        q_tok = cols(fn, 0, (T, D), BF16)
        q_f = cols(fh, 0, (K, N), BF16)
        yo = cols(bigB, 0, (T, D))
        stats, mv = sb("stats", [P, T, 6]), sb("mv", [P, T, 2])
        std = sb("std", [P, T])
        ls, linv = sb("ls", [P, T]), sb("linv", [P, T])
        F3 = lines("f3", pe=(*(f"x{i}" for i in range(T)), "rq", "rsb", *(f"q{i}" for i in range(T)), *(f"y{i}" for i in range(T))),
                   act=(*(f"x{i}" for i in range(T)), "std", *(f"q{i}" for i in range(T))),
                   dve=("identb", "rmax", "rs", "rinv", "rmul", "rround", "rclip", "rq", "rdiag0", "rdiag1", "rsb",
                        *(f"stats{i}" for i in range(T)), *(f"mv{i}" for i in range(T)),
                        "eps", "rstd", *(f"n{i}" for i in range(T)), "amax", "ls", "linv", *(f"mul{i}" for i in range(T)), "round", "clip",
                        *(f"{w}{i}" for i in range(T) for w in ("y", "x"))))

        def f3_sp(sp):
            finished(sp, F2, E * B)
            sp.dma_start(rhsT, dram["f3_rhsT"]).then_inc(in_f3, 16)
            for i in range(T):
                sp.wait_ge(*F3["dve"].after(f"x{i}"))
                sp.dma_start(out[i * P:(i + 1) * P, :], yo[:, i, :]).then_inc(sent, 16)
            sp.wait_ge(sent, 16 * T)

        def f3_pe(pe):
            finished(pe, X3, B)
            L = F3["pe"]
            for i in range(T):
                if i >= 4:
                    pe.wait_ge(*F3["act"].after(f"x{i - 4}"))
                for k in range(K):
                    m = nc.tensor.transpose(bank[i % 4][:, k * P:(k + 1) * P], xT[:, k, i * P:(i + 1) * P], ident)
                m.then_inc(L.sem, 1)
            pe.wait_ge(*F3["dve"].after("rclip"))
            b16 = bank[4][:, 0:2 * P].bitcast(BF16)
            for k in range(K):
                for o in range(K):
                    m = nc.tensor.transpose(b16[:, (k * K + o) * P:(k * K + o + 1) * P], rqT[:, o, k * P:(k + 1) * P], identb)
            m.then_inc(L.sem, 1)
            pe.wait_ge(*F3["dve"].after("rdiag1"))
            nc.tensor.matmul(bank[5][:, 0:D], ones, rdiag, start=True, stop=True).then_inc(L.sem, 1)
            pe.wait_ge(*F3["dve"].after("clip"))
            for i in range(T):
                if i >= 2:
                    pe.wait_ge(*F3["act"].after(f"q{i - 2}"))
                bq = bank[6 + i % 2][:, 0:P].bitcast(BF16)
                for k in range(K):
                    m = nc.tensor.transpose(bq[:, k * P:(k + 1) * P], q_tok[:, i, k * P:(k + 1) * P], identb)
                m.then_inc(L.sem, 1)
            for i in range(T):
                pe.wait_ge(*F3["act"].after(f"q{i}"))
                if i >= 4:
                    pe.wait_ge(*F3["dve"].after(f"y{i - 4}"))
                for k in range(K):
                    m = nc.tensor.matmul(bank[i % 4][:, 0:D], q_f[:, k, i * P:(i + 1) * P], rq[:, k, :], start=k == 0,
                                         stop=k == K - 1)
                m.then_inc(L.sem, 1)

        def f3_act(act):
            finished(act, X3, B)
            L = F3["act"]
            for i in range(T):
                act.wait_ge(*F3["pe"].after(f"x{i}"))
                nc.scalar.activation(xt[:, i, :], bank[i % 4][:, 0:D], ACT.Copy).then_inc(L.sem, 1)
            act.wait_ge(*F3["dve"].after("eps"))
            nc.scalar.activation(std[:, :], std[:, :], ACT.Sqrt).then_inc(L.sem, 1)
            for i in range(T):
                act.wait_ge(*F3["pe"].after(f"q{i}"))
                bq = bank[6 + i % 2][:, 0:P].bitcast(BF16)
                nc.scalar.activation(q_f[:, :, i * P:(i + 1) * P], bq.rearrange("p (k q) -> p k q", k=K),
                                     ACT.Copy).then_inc(L.sem, 1)

        def f3_dve(dve):
            finished(dve, X3, B)
            dve.wait_ge(in_f3, 16)
            L = F3["dve"]
            nc.vector.tensor_copy(identb, ident).then_inc(L.sem, 1)
            nc.vector.tensor_reduce(rs[:, :], rhsT, AX.X, ALU.max, apply_absolute_value=True).then_inc(L.sem, 1)
            dve.wait_ge(*L.after("rmax"))
            nc.vector.tensor_scalar(rs[:, :], rs[:, :], 1e-12, 1.0 / 127.0, ALU.max, ALU.mult).then_inc(L.sem, 1)
            dve.wait_ge(*L.after("rs"))
            nc.vector.reciprocal(rinv[:, :], rs[:, :]).then_inc(L.sem, 1)
            dve.wait_ge(*L.after("rinv"))
            for k in range(K):
                i = nc.vector.tensor_scalar(rq32[:, k, :], rhsT[:, k, :], rinv[:, k:k + 1], ROUND, ALU.mult, ALU.add)
            i.then_inc(L.sem, 1)
            dve.wait_ge(*L.after("rmul"))
            nc.vector.tensor_scalar(rq32, rq32, ROUND, 127.0, ALU.subtract, ALU.min).then_inc(L.sem, 1)
            dve.wait_ge(*L.after("rround"))
            nc.vector.tensor_scalar(rqT, rq32, -127.0, None, ALU.max).then_inc(L.sem, 1)
            dve.wait_ge(*F3["pe"].after("rq"))
            nc.vector.tensor_copy(rq.rearrange("p k d -> p (k d)"), bank[4][:, 0:2 * P].bitcast(BF16)).then_inc(L.sem, 1)
            for k in range(K):
                nc.vector.tensor_scalar(rdiag[:, k * P:(k + 1) * P], ident, rs[:, k:k + 1], None, ALU.mult).then_inc(L.sem, 1)
            dve.wait_ge(*F3["pe"].after("rsb"))
            nc.vector.tensor_copy(rsb, bank[5][:, 0:D]).then_inc(L.sem, 1)
            for i in range(T):
                dve.wait_ge(*F3["act"].after(f"x{i}"))
                nc.vector.bn_stats(stats[:, i, :], xt[:, i, :]).then_inc(L.sem, 1)
            for i in range(T):
                dve.wait_ge(*L.after(f"stats{i}"))
                nc.vector.bn_aggr(mv[:, i, :], stats[:, i, :]).then_inc(L.sem, 1)
            dve.wait_ge(*L.after(f"mv{T - 1}"))
            nc.vector.tensor_scalar(std[:, :], mv[:, :, 1], EPS, None, ALU.add).then_inc(L.sem, 1)
            dve.wait_ge(*F3["act"].after("std"))
            nc.vector.reciprocal(std[:, :], std[:, :]).then_inc(L.sem, 1)
            dve.wait_ge(*L.after("rstd"))
            for i in range(T):
                nc.vector.tensor_scalar(xn[:, i, :], xt[:, i, :], mv[:, i, 0:1], std[:, i:i + 1], ALU.subtract,
                                        ALU.mult).then_inc(L.sem, 1)
            dve.wait_ge(*L.after(f"n{T - 1}"))
            nc.vector.tensor_reduce(ls[:, :], xn, AX.X, ALU.max, apply_absolute_value=True).then_inc(L.sem, 1)
            dve.wait_ge(*L.after("amax"))
            nc.vector.tensor_scalar(ls[:, :], ls[:, :], 1e-12, 1.0 / 127.0, ALU.max, ALU.mult).then_inc(L.sem, 1)
            dve.wait_ge(*L.after("ls"))
            nc.vector.reciprocal(linv[:, :], ls[:, :]).then_inc(L.sem, 1)
            dve.wait_ge(*L.after("linv"))
            for i in range(T):
                nc.vector.tensor_scalar(xn[:, i, :], xn[:, i, :], linv[:, i:i + 1], ROUND, ALU.mult, ALU.add).then_inc(L.sem, 1)
            dve.wait_ge(*L.after(f"mul{T - 1}"))
            nc.vector.tensor_scalar(xn, xn, ROUND, 127.0, ALU.subtract, ALU.min).then_inc(L.sem, 1)
            dve.wait_ge(*L.after("round"))
            nc.vector.tensor_scalar(q_tok, xn, -127.0, None, ALU.max).then_inc(L.sem, 1)
            for i in range(T):
                dve.wait_ge(*F3["pe"].after(f"y{i}"))
                nc.vector.scalar_tensor_tensor(yo[:, i, :], bank[i % 4][:, 0:D], ls[:, i:i + 1], rsb, ALU.mult,
                                               ALU.mult).then_inc(L.sem, 1)
                dve.wait_ge(*L.after(f"y{i}"))
                nc.vector.scalar_tensor_tensor(yo[:, i, :], yo[:, i, :], tgf[:, 3:4], xt[:, i, :], ALU.mult,
                                               ALU.add).then_inc(L.sem, 1)

        block = ctx.enter_context(nc.Block())

        @block.sync
        def _(sp):
            setup_sp(sp)
            lstm2_sp(sp)
            x1_load(sp)
            f0_route_sp(sp)
            f0_sp(sp)
            f1_route_sp(sp)
            x2_load(sp)
            f1_sp(sp)
            f2_route_sp(sp)
            x3_load(sp)
            f2_sp(sp)
            f3_sp(sp)

        @block.tensor
        def _(pe):
            opened(pe, "pe")
            setup_pe(pe)
            xproj_pe(pe)
            rec_pe(pe)
            lstm2_pe(pe)
            f0_route_pe(pe)
            f0_pe(pe)
            x1_pe(pe)
            f1_route_pe(pe)
            f1_pe(pe)
            x2_pe(pe)
            f2_route_pe(pe)
            f2_pe(pe)
            x3_pe(pe)
            f3_pe(pe)

        @block.gpsimd
        def _(pool):
            opened(pool, "pool")
            setup_pool(pool)
            rec_pool(pool)
            f0_pool(pool)
            f1_pool(pool)
            f2_pool(pool)
            x3_pool(pool)

        @block.scalar
        def _(act):
            opened(act, "act")
            setup_act(act)
            xproj_act(act)
            rec_act(act)
            lstm2_act(act)
            f0_route_act(act)
            f0_act(act)
            x1_act(act)
            f1_route_act(act)
            f1_act(act)
            x2_act(act)
            f2_route_act(act)
            f2_act(act)
            x3_act(act)
            f3_act(act)

        @block.vector
        def _(dve):
            opened(dve, "dve")
            setup_dve(dve)
            xproj_dve(dve)
            rec_dve(dve)
            lstm2_dve(dve)
            f0_route_dve(dve)
            f0_dve(dve)
            x1_dve(dve)
            f1_route_dve(dve)
            f1_dve(dve)
            x2_dve(dve)
            f2_route_dve(dve)
            f2_dve(dve)
            x3_dve(dve)
            f3_dve(dve)


def feature_major(a):
    import numpy as np
    r, c = a.shape
    return np.ascontiguousarray(a.T.reshape(c // P, P, r).transpose(1, 0, 2))


def row_tiles(a):
    import numpy as np
    r, c = a.shape
    return np.ascontiguousarray(a.reshape(r // P, P, c).transpose(1, 0, 2))


def pack(inp):
    import numpy as np
    arr = {k: np.asarray(v) for k, v in inp.items()}

    def col(a):
        return a.reshape(-1, P).T

    def rep(a):
        return np.broadcast_to(a.reshape(1, -1), (P, a.size))

    x0, x1, x2, x3 = (f"L{i}_xattn_" for i in range(4))
    f0, f1, f2, f3 = (f"L{i}_ffn_" for i in range(4))
    vecs = dict(
        b_att=col(arr[x0 + "b_att"]), v=col(arr[x0 + "v"]),
        b_ih0=col(arr[x0 + "b_ih0"]), b_hh0=col(arr[x0 + "b_hh0"]),
        b_ih1=col(arr[x0 + "b_ih1"]), b_hh1=col(arr[x0 + "b_hh1"]),
        f0_b1=col(arr[f0 + "b1"]), f0_b2=col(arr[f0 + "b2"]), f0_br=rep(arr[f0 + "br"]),
        f2_b1=col(arr[f2 + "b1"]), f2_b2=col(arr[f2 + "b2"]), f2_br=rep(arr[f2 + "br"]),
        **{n: col(arr[x1 + n]) for n in ("bq_c", "bk_s", "bv_s", "bq_s", "bk_c", "bv_c", "bg")},
        ab=col(arr[x2 + "b"]), aw=col(arr[x2 + "w"]), wcw=col(arr[x2 + "Wcw"]), wcb=col(arr[x2 + "Wcb"]),
        bcw=rep(arr[x2 + "bcw"]), bcb=rep(arr[x2 + "bcb"]), bo=col(arr[x3 + "bo"]),
        gx=rep(arr["g_xattn"]), gf=rep(arr["g_ffn"]))
    vec = np.ascontiguousarray(np.concatenate([vecs[n] for n in VECS], axis=1))

    ident = np.eye(P, dtype=np.float32)
    p = np.arange(P)
    diag_b = (p[:, None] // 32 == np.arange(B)[None]).astype(np.float32)
    i, j = np.arange(E)[:, None], np.arange(E)[None]
    before, upto = ((j < i).astype(np.float32).reshape(1, -1), (j <= i).astype(np.float32).reshape(1, -1))
    pos = np.clip((np.arange(S) + 0.5) * (C / S) - 0.5, 0.0, C - 1)
    lo = np.floor(pos).astype(int)
    hi = np.minimum(lo + 1, C - 1)
    interp = np.zeros((P, S), np.float32)
    interp[lo, np.arange(S)] += (1.0 - (pos - lo)).astype(np.float32)
    interp[hi, np.arange(S)] += (pos - lo).astype(np.float32)
    consts = dict(ident=ident, ones=np.ones((P, P), np.float32), mean=np.full((P, P), 1.0 / D, np.float32),
                  diag_b=diag_b, before=np.broadcast_to(before, (P, E * E)), upto=np.broadcast_to(upto, (P, E * E)),
                  interp=interp)
    cst = np.ascontiguousarray(np.concatenate([consts[n] for n in CONSTS], axis=1), dtype=np.float32)

    ctx = arr["ctx_1024"].reshape(B * C, D)
    ctxq = arr["ctx_1024"].reshape(B, 2, 32, D).transpose(1, 0, 2, 3).reshape(B * C, D)
    w_ih0 = arr[x0 + "W_ih0"]
    w1x = np.stack([feature_major(arr[x1 + n]) for n in ("Wq_c", "Wk_s", "Wv_s", "Wq_s", "Wk_c", "Wv_c")], axis=1)
    mask = np.ascontiguousarray(np.broadcast_to(arr["mask_BxS2_ik0"].reshape(1, B * C), (P, B * C)))
    return dict(
        vec=vec, cst=cst, ctxT=feature_major(ctx), ctxTq=feature_major(ctxq), xT=feature_major(arr["x"].reshape(N, D)),
        w_f=row_tiles(arr[x0 + "Wf"]), w_h=row_tiles(arr[x0 + "Wh"]),
        w_x=feature_major(w_ih0[:, :D]), w_at=feature_major(w_ih0[:, D:]), w_hh=feature_major(arr[x0 + "W_hh0"]),
        w_ih1=feature_major(arr[x0 + "W_ih1"]), w_hh1=feature_major(arr[x0 + "W_hh1"]),
        f0_w1=np.stack([row_tiles(a) for a in arr[f0 + "w1"]]), f0_w2=np.stack([row_tiles(a) for a in arr[f0 + "w2"]]),
        f0_wr=row_tiles(arr[f0 + "wr"]),
        f1_w1=np.stack([row_tiles(a) for a in arr[f1 + "w1"]]), f1_w3=np.stack([row_tiles(a) for a in arr[f1 + "w3"]]),
        f1_w2=np.stack([row_tiles(a) for a in arr[f1 + "w2"]]), f1_wr=row_tiles(arr[f1 + "router_w"]),
        f2_w1=np.stack([row_tiles(a) for a in arr[f2 + "W1"]]), f2_w2=np.stack([row_tiles(a) for a in arr[f2 + "W2"]]),
        f2_wr=row_tiles(arr[f2 + "Wr"]),
        x1_w=np.ascontiguousarray(w1x), x1_wg=feature_major(arr[x1 + "Wg"]),
        x2_ws=row_tiles(arr[x2 + "Ws"]), x2_w=row_tiles(arr[x2 + "W"]), mask=mask,
        x3_wq=feature_major(arr[x3 + "Wq"]), x3_wk=feature_major(arr[x3 + "Wk"]), x3_wv=feature_major(arr[x3 + "Wv"]),
        x3_wo=feature_major(arr[x3 + "Wo"]), f3_rhsT=feature_major(arr[f3 + "rhs"]))


def kernel(**inputs):
    import numpy as np
    import concourse.bacc as bacc
    from concourse.bass_utils import run_bass_kernel_spmd

    arrays = pack(inputs)
    nc = bacc.Bacc("TRN2", target_bir_lowering=False, num_devices=1)
    dram = {n: nc.dram_tensor(f"in_{n}", a.shape, mybir.dt.from_np(a.dtype), kind="ExternalInput").ap()
            for n, a in arrays.items()}
    out = nc.dram_tensor("out_x", (N, D), F32, kind="ExternalOutput").ap()
    build(nc, dram, out)
    r = run_bass_kernel_spmd(nc, [{f"in_{n}": a for n, a in arrays.items()}], core_ids=[0])
    return np.asarray(r.results[0]["out_x"]).reshape(B, S, D)
```
